# Optimizing a Trainium2 kernel written in Bass

```python
import numpy as np
import jax
import jax.numpy as jnp

def _softmax(x, axis=-1):
    return jax.nn.softmax(x, axis=axis)

def _gelu(x):
    return jax.nn.gelu(x, approximate=True)

def _silu(x):
    return jax.nn.silu(x)

def _sigmoid(x):
    return jax.nn.sigmoid(x)

def _layernorm(x, axis=-1, eps=1e-05):
    m = jnp.mean(x, axis=axis, keepdims=True)
    v = jnp.var(x, axis=axis, keepdims=True)
    return (x - m) / jnp.sqrt(v + eps)

def _scatter_add(tgt, idx, src, axis=0):
    return tgt.at[idx].add(src)

def _segment_sum(src, seg, n):
    return jax.ops.segment_sum(src, seg, n)
kernel_name = 'mk_flamingo_gated_d1_seqx_r2_c8eeb5'

def setup_inputs(seed: int=0):
    np.random.seed(seed)
    _w = jnp.asarray

    def _rec_inputs():
        import jax
        import jax.numpy as jnp
        _rk = jax.random.key(seed)
        x = -0.0002928 + 1 * jax.random.normal(jax.random.fold_in(_rk, 1), (16, 256, 512), jnp.float32)
        _lenS = 256 - jax.random.randint(jax.random.fold_in(_rk, 7), (16,), 0, max(1, 256 // 4) + 1, jnp.int32)
        _lenS2 = 256 - jax.random.randint(jax.random.fold_in(_rk, 8), (16,), 0, max(1, 256 // 4) + 1, jnp.int32)
        _ctx_1024P = jax.random.normal(jax.random.fold_in(_rk, 11), (16, 16, 512), jnp.float32)
        _ctx_1024c = jax.random.dirichlet(jax.random.fold_in(_rk, 511), 0.3 * jnp.ones((16,), jnp.float32), (16, 256))
        _ctx_1024t = jnp.einsum('bsk,bkd->bsd', _ctx_1024c, _ctx_1024P)
        _ctx_1024t = _ctx_1024t * jax.lax.rsqrt(jnp.mean(jnp.square(_ctx_1024t)) + 1e-12) * 0.953939
        ctx_1024 = -1.39393e-06 + 0.999914 * (_ctx_1024t + 0.3 * jax.random.normal(jax.random.fold_in(_rk, 611), (16, 256, 512), jnp.float32))
        _g = jax.random.normal(jax.random.fold_in(_rk, 9001), (2, 1), jnp.float32)
        _g = jnp.sign(_g) * jnp.maximum(jnp.abs(_g), 1.0) + (_g == 0) * 1.0
        g_xattn = _g[0]
        g_ffn = _g[1]
        return (x, ctx_1024, g_xattn, g_ffn)
    x, ctx_1024, g_xattn, g_ffn = _rec_inputs()

    def _L0_xattn_setup():
        import jax, jax.numpy as jnp
        import numpy as np
        D_MODEL = 512
        NHEAD = 16
        HEAD_DIM = D_MODEL // NHEAD
        key = jax.random.key(seed)
        ks = jax.random.split(key, 11)
        B, S = (2, 1024)
        s = 1.0 / np.sqrt(D_MODEL)
        return {'query': jax.random.normal(ks[0], (B, S, D_MODEL), jnp.float32), 'key': jax.random.normal(ks[1], (B, S, D_MODEL), jnp.float32), 'value': jax.random.normal(ks[2], (B, S, D_MODEL), jnp.float32), 'wq_w': jax.random.normal(ks[3], (D_MODEL, D_MODEL), jnp.float32) * s, 'wq_b': jax.random.normal(ks[4], (D_MODEL,), jnp.float32) * s, 'wk_w': jax.random.normal(ks[5], (D_MODEL, D_MODEL), jnp.float32) * s, 'wk_b': jax.random.normal(ks[6], (D_MODEL,), jnp.float32) * s, 'wv_w': jax.random.normal(ks[7], (D_MODEL, D_MODEL), jnp.float32) * s, 'wv_b': jax.random.normal(ks[8], (D_MODEL,), jnp.float32) * s, 'wo_w': jax.random.normal(ks[9], (D_MODEL, D_MODEL), jnp.float32) * s, 'wo_b': jax.random.normal(ks[10], (D_MODEL,), jnp.float32) * s}
    _L0_xattn_all = _L0_xattn_setup()
    _L0_xattn_in = {k: v for k, v in _L0_xattn_all.items() if k in ('wq_w', 'wq_b', 'wk_w', 'wk_b', 'wv_w', 'wv_b', 'wo_w', 'wo_b')}
    del _L0_xattn_all

    def _L0_ffn_setup():
        import jax, jax.numpy as jnp
        import numpy as np
        from math import ceil
        CAPACITY_FACTOR = 2.0
        MIN_CAPACITY = 4
        key = jax.random.key(seed)
        ks = jax.random.split(key, 4)
        B, S, D, Di, E = (4, 1024, 512, 2048, 8)
        x = jax.random.normal(ks[0], (B, S, D), dtype=jnp.float32)
        Wr = jax.random.normal(ks[1], (D, E), dtype=jnp.float32) * D ** (-0.5)
        W1 = jax.random.normal(ks[2], (E, D, Di), dtype=jnp.float32) * D ** (-0.5)
        b1 = jnp.zeros((E, Di), dtype=jnp.float32)
        W2 = jax.random.normal(ks[3], (E, Di, D), dtype=jnp.float32) * Di ** (-0.5)
        b2 = jnp.zeros((E, D), dtype=jnp.float32)
        return {'x': x, 'Wr': Wr, 'W1': W1, 'b1': b1, 'W2': W2, 'b2': b2}
    _L0_ffn_all = _L0_ffn_setup()
    _L0_ffn_in = {k: v for k, v in _L0_ffn_all.items() if k in ('Wr', 'W1', 'b1', 'W2', 'b2')}
    del _L0_ffn_all
    return {'x': x, 'ctx_1024': ctx_1024, 'g_xattn': g_xattn, 'g_ffn': g_ffn, 'L0_xattn_wq_w': _L0_xattn_in['wq_w'], 'L0_xattn_wq_b': _L0_xattn_in['wq_b'], 'L0_xattn_wk_w': _L0_xattn_in['wk_w'], 'L0_xattn_wk_b': _L0_xattn_in['wk_b'], 'L0_xattn_wv_w': _L0_xattn_in['wv_w'], 'L0_xattn_wv_b': _L0_xattn_in['wv_b'], 'L0_xattn_wo_w': _L0_xattn_in['wo_w'], 'L0_xattn_wo_b': _L0_xattn_in['wo_b'], 'L0_ffn_Wr': _L0_ffn_in['Wr'], 'L0_ffn_W1': _L0_ffn_in['W1'], 'L0_ffn_b1': _L0_ffn_in['b1'], 'L0_ffn_W2': _L0_ffn_in['W2'], 'L0_ffn_b2': _L0_ffn_in['b2']}

def reference(x, ctx_1024, g_xattn, g_ffn, L0_xattn_wq_w, L0_xattn_wq_b, L0_xattn_wk_w, L0_xattn_wk_b, L0_xattn_wv_w, L0_xattn_wv_b, L0_xattn_wo_w, L0_xattn_wo_b, L0_ffn_Wr, L0_ffn_W1, L0_ffn_b1, L0_ffn_W2, L0_ffn_b2):
    import jax
    import jax.numpy as jnp

    def _L0_xattn_ref(query, key, value, wq_w, wq_b, wk_w, wk_b, wv_w, wv_b, wo_w, wo_b):
        import jax, jax.numpy as jnp
        import numpy as np
        D_MODEL = 512
        NHEAD = 16
        HEAD_DIM = D_MODEL // NHEAD
        B, S, _ = query.shape

        def proj(x, w, b):
            y = x @ w.T + b
            return y.reshape(B, S, NHEAD, HEAD_DIM).transpose(0, 2, 1, 3)
        Q = proj(query, wq_w, wq_b)
        K = proj(key, wk_w, wk_b)
        V = proj(value, wv_w, wv_b)
        scale = 1.0 / np.sqrt(HEAD_DIM).astype(np.float32)
        scores = jnp.einsum('bhqd,bhkd->bhqk', Q, K) * scale
        causal = jnp.tril(jnp.ones((S, S), dtype=bool))
        scores = jnp.where(causal, scores, -jnp.inf)
        attn = jax.nn.softmax(scores, axis=-1)
        out = jnp.einsum('bhqk,bhkd->bhqd', attn, V)
        out = out.transpose(0, 2, 1, 3).reshape(B, S, D_MODEL)
        return out @ wo_w.T + wo_b

    def _L0_ffn_ref(x, Wr, W1, b1, W2, b2):
        import jax, jax.numpy as jnp
        import numpy as np
        from math import ceil
        CAPACITY_FACTOR = 2.0
        MIN_CAPACITY = 4
        B, S, D = x.shape
        E = Wr.shape[1]
        N = B * S
        k = max(MIN_CAPACITY, ceil(N * CAPACITY_FACTOR / E))
        xt = x.reshape(N, D)
        scores = jax.nn.softmax(xt @ Wr, axis=-1)
        G, idx = jax.lax.top_k(scores.T, k)
        X_in = xt[idx]
        h = jax.nn.gelu(jnp.einsum('ekd,edh->ekh', X_in, W1) + b1[:, None, :], approximate=False)
        X_e = jnp.einsum('ekh,ehd->ekd', h, W2) + b2[:, None, :]
        contrib = (G[..., None] * X_e).reshape(E * k, D)
        out = jnp.zeros((N, D), dtype=x.dtype).at[idx.reshape(-1)].add(contrib)
        return out.reshape(B, S, D)
    x = x + jnp.tanh(g_xattn[0]) * _L0_xattn_ref(_layernorm(x, axis=-1), ctx_1024, ctx_1024, L0_xattn_wq_w, L0_xattn_wq_b, L0_xattn_wk_w, L0_xattn_wk_b, L0_xattn_wv_w, L0_xattn_wv_b, L0_xattn_wo_w, L0_xattn_wo_b)
    x = x + jnp.tanh(g_ffn[0]) * _L0_ffn_ref(_layernorm(x, axis=-1), L0_ffn_Wr, L0_ffn_W1, L0_ffn_b1, L0_ffn_W2, L0_ffn_b2)
    return x

_drawn_inputs = setup_inputs


def setup_inputs(seed=0):
    import zlib

    import numpy as np

    out = dict(_drawn_inputs(seed))
    spreads = {'L0_ffn_b1': (0.0, 0.32), 'L0_ffn_b2': (0.0, 0.1)}
    factors = {'L0_xattn_wq_b': 4.512, 'L0_xattn_wk_b': 8.0}
    for name, (base, spread) in spreads.items():
        noise = np.random.default_rng([zlib.crc32(name.encode()), seed]).standard_normal(out[name].shape)
        drawn = base * np.exp(spread * noise) if base else spread * noise
        out[name] = jnp.asarray(drawn.astype(out[name].dtype))
    for name, factor in factors.items():
        out[name] = (out[name] * factor).astype(out[name].dtype)
    return out
```

```python
from contextlib import ExitStack

import concourse.bass as bass
from concourse import mybir

ALU = mybir.AluOpType
ACT = mybir.ActivationFunctionType
AX = mybir.AxisListType.X
F32 = mybir.dt.float32
F32R = mybir.dt.float32r
BF16 = mybir.dt.bfloat16
I32 = mybir.dt.int32
U32 = mybir.dt.uint32

P = 128
BATCH, SEQ, D = 16, 256, 512
HEADS = 16
DH = D // HEADS
HPB = P // DH
KB = D // P
TPB = SEQ // P
N = BATCH * SEQ
EXPERTS = 8
TOPK = max(4, -(-N * 2 // EXPERTS))
DI = 2048
HB = DI // P
SCALE = float(DH) ** -0.5
EPS = 1e-5
MASKED = -1e30
ROW = D + EXPERTS
SLOTS = 512
PASSES = TOPK // SLOTS
STILES = SLOTS // P
CHUNKS = P // EXPERTS
CHUNK = N // CHUNKS
VW = DH + 1

FILLS = [("AT0", "U", 0), ("AT1", "U", 1), ("O0", "U", 2), ("XT0", "P", 3), ("O1", "U", 4), ("XT1", "P", 5),
         ("Q0", "P", 6), ("CT0", "P", 7), ("X2T0", "U", 7), ("CT1", "P", 8), ("X2T1", "U", 8), ("K0", "P", 9),
         ("R", "U", 10), ("V0", "P", 11), ("K1", "P", 12), ("Q2", "P", 13), ("V1", "P", 14), ("Q3", "P", 15)]
ORDER = [w for w, _, _ in FILLS]
LAST = BATCH
STEADY = (3, BATCH - 1)


def stages(i):
    if not isinstance(i, int):
        return "PAU"
    return "P" * (i + 1 < BATCH) + "A" * (0 <= i < BATCH) + "U" * (i >= 1)


def fills(i):
    return [(w, s, h) for w, s, h in FILLS if s in stages(i)]


def fill(i, what):
    names = [w for w, _, _ in fills(i)]
    at = names.index(what)
    per = len(FILLS) // 2

    def before(step, bank):
        return sum(sum(n % 2 == bank for n in range(len(fills(s)))) for s in range(-1, step))

    if isinstance(i, int):
        return at % 2, before(i, at % 2) + at // 2 + 1
    return at % 2, i * per + (before(1, at % 2) - per + at // 2 + 1)


def of_row(what, b):
    stage = next(s for w, s, _ in FILLS if w == what)
    return fill(b - 1 if stage == "P" else b + 1, what)


def block_program(nc, a, out):
    ctx = ExitStack()
    with ctx:
        def sb(name, shape, dt=F32, where=ctx):
            return where.enter_context(nc.sbuf_tensor(name, shape, dt))

        def sem(name):
            return ctx.enter_context(nc.semaphore(name))

        rows_dram = nc.dram_tensor("token_rows", [N, ROW], F32)
        ident = sb("ident", [P, P])
        scores = sb("scores", [P, TPB, EXPERTS, BATCH])
        tanh_g = sb("tanh_g", [P, 2])
        psum = [ctx.enter_context(nc.psum_tensor(f"bank{i}", [P, 512], F32)) for i in range(8)]
        attention_phase(nc, a, out, rows_dram, ident, scores, tanh_g, psum, sb, sem)

        ring = {n: sb(n, shape, F32R) for n, shape in (
            ("w1_hi", [P, HB, KB, P]), ("w1_lo", [P, HB, KB, P]), ("w2_hi", [P, HB, D]), ("w2_lo", [P, HB, D]))}
        raw1 = [sb(f"w1_raw{p}", [P, KB, P]) for p in range(2)]
        raw2 = [sb(f"w2_raw{p}", [P, D]) for p in range(2)]
        index = sb("index", [P, EXPERTS, TOPK // P], U32)
        b1 = sb("b1", [P, EXPERTS, HB])
        w_in = [sem(f"w_in{p}") for p in range(2)]
        selection_phase(nc, a, ident, scores, ring, raw1, raw2, w_in, index, b1, psum, sem)
        expert_phase(nc, a, out, rows_dram, ident, tanh_g, ring, raw1, raw2, w_in, index, b1, psum, sb, sem)


def attention_phase(nc, a, out, rows_dram, ident, scores, tanh_g, psum, sb_all, sem):
    ctx = ExitStack()
    with ctx:
        def sb(name, shape, dt=F32):
            return sb_all(name, shape, dt, ctx)

        mask = sb("mask", [P, 3 * P])
        half = sb("half", [P, TPB])
        bq = sb("bq", [P, KB])
        bk = sb("bk", [P, KB])
        bv = sb("bv", [P, D])
        bo = sb("bo", [P, D])
        wr = sb("wr", [P, KB, EXPERTS])
        names = ("wq", "wk", "wv", "wo")
        w_hi = {n: sb(n + "_hi", [P, KB, D], F32R) for n in names}
        w_lo = {n: sb(n + "_lo", [P, KB, D], F32R) for n in names}
        S, PT, O, W = psum[0:2], psum[2:4], psum[4:6], psum[6:8]

        const_ready = sem("const_ready")
        weights_setup(nc, a, const_ready, ident, mask, half, bq, bk, bv, bo, wr, tanh_g, w_hi, w_lo, names, W, sem)

        xin = [sb(f"xin{p}", [P, TPB, D]) for p in range(2)]
        cin = [sb(f"cin{p}", [P, TPB, D]) for p in range(2)]
        x1 = [sb(f"x1{p}", [P, TPB, D]) for p in range(2)]
        xn = sb("xn", [P, TPB, D])
        xnT = [sb(f"xnT_{s}", [P, KB, SEQ], F32R) for s in ("hi", "lo")]
        cT = [sb(f"cT_{s}", [P, KB, SEQ], F32R) for s in ("hi", "lo")]
        aT = [sb(f"aT_{s}", [P, KB, SEQ], F32R) for s in ("hi", "lo")]
        QT = [sb(f"QT{p}", [P, KB, SEQ]) for p in range(2)]
        KT = [sb(f"KT{p}", [P, KB, SEQ]) for p in range(2)]
        V = [sb(f"V{p}", [P, TPB, HEADS, VW]) for p in range(2)]
        E = [sb(f"E{p}", [P, 3 * P]) for p in range(2)]
        ET = [sb(f"ET{p}", [P, 3 * P]) for p in range(2)]
        least = [sb(f"least{p}", [P, 2]) for p in range(2)]
        attn = [sb(f"attn{p}", [P, TPB, D]) for p in range(2)]
        rsum = sb("rsum", [P, TPB * HPB])
        rows = [sb(f"rows{p}", [P, TPB, ROW]) for p in range(2)]
        xn2T = sb("xn2T", [P, TPB, KB, P])
        stats1 = sb("stats1", [P, TPB, 6])
        mv1 = sb("mv1", [P, TPB, 2])
        ve1 = sb("ve1", [P, TPB])
        rstd1 = sb("rstd1", [P, TPB])
        stats2 = sb("stats2", [P, TPB, 6])
        mv2 = sb("mv2", [P, TPB, 2])
        ve2 = sb("ve2", [P, TPB])
        rstd2 = sb("rstd2", [P, TPB])
        rmax = sb("rmax", [P, TPB])
        rdiff = sb("rdiff", [P, TPB, EXPERTS])
        rexp = sb("rexp", [P, TPB, EXPERTS])
        rtot = sb("rtot", [P, TPB])
        rinv = sb("rinv", [P, TPB])
        prob = sb("prob", [P, TPB, EXPERTS])

        x_in = [sem(f"x_in{p}") for p in range(2)]
        c_in = [sem(f"c_in{p}") for p in range(2)]
        xres_in = [sem(f"xres_in{p}") for p in range(2)]
        x1_stored = [sem(f"x1_stored{p}") for p in range(2)]
        rows_stored = [sem(f"rows_stored{p}") for p in range(2)]
        ones_set = sem("ones_set")
        waited = sem("waited")
        ln1_stats, ln1_mv, ln1_ve, ln1_rstd, xn_ready = map(sem, ("ln1_stats", "ln1_mv", "ln1_ve", "ln1_rstd", "xn_ready"))
        ln2_stats, ln2_mv, ln2_ve, ln2_rstd, xn2_ready = map(sem, ("ln2_stats", "ln2_mv", "ln2_ve", "ln2_rstd", "xn2_ready"))
        filled = [sem(f"filled{n}") for n in range(2)]
        drained = [sem(f"drained{n}") for n in range(2)]
        x_hi, c_hi, a_hi = map(sem, ("x_hi", "c_hi", "a_hi"))
        xb_ready = sem("xb_ready")
        s_done, least_done, e_done, t_done, et_done, pv_done = map(
            sem, ("s_done", "least_done", "e_done", "t_done", "et_done", "pv_done"))
        sums_inv, norm_done = sem("sums_inv"), sem("norm_done")
        r_max, r_exp, r_tot, r_inv, prob_ready, score_kept = map(
            sem, ("r_max", "r_exp", "r_tot", "r_inv", "prob_ready", "score_kept"))

        x_v = a["x"].rearrange("b (t p) d -> b p t d", p=P)
        c_v = a["ctx_1024"].rearrange("b (t p) d -> b p t d", p=P)
        out_v = out.rearrange("b (t p) d -> b p t d", p=P)
        rows_v = rows_dram[:, :].rearrange("(b t p) d -> b p t d", p=P, t=TPB)

        def wait(eng, semaphore, value):
            if not isinstance(value, int) or value > 0:
                eng.wait_ge(semaphore, value)

        def wait_banks(eng, semaphores, b, whats, banks=(0, 1)):
            for bank in banks:
                of_bank = [w for w in whats if of_row(w, b)[0] == bank]
                if of_bank:
                    eng.wait_ge(semaphores[bank], of_row(max(of_bank, key=ORDER.index), b)[1])

        def wait_filled(eng, b, *whats):
            wait_banks(eng, filled, b, whats)

        def wait_drained(eng, b, *whats):
            wait_banks(eng, drained, b, whats)

        def exists(b):
            return not isinstance(b, int) or b >= 0

        def at_start(i):
            return isinstance(i, int) and i == -1

        def steps(eng, step):
            for i in range(-1, STEADY[0]):
                step(i, i % 2, i // 2)
            first = STEADY[0]
            with eng.Fori(0, (STEADY[1] - first) // 2) as j:
                for k in range(2):
                    step(2 * j + (first + k), (first + k) % 2, j + (first + k) // 2)
            for i in range(STEADY[1], LAST + 1):
                step(i, i % 2, i // 2)

        block = ctx.enter_context(nc.Block())

        @block.sync
        def _(sp):
            def load_x(b):
                if b >= 2:
                    sp.wait_ge(xn_ready, TPB * (b - 1))
                sp.dma_start(xin[b % 2][:], x_v[b]).then_inc(x_in[b % 2], 16)

            def load_c(b):
                if b >= 2:
                    wait_filled(sp, b - 2, "CT1")
                sp.dma_start(cin[b % 2][:], c_v[b]).then_inc(c_in[b % 2], 16)

            def step(i, p, h):
                if not isinstance(i, int) or i + 2 < BATCH:
                    wait(sp, xn_ready, TPB * (i + 1))
                    sp.dma_start(xin[p][:], x_v[i + 2]).then_inc(x_in[p], 16)
                    if exists(i):
                        wait_filled(sp, i, "CT1")
                    sp.dma_start(cin[p][:], c_v[i + 2]).then_inc(c_in[p], 16)
                if "A" in stages(i):
                    if exists(i - 2):
                        sp.wait_ge(x1_stored[p], 16 * h)
                    sp.dma_start(x1[p][:], x_v[i]).then_inc(xres_in[p], 16)
                if "U" in stages(i):
                    q = 1 - p
                    wait_drained(sp, i - 1, "O1")
                    sp.dma_start(out_v[i - 1], x1[q][:]).then_inc(x1_stored[q], 16)
                    sp.wait_ge(prob_ready, i)
                    sp.dma_start(rows_v[i - 1], rows[q][:]).then_inc(rows_stored[q], 16)

            sp.dma_start(xin[0][:], x_v[0]).then_inc(x_in[0], 16)
            sp.dma_start(cin[0][:], c_v[0]).then_inc(c_in[0], 16)
            for i in range(-1, STEADY[0]):
                step(i, i % 2, i // 2)
            first = STEADY[0]
            with sp.Fori(0, (STEADY[1] - 1 - first) // 2) as j:
                for k in range(2):
                    step(2 * j + (first + k), (first + k) % 2, j + (first + k) // 2)
            for i in range(first + (STEADY[1] - 1 - first) // 2 * 2, LAST + 1):
                step(i, i % 2, i // 2)
            for p in range(2):
                sp.wait_ge(x1_stored[p], 16 * (BATCH // 2))
                sp.wait_ge(rows_stored[p], 16 * (BATCH // 2))

        @block.gpsimd
        def _(pool):
            def normalise(x, mv, ve, rstd, to, ready_mv, n_mv, s_ve, n_ve, s_rstd, s_to):
                pool.wait_ge(ready_mv, n_mv)
                pool.sem_inc(waited)
                pool.tensor_scalar(ve, mv[:, :, 1], EPS, None, ALU.add).then_inc(s_ve, 1)
                pool.wait_ge(s_ve, n_ve + 1)
                pool.tensor_tensor(rstd, ve, half[:, 0:ve.shape[1]], ALU.pow).then_inc(s_rstd, 1)
                pool.wait_ge(s_rstd, n_ve + 1)
                pool.sem_inc(waited)

            def norm1(b, p, h):
                normalise(None, mv1, ve1[:], rstd1[:], None, ln1_mv, TPB * (b + 1), ln1_ve, b, ln1_rstd, None)
                if exists(b - 1):
                    wait_filled(pool, b - 1, "XT1")
                pool.sem_inc(waited)
                for t in range(TPB):
                    pool.tensor_scalar(xn[:, t, :], xin[p][:, t, :], mv1[:, t, 0:1], rstd1[:, t:t + 1],
                                       ALU.subtract, ALU.mult).then_inc(xn_ready, 1)

            def norm2(b, p, h, t):
                normalise(None, mv2[:, t:t + 1, :], ve2[:, t:t + 1], rstd2[:, t:t + 1], None, ln2_mv,
                          TPB * b + t + 1, ln2_ve, TPB * b + t, ln2_rstd, None)
                if t == 0 and exists(b - 2):
                    pool.wait_ge(rows_stored[p], 16 * h)
                pool.sem_inc(waited)
                pool.tensor_scalar(rows[p][:, t, 0:D], x1[p][:, t, :], mv2[:, t, 0:1], rstd2[:, t:t + 1],
                                   ALU.subtract, ALU.mult).then_inc(xn2_ready, 1)

            def step(i, p, h):
                q = 1 - p
                hq = h if p else h - 1
                if "U" in stages(i):
                    pool.wait_ge(xres_in[q], 16 * (hq + 1))
                    pool.tensor_tensor(x1[q][:], x1[q][:], bo[:, None, :].to_broadcast([P, TPB, D]),
                                       ALU.add).then_inc(xb_ready, 1)
                if "P" in stages(i):
                    norm1(i + 1, q, None)
                if "U" in stages(i):
                    for t in range(TPB):
                        norm2(i - 1, q, hq, t)
                    pool.wait_ge(prob_ready, i)
                    pool.tensor_copy(scores[:, :, :, bass.ds(i - 1, 1)], prob[:, :, :, None]).then_inc(score_kept, 1)

            steps(pool, step)

        @block.scalar
        def _(act):
            def exp_head(n, e):
                act.wait_ge(least_done, n + 1)
                act.activation(E[e][:, 0:P], E[e][:, 0:P], ACT.Exp, bias=least[e][:, 0:1], scale=-1.0)
                act.activation(E[e][:, P:3 * P], E[e][:, P:3 * P], ACT.Exp, bias=least[e][:, 1:2],
                               scale=-1.0).then_inc(e_done, 1)

            def evacuate(what, i, p):
                bank, n = fill(i, what)
                w = W[bank]
                b, q = i + 1, 1 - p
                two = w[:, :].rearrange("p (k s) -> p k s", k=2)
                if what in ("XT0", "XT1", "CT0", "CT1", "AT0", "AT1"):
                    k = 2 * int(what[-1])
                    to, s_hi = {"X": (xnT, x_hi), "C": (cT, c_hi), "A": (aT, a_hi)}[what[0]]
                    if what == "XT0" and exists(b - 1):
                        wait_filled(act, b - 1, "Q3")
                    if what == "CT0" and exists(b - 1):
                        wait_filled(act, b - 1, "K1", "V1")
                    if what == "AT0" and exists(i - 2):
                        wait_filled(act, i - 2, "O1")
                    act.wait_ge(filled[bank], n)
                    act.activation(to[0][:, k:k + 2, :], two, ACT.Copy).then_inc(s_hi, 1)
                if what in ("Q0", "Q2", "Q3", "K0", "K1"):
                    k = {"Q0": 0, "Q2": 2, "Q3": 3, "K0": 0, "K1": 2}[what]
                    last = k + (1 if what in ("Q0", "K0", "K1") else 0)
                    to, bias = (QT[q], bq) if what[0] == "Q" else (KT[q], bk)
                    if what in ("Q0", "K0") and exists(b - 2):
                        act.wait_ge(s_done, HEADS * (b - 1))
                    act.wait_ge(filled[bank], n)
                    for f in range(k, last + 1):
                        ins = act.activation(to[:, f, :], two[:, f - k, :], ACT.Identity, bias=bias[:, f:f + 1])
                    ins.then_inc(drained[bank], 1)
                if what in ("X2T0", "X2T1"):
                    t = int(what[-1])
                    if t == 0 and exists(i - 2):
                        wait_filled(act, i - 2, "R")
                    act.wait_ge(filled[bank], n)
                    act.activation(xn2T[:, t, :, :], w[:, :].rearrange("p (k s) -> p k s", k=KB),
                                   ACT.Copy).then_inc(drained[bank], 1)
                if what == "R":
                    bank, n = fill(i, "R")
                    act.wait_ge(drained[bank], n)
                    act.activation(rexp[:], rdiff[:], ACT.Exp).then_inc(r_exp, 1)

            def step(i, p, h):
                for n in range(HEADS if "A" in stages(i) else 1):
                    if "A" in stages(i):
                        g = i * HEADS + n
                        act.wait_ge(t_done, g + 1)
                        wait(act, pv_done, g - 1)
                        act.activation(ET[n % 2][:], PT[n % 2][:, 0:3 * P], ACT.Copy).then_inc(et_done, 1)
                        if n + 1 < HEADS or "P" in stages(i):
                            exp_head(g + 1, (n + 1) % 2)
                    for what, _, at in fills(i):
                        if at == n or "A" not in stages(i):
                            evacuate(what, i, p)
                if at_start(i):
                    exp_head(0, 0)

            steps(act, step)

        @block.vector
        def _(dve):
            def masked_scores(n, e):
                dve.wait_ge(s_done, n + 1)
                wait(dve, t_done, n - 1)
                dve.sem_inc(waited)
                for t, (lo, hi) in enumerate(((0, P), (P, 3 * P))):
                    ins = dve.tensor_tensor_reduce(out=E[e][:, lo:hi], in0=S[e][:, lo:hi], in1=mask[:, lo:hi],
                                                   scale=-SCALE, scalar=-MASKED, op0=ALU.add, op1=ALU.min,
                                                   accum_out=least[e][:, t:t + 1])
                ins.then_inc(least_done, 1)

            def normalise_group(g, p, fb):
                o = O[fb % 2][:, 0:TPB * HPB * VW].rearrange("p (t h v) -> p t h v", t=TPB, v=VW)
                flat = O[fb % 2][:, 0:TPB * HPB * VW].rearrange("p (g v) -> p g v", v=VW)
                dve.wait_ge(pv_done, HPB * (g + 1))
                dve.reciprocal(rsum[:, :], flat[:, :, DH]).then_inc(sums_inv, 1)
                dve.wait_ge(sums_inv, g + 1)
                inv = rsum[:, :].rearrange("p (t h) -> p t h", t=TPB)[:, :, :, None].to_broadcast([P, TPB, HPB, DH])
                dve.tensor_tensor(attn[p][:, :, fb * P:(fb + 1) * P].rearrange("p t (h v) -> p t h v", v=DH),
                                  o[:, :, :, 0:DH], inv, ALU.mult).then_inc(norm_done, 1)

            def ln1(b, p, h):
                dve.wait_ge(x_in[p], 16 * (h + 1))
                for t in range(TPB):
                    dve.bn_stats(stats1[:, t, :], xin[p][:, t, :]).then_inc(ln1_stats, 1)
                dve.wait_ge(ln1_stats, TPB * (b + 1))
                wait(dve, xn_ready, TPB * b)
                dve.sem_inc(waited)
                for t in range(TPB):
                    dve.bn_aggr(mv1[:, t, :], stats1[:, t, :]).then_inc(ln1_mv, 1)

            def evacuate(what, i, p):
                bank, n = fill(i, what)
                w = W[bank]
                b, q = i + 1, 1 - p
                two = w[:, :].rearrange("p (k s) -> p k s", k=2)
                if what in ("XT0", "XT1", "CT0", "CT1", "AT0", "AT1"):
                    f = int(what[-1])
                    k = 2 * f
                    to, s_hi = {"X": (xnT, x_hi), "C": (cT, c_hi), "A": (aT, a_hi)}[what[0]]
                    row = i - 1 if what[0] == "A" else b
                    dve.wait_ge(s_hi, 2 * row + f + 1)
                    dve.tensor_tensor(to[1][:, k:k + 2, :], two, to[0][:, k:k + 2, :].bitcast(F32),
                                      ALU.subtract).then_inc(drained[bank], 1)
                if what in ("V0", "V1"):
                    t = int(what[-1])
                    if t == 0 and exists(b - 2):
                        dve.wait_ge(pv_done, HEADS * (b - 1))
                    dve.wait_ge(filled[bank], n)
                    dve.tensor_tensor(V[q][:, t, :, 0:DH], w[:, :].rearrange("p (h v) -> p h v", v=DH),
                                      bv[:, :].rearrange("p (h v) -> p h v", v=DH), ALU.add).then_inc(drained[bank], 1)
                if what in ("O0", "O1"):
                    t = int(what[-1])
                    dve.wait_ge(filled[bank], n)
                    dve.wait_ge(xb_ready, i)
                    dve.scalar_tensor_tensor(out=x1[q][:, t, :], in0=w[:, :], scalar=tanh_g[:, 0:1],
                                             in1=x1[q][:, t, :], op0=ALU.mult, op1=ALU.add).then_inc(drained[bank], 1)
                    dve.wait_ge(drained[bank], n)
                    wait(dve, ln2_mv, TPB * (i - 2) + t + 1)
                    dve.bn_stats(stats2[:, t, :], x1[q][:, t, :]).then_inc(ln2_stats, 1)
                    dve.wait_ge(ln2_stats, TPB * (i - 1) + t + 1)
                    wait(dve, xn2_ready, TPB * (i - 2) + t + 1)
                    dve.sem_inc(waited)
                    dve.bn_aggr(mv2[:, t, :], stats2[:, t, :]).then_inc(ln2_mv, 1)
                if what == "R":
                    logits = w[:, 0:TPB * EXPERTS].rearrange("p (t e) -> p t e", t=TPB)
                    dve.wait_ge(filled[bank], n)
                    dve.tensor_reduce(rmax[:], logits, AX, ALU.max).then_inc(r_max, 1)
                    dve.wait_ge(r_max, i)
                    wait(dve, r_exp, i - 1)
                    dve.tensor_tensor(rdiff[:], logits, rmax[:, :, None].to_broadcast([P, TPB, EXPERTS]),
                                      ALU.subtract).then_inc(drained[bank], 1)

            def router_end(i, p):
                q = 1 - p
                dve.wait_ge(r_exp, i)
                dve.tensor_reduce(rtot[:], rexp[:], AX, ALU.add).then_inc(r_tot, 1)
                dve.wait_ge(r_tot, i)
                dve.reciprocal(rinv[:], rtot[:]).then_inc(r_inv, 1)
                dve.wait_ge(r_inv, i)
                inv = rinv[:, :, None].to_broadcast([P, TPB, EXPERTS])
                wait(dve, score_kept, i - 1)
                dve.tensor_tensor(prob[:], rexp[:], inv, ALU.mult)
                dve.tensor_tensor(rows[q][:, :, D:ROW], rexp[:], inv, ALU.mult).then_inc(prob_ready, 1)

            def step(i, p, h):
                if at_start(i):
                    for p2 in range(2):
                        dve.memset(V[p2][:, :, :, DH:VW], 1.0).then_inc(ones_set, 1)
                if "P" in stages(i):
                    ln1(i + 1, 1 - p, h if not p else (h + 1))
                for n in range(HEADS if "A" in stages(i) else 1):
                    if "A" in stages(i):
                        g = i * HEADS + n
                        if n + 1 < HEADS or "P" in stages(i):
                            masked_scores(g + 1, (n + 1) % 2)
                        if n % HPB == 0 and n > 0:
                            normalise_group(i * KB + n // HPB - 1, p, n // HPB - 1)
                    if n == 0 and "U" in stages(i):
                        normalise_group(i * KB - 1, 1 - p, KB - 1)
                    if n == 1 and "A" in stages(i) and exists(i - 2):
                        pass
                    for what, _, at in fills(i):
                        if at == n or "A" not in stages(i):
                            evacuate(what, i, p)
                    if "U" in stages(i) and n == (12 if "A" in stages(i) else 0):
                        router_end(i, p)
                if at_start(i):
                    masked_scores(0, 0)

            steps(dve, step)

        @block.tensor
        def _(pe):
            def scores_of(i, p, n):
                fb, j = divmod(n, HPB)
                rows_ = slice(DH * j, DH * (j + 1))
                g = i * HEADS + n
                if j == 0:
                    wait_drained(pe, i, ("Q0", "Q0", "Q2", "Q3")[fb], ("K0", "K0", "K1", "K1")[fb])
                wait(pe, least_done, g - 1)
                s = S[n % 2]
                pe.matmul(s[:, 0:P], QT[p][rows_, fb, 0:P], KT[p][rows_, fb, 0:P], start=True, stop=True)
                pe.matmul(s[:, P:3 * P], QT[p][rows_, fb, P:2 * P], KT[p][rows_, fb, 0:2 * P],
                          start=True, stop=True).then_inc(s_done, 1)

            def turn(i, n):
                g = i * HEADS + n
                pe.wait_ge(e_done, g + 1)
                wait(pe, et_done, g - 1)
                for k in range(3):
                    ins = pe.transpose(PT[n % 2][:, k * P:(k + 1) * P], E[n % 2][:, k * P:(k + 1) * P], ident[:])
                ins.then_inc(t_done, 1)

            def values_of(i, p, n):
                fb, j = divmod(n, HPB)
                g = i * HEADS + n
                if n == 0:
                    wait_drained(pe, i, "V0", "V1")
                    if isinstance(i, int) and i == 0:
                        pe.wait_ge(ones_set, 2)
                pe.wait_ge(et_done, g + 1)
                if j == 0:
                    wait(pe, norm_done, i * KB + fb - 1)
                o = O[fb % 2]
                at0, at1 = j * VW, (HPB + j) * VW
                et, v = ET[n % 2], V[p]
                pe.matmul(o[:, at0:at0 + VW], et[:, 0:P], v[:, 0, n, :], start=True, stop=True)
                pe.matmul(o[:, at1:at1 + VW], et[:, P:2 * P], v[:, 0, n, :], start=True, stop=False)
                pe.matmul(o[:, at1:at1 + VW], et[:, 2 * P:3 * P], v[:, 1, n, :], start=False,
                          stop=True).then_inc(pv_done, 1)

            def products(to, pairs):
                n = 3 * len(pairs)
                at = 0
                for (lh, ll), (rh, rl) in pairs:
                    for x, y in ((lh, rh), (lh, rl), (ll, rh)):
                        ins = pe.matmul(to, x, y, start=(at == 0), stop=(at == n - 1))
                        at += 1
                return ins

            def filling(what, i, p):
                bank, n = fill(i, what)
                w = W[bank]
                b, q = i + 1, 1 - p
                wait(pe, drained[bank], n - 1)
                if what in ("XT0", "XT1", "CT0", "CT1", "AT0", "AT1"):
                    k0 = 2 * int(what[-1])
                    if what[0] == "X":
                        src = xn
                        pe.wait_ge(xn_ready, TPB * (b + 1))
                    elif what[0] == "C":
                        src = cin[q]
                        pe.wait_ge(c_in[q], 16 * (hrow(b, q)))
                    else:
                        src = attn[q]
                        pe.wait_ge(norm_done, KB * i)
                    for k in range(2):
                        for t in range(TPB):
                            ins = pe.transpose(w[:, (k * TPB + t) * P:(k * TPB + t + 1) * P],
                                               src[:, t, (k0 + k) * P:(k0 + k + 1) * P], ident[:])
                if what in ("Q0", "Q2", "Q3", "K0", "K1"):
                    if what == "Q0":
                        wait_banks(pe, drained, b, ("XT0", "XT1"), (1 - bank,))
                    if what == "K0":
                        wait_banks(pe, drained, b, ("CT0", "CT1"), (1 - bank,))
                    k = {"Q0": 0, "Q2": 2, "Q3": 3, "K0": 0, "K1": 2}[what]
                    last = k + (1 if what in ("Q0", "K0", "K1") else 0)
                    name, src = ("wq", xnT) if what[0] == "Q" else ("wk", cT)
                    for f in range(k, last + 1):
                        cols = slice(f * P, (f + 1) * P)
                        ins = products(w[:, (f - k) * SEQ:(f - k + 1) * SEQ],
                                       [((w_hi[name][:, c, cols], w_lo[name][:, c, cols]),
                                         (src[0][:, c, :], src[1][:, c, :])) for c in range(KB)])
                if what in ("V0", "V1", "O0", "O1"):
                    if what == "O0":
                        wait_banks(pe, drained, i - 1, ("AT0", "AT1"), (1 - bank,))
                    if what == "V0":
                        wait_banks(pe, drained, b, ("CT0", "CT1"), (1 - bank,))
                    t = int(what[-1])
                    cols = slice(t * P, (t + 1) * P)
                    name, src = ("wv", cT) if what[0] == "V" else ("wo", aT)
                    ins = products(w[:, :], [((src[0][:, c, cols], src[1][:, c, cols]),
                                              (w_hi[name][:, c, :], w_lo[name][:, c, :])) for c in range(KB)])
                if what in ("X2T0", "X2T1"):
                    t = int(what[-1])
                    pe.wait_ge(xn2_ready, TPB * (i - 1) + t + 1)
                    for k in range(KB):
                        ins = pe.transpose(w[:, k * P:(k + 1) * P], rows[q][:, t, k * P:(k + 1) * P], ident[:])
                if what == "R":
                    wait_banks(pe, drained, i - 1, ("X2T0", "X2T1"), (1 - bank,))
                    for t in range(TPB):
                        for k in range(KB):
                            ins = pe.matmul(w[:, t * EXPERTS:(t + 1) * EXPERTS], xn2T[:, t, k, :], wr[:, k, :],
                                            start=(k == 0), stop=(k == KB - 1))
                ins.then_inc(filled[bank], 1)

            halves_of = {}

            def hrow(b, q):
                return halves_of["h"] + 1

            def step(i, p, h):
                halves_of["h"] = h if not p else h + 1
                for n in range(HEADS if "A" in stages(i) else 1):
                    if "A" in stages(i):
                        if n + 1 < HEADS:
                            scores_of(i, p, n + 1)
                        turn(i, n)
                    for what, _, at in fills(i):
                        if at == n or "A" not in stages(i):
                            filling(what, i, p)
                    if "A" in stages(i):
                        values_of(i, p, n)
                if "P" in stages(i):
                    scores_of(i + 1, 1 - p, 0)

            steps(pe, step)


def weights_setup(nc, a, const_ready, ident, mask, half, bq, bk, bv, bo, wr, tanh_g, w_hi, w_lo, names, W, sem):
    ctx = ExitStack()
    with ctx:
        raw = {n: ctx.enter_context(nc.sbuf_tensor(n + "_raw", [P, KB, D], F32)) for n in names}
        gates = ctx.enter_context(nc.sbuf_tensor("gates", [P, 2], F32))
        bo_raw = ctx.enter_context(nc.sbuf_tensor("bo_raw", [P, D], F32))
        w_in = {n: sem(n + "_in") for n in names}
        small_in, cleared, ident_ready = map(sem, ("small_in", "cleared", "ident_ready"))
        gate_ready, bo_ready = sem("gate_ready"), sem("bo_ready")
        w_turned, w_hi_done, w_lo_done = map(sem, ("w_turned", "w_hi_done", "w_lo_done"))
        block = ctx.enter_context(nc.Block())
        small = 7

        @block.sync
        def _(sp):
            for n in names:
                src = a[f"L0_xattn_{n}_w"].rearrange("(f p) d -> p f d", p=P)
                sp.dma_start(raw[n][:], src).then_inc(w_in[n], 16)

        @block.gpsimd
        def _(pool):
            pool.memset(ident[:], 0.0).then_inc(cleared, 1)
            pool.memset(mask[:], 0.0).then_inc(cleared, 1)
            pool.memset(half[:], -0.5).then_inc(const_ready, 1)
            pool.wait_ge(cleared, 2)
            pool.affine_select(out=ident[:], in_=ident[:], compare_op=ALU.not_equal, fill=1.0, base=0,
                               pattern=[[-1, P]], channel_multiplier=1).then_inc(ident_ready, 1)
            for c in (0, 2):
                pool.affine_select(out=mask[:, c * P:(c + 1) * P], in_=mask[:, c * P:(c + 1) * P],
                                   compare_op=ALU.is_ge, fill=MASKED, base=0, pattern=[[-1, P]],
                                   channel_multiplier=1).then_inc(const_ready, 1)
            with nc.allow_non_contiguous_dma(reason="512 words of each bias"):
                pool.dma_start(bq[:], a["L0_xattn_wq_b"].rearrange("(f p) -> p f", p=P)).then_inc(small_in, 16)
                pool.dma_start(bk[:], a["L0_xattn_wk_b"].rearrange("(f p) -> p f", p=P)).then_inc(small_in, 16)
                pool.dma_start(wr[:], a["L0_ffn_Wr"].rearrange("(k p) e -> p k e", p=P)).then_inc(small_in, 16)
            pool.dma_start(bv[:], a["L0_xattn_wv_b"].partition_broadcast(P)).then_inc(small_in, 16)
            pool.dma_start(bo_raw[:], a["L0_xattn_wo_b"].partition_broadcast(P)).then_inc(small_in, 16)
            pool.dma_start(gates[:, 0:1], a["g_xattn"].partition_broadcast(P)).then_inc(small_in, 16)
            pool.dma_start(gates[:, 1:2], a["g_ffn"].partition_broadcast(P)).then_inc(small_in, 16)
            pool.wait_ge(small_in, 16 * small)
            pool.wait_ge(gate_ready, 1)
            pool.tensor_scalar(bo[:], bo_raw[:], tanh_g[:, 0:1], None, ALU.mult).then_inc(bo_ready, 1)

        @block.scalar
        def _(act):
            act.wait_ge(small_in, 16 * small)
            act.activation(tanh_g[:], gates[:], ACT.Tanh).then_inc(gate_ready, 1)
            for n, name in enumerate(names):
                for k in range(KB):
                    f = n * KB + k
                    act.wait_ge(w_turned, f + 1)
                    act.activation(w_hi[name][:, k, :], W[f % 2][:, :], ACT.Copy).then_inc(w_hi_done, 1)

        @block.vector
        def _(dve):
            for n, name in enumerate(names):
                for k in range(KB):
                    f = n * KB + k
                    dve.wait_ge(w_hi_done, f + 1)
                    dve.tensor_tensor(w_lo[name][:, k, :], W[f % 2][:, :], w_hi[name][:, k, :].bitcast(F32),
                                      ALU.subtract).then_inc(w_lo_done, 1)

        @block.tensor
        def _(pe):
            pe.wait_ge(ident_ready, 1)
            for n, name in enumerate(names):
                pe.wait_ge(w_in[name], 16)
                for k in range(KB):
                    f = n * KB + k
                    if f >= 2:
                        pe.wait_ge(w_lo_done, f - 1)
                    for c in range(KB):
                        ins = pe.transpose(W[f % 2][:, c * P:(c + 1) * P], raw[name][:, c, k * P:(k + 1) * P], ident[:])
                    ins.then_inc(w_turned, 1)


def load_block(sp, a, raw1, raw2, w_in, e, m):
    w1 = a["L0_ffn_W1"].rearrange("e (k p) (m h) -> e m p k h", p=P, h=P)
    w2 = a["L0_ffn_W2"].rearrange("e (m p) d -> e m p d", p=P)
    sp.dma_start(raw1[m % 2][:], w1[e, m]).then_inc(w_in[m % 2], 16)
    sp.dma_start(raw2[m % 2][:], w2[e, m]).then_inc(w_in[m % 2], 16)


def selection_phase(nc, a, ident, scores, ring, raw1, raw2, w_in, index, b1, psum, sem):
    ctx = ExitStack()
    TOP_BIT = 29
    NT = N // P
    NS = TOPK // P
    with ctx:
        def sb(name, shape, dt=F32):
            return ctx.enter_context(nc.sbuf_tensor(name, shape, dt))

        sc = sb("sc", [P, CHUNK])
        same = sb("same_expert", [P, P], BF16)
        before = sb("chunks_before", [P, P], BF16)
        seen = sb("seen", [P, CHUNK])
        cand = sb("cand", [P, 1], I32)
        bit = [sb(f"bit{p}", [P, 1]) for p in range(2)]
        next_bit = sb("next_bit", [P, 1], I32)
        undo = sb("undo", [P, 1], I32)
        count = sb("count", [P, 1], BF16)
        larger = sb("larger", [P, CHUNK])
        equal = sb("equal", [P, CHUNK])
        zeros = sb("zeros", [P, CHUNK])
        rank = sb("rank", [P, CHUNK])
        taken = sb("taken", [P, CHUNK])
        chosen = sb("chosen", [P, CHUNK])
        place = sb("place", [P, CHUNK])
        need = sb("need", [P, 1])
        offset = sb("offset", [P, 1])
        place_i = sb("place_i", [P, TPB, P], I32)
        part_i = sb("part_i", [P, 2, TPB * P], I32)
        part = sb("part", [P, 2, TPB, P], BF16)
        iota_i = sb("iota_i", [P, P], I32)
        iota = sb("iota", [P, P], BF16)
        tile_i = sb("tile_i", [P, TPB, BATCH], I32)
        tile_no = sb("tile_no", [P, TPB, BATCH], BF16)
        lane_i = sb("lane_i", [P, 1], I32)
        lane = sb("lane", [P, 1])
        slot = [sb(f"slot{p}", [P, TPB, BATCH, P], BF16) for p in range(2)]
        column = [sb(f"column{p}", [P, TPB, BATCH, NS], BF16) for p in range(2)]
        token = [sb(f"token{p}", [P, TPB, BATCH, NS, 2], BF16) for p in range(2)]
        found = sb("found", [P, EXPERTS, NS, 2])

        consts, sc_turned, sc_ready = sem("sel_consts"), sem("sc_turned"), sem("sc_ready")
        made, counted, summed = sem("made"), sem("counted"), sem("summed")
        cand_ready, bit_ready, undo_ready = sem("cand_ready"), sem("bit_ready"), sem("undo_ready")
        made_up = sem("made_up")
        step_done, turned, sums = sem("step_done"), sem("place_turned"), sem("chunk_sums")
        hot_ready, hot_used, index_ready = sem("hot_ready"), sem("hot_used"), sem("index_ready")
        column_ready = sem("column_ready")
        w_hi_done, w_lo_done, b1_in = sem("w_hi_first"), sem("w_lo_first"), sem("b1_in")
        block = ctx.enter_context(nc.Block())

        @block.sync
        def _(sp):
            with nc.allow_non_contiguous_dma(reason="the experts' first biases, one word to a partition"):
                sp.dma_start(b1[:], a["L0_ffn_b1"].rearrange("e (m p) -> p e m", p=P)).then_inc(b1_in, 16)
            for m in range(HB):
                if m >= 2:
                    sp.wait_ge(w_lo_done, m - 1)
                load_block(sp, a, raw1, raw2, w_in, 0, m)
            sp.wait_ge(b1_in, 16)

        @block.scalar
        def _(act):
            for m in range(HB):
                act.wait_ge(w_in[m % 2], 32 * (m // 2 + 1))
                act.activation(ring["w1_hi"][:, m], raw1[m % 2][:], ACT.Copy)
                act.activation(ring["w2_hi"][:, m], raw2[m % 2][:], ACT.Copy).then_inc(w_hi_done, 1)

        @block.gpsimd
        def _(pool):
            pool.memset(same[:], 1.0).then_inc(made, 1)
            pool.wait_ge(made, 1)
            by_expert = same[:].rearrange("p (e c) -> p e c", c=CHUNKS)
            pool.affine_select(out=by_expert, in_=by_expert, compare_op=ALU.is_ge, fill=0.0, base=0,
                               pattern=[[-CHUNKS, EXPERTS], [0, CHUNKS]], channel_multiplier=1).then_inc(made, 1)
            pool.wait_ge(made, 2)
            pool.affine_select(out=by_expert, in_=by_expert, compare_op=ALU.is_ge, fill=0.0, base=CHUNKS - 1,
                               pattern=[[CHUNKS, EXPERTS], [0, CHUNKS]], channel_multiplier=-1).then_inc(made, 1)
            pool.wait_ge(made, 3)
            pool.affine_select(out=before[:], in_=same[:], compare_op=ALU.is_gt, fill=0.0, base=0,
                               pattern=[[1, P]], channel_multiplier=-1).then_inc(made, 1)
            pool.iota(iota_i[:], pattern=[[1, P]], base=0, channel_multiplier=0).then_inc(made, 1)
            pool.iota(tile_i[:], pattern=[[1, TPB], [TPB, BATCH]], base=0, channel_multiplier=0).then_inc(made, 1)
            pool.iota(lane_i[:], pattern=[[0, 1]], base=0, channel_multiplier=1).then_inc(made, 1)
            pool.wait_ge(made, 7)
            pool.tensor_copy(iota[:], iota_i[:]).then_inc(consts, 1)
            pool.tensor_copy(tile_no[:], tile_i[:]).then_inc(consts, 1)
            pool.tensor_copy(lane[:], lane_i[:]).then_inc(consts, 1)
            for m in range(HB):
                pool.wait_ge(w_hi_done, m + 1)
                pool.tensor_tensor(ring["w1_lo"][:, m], raw1[m % 2][:], ring["w1_hi"][:, m].bitcast(F32), ALU.subtract)
                pool.tensor_tensor(ring["w2_lo"][:, m], raw2[m % 2][:], ring["w2_hi"][:, m].bitcast(F32),
                                   ALU.subtract).then_inc(w_lo_done, 1)

        @block.vector
        def _(dve):
            dve.memset(zeros[:], 0.0).then_inc(step_done, 1)
            dve.memset(cand[:], 1 << TOP_BIT).then_inc(step_done, 1)
            dve.memset(bit[0][:], float(1 << TOP_BIT)).then_inc(step_done, 1)
            dve.wait_ge(sc_turned, 1)
            dve.tensor_copy(sc[:], psum[0][:, 0:CHUNK]).then_inc(sc_ready, 1)
            dve.wait_ge(sc_ready, 1)
            dve.wait_ge(step_done, 3)

            with dve.Fori(1, TOP_BIT + 2, 2) as it:
                for k in range(2):
                    n = it + k
                    dve.tensor_scalar(seen[:], sc[:], cand[:].bitcast(F32), 0.0, ALU.is_ge, ALU.add,
                                      accum_out=count[:]).then_inc(counted, 1)
                    dve.tensor_scalar(bit[1 - k][:], bit[k][:], 0.5, None, ALU.mult)
                    dve.tensor_scalar(next_bit[:], bit[k][:], 0.5, None, ALU.mult).then_inc(bit_ready, 1)
                    dve.wait_ge(summed, n)
                    dve.tensor_scalar(undo[:], psum[1][:, 0:1], float(TOPK), bit[k][:, 0:1], ALU.is_lt,
                                      ALU.mult).then_inc(undo_ready, 1)
                    dve.wait_ge(undo_ready, n)
                    dve.wait_ge(bit_ready, n)
                    dve.tensor_tensor(undo[:], undo[:], next_bit[:], ALU.bitwise_or).then_inc(made_up, 1)
                    dve.wait_ge(made_up, n)
                    dve.tensor_tensor(cand[:], cand[:], undo[:], ALU.bitwise_xor).then_inc(cand_ready, 1)
                    dve.wait_ge(cand_ready, n)

            limit = cand[:].bitcast(F32)
            done = [3]

            def then(ins):
                done[0] += 1
                ins.then_inc(step_done, 1)
                dve.wait_ge(step_done, done[0])

            dve.tensor_scalar(larger[:], sc[:], limit, 0.0, ALU.is_gt, ALU.add, accum_out=count[:]).then_inc(sums, 1)
            then(dve.tensor_scalar(equal[:], sc[:], limit, None, ALU.is_equal))
            then(dve.tensor_tensor_scan(rank[:], equal[:], zeros[:], 0.0, ALU.add, ALU.add))
            dve.wait_ge(turned, 1)
            dve.tensor_scalar(need[:], psum[1][:, 0:1], -1.0, float(TOPK), ALU.mult, ALU.add)
            then(dve.tensor_copy(count[:], rank[:, CHUNK - 1:CHUNK]))
            dve.sem_inc(sums)
            dve.wait_ge(turned, 2)
            then(dve.tensor_copy(offset[:], psum[2][:, 0:1]))
            then(dve.tensor_scalar(taken[:], rank[:], offset[:, 0:1], need[:, 0:1], ALU.add, ALU.is_le))
            then(dve.tensor_tensor(taken[:], taken[:], equal[:], ALU.mult))
            then(dve.tensor_tensor(chosen[:], taken[:], larger[:], ALU.add))
            then(dve.tensor_tensor_scan(rank[:], chosen[:], zeros[:], 0.0, ALU.add, ALU.add))
            then(dve.tensor_copy(count[:], rank[:, CHUNK - 1:CHUNK]))
            dve.sem_inc(sums)
            dve.wait_ge(turned, 3)
            then(dve.tensor_copy(offset[:], psum[3][:, 0:1]))
            dve.scalar_tensor_tensor(out=place[:], in0=rank[:], scalar=offset[:, 0:1], in1=chosen[:],
                                     op0=ALU.add, op1=ALU.mult).then_inc(sums, 1)
            dve.wait_ge(turned, 4)
            then(dve.tensor_scalar(place_i[:].rearrange("p t f -> p (t f)"), psum[4][:, 0:TPB * P], -1.0, None, ALU.add))
            flat = place_i[:].rearrange("p t f -> p (t f)")
            dve.tensor_scalar(part_i[:, 0], flat, P - 1, None, ALU.bitwise_and)
            then(dve.tensor_scalar(part_i[:, 1], flat, P.bit_length() - 1, None, ALU.arith_shift_right))
            then(dve.tensor_copy(part[:].rearrange("p a t f -> p (a t f)"), part_i[:].rearrange("p a f -> p (a f)")))
            dve.wait_ge(consts, 3)
            shape = [P, TPB, BATCH]
            for e in range(EXPERTS):
                cols = slice(e * CHUNKS, (e + 1) * CHUNKS)
                if e >= 2:
                    dve.wait_ge(hot_used, e - 1)
                for t in range(TPB):
                    dve.tensor_tensor(slot[e % 2][:, t], iota[:, None, :].to_broadcast([P, BATCH, P]),
                                      part[:, 0, t, cols, None].to_broadcast([P, BATCH, P]), ALU.is_equal)
                    ins = dve.tensor_tensor(column[e % 2][:, t], iota[:, None, 0:NS].to_broadcast([P, BATCH, NS]),
                                      part[:, 1, t, cols, None].to_broadcast([P, BATCH, NS]), ALU.is_equal)
                ins.then_inc(column_ready, 1)
                dve.wait_ge(column_ready, e + 1)
                for t in range(TPB):
                    dve.tensor_tensor(token[e % 2][:, t, :, :, 0], column[e % 2][:, t],
                                      tile_no[:, t, :, None].to_broadcast([P, BATCH, NS]), ALU.mult)
                    ins = dve.tensor_scalar(token[e % 2][:, t, :, :, 1], column[e % 2][:, t], lane[:, 0:1], None, ALU.mult)
                ins.then_inc(hot_ready, 1)
            dve.wait_ge(hot_used, EXPERTS)
            then(dve.tensor_copy(found[:].rearrange("p e s v -> p (e s v)"), psum[5][:, 0:EXPERTS * NS * 2]))
            dve.scalar_tensor_tensor(out=index[:], in0=found[:, :, :, 0], scalar=float(P), in1=found[:, :, :, 1],
                                     op0=ALU.mult, op1=ALU.add)

        @block.tensor
        def _(pe):
            for t in range(TPB):
                ins = pe.transpose(psum[0][:, t * P:(t + 1) * P], scores[:, t].rearrange("p e c -> p (e c)"), ident[:])
            ins.then_inc(sc_turned, 1)
            pe.wait_ge(made, 4)
            with pe.Fori(1, TOP_BIT + 2) as n:
                pe.wait_ge(counted, n)
                pe.matmul(psum[1][:, 0:1], same[:], count[:], start=True, stop=True).then_inc(summed, 1)
            for k, m in enumerate((same, before, before)):
                pe.wait_ge(sums, k + 1)
                pe.matmul(psum[1 + k][:, 0:1], m[:], count[:], start=True, stop=True).then_inc(turned, 1)
            pe.wait_ge(sums, 4)
            for t in range(TPB):
                ins = pe.transpose(psum[4][:, t * P:(t + 1) * P], place[:, t * P:(t + 1) * P], ident[:])
            ins.then_inc(turned, 1)
            for e in range(EXPERTS):
                pe.wait_ge(hot_ready, e + 1)
                to = psum[5][:, e * NS * 2:(e + 1) * NS * 2]
                for n in range(NT):
                    t, c = divmod(n, BATCH)
                    ins = pe.matmul(to, slot[e % 2][:, t, c, :], token[e % 2][:, t, c].rearrange("p s v -> p (s v)"),
                                    start=(n == 0), stop=(n == NT - 1))
                ins.then_inc(hot_used, 1)


def expert_phase(nc, a, out, rows_dram, ident, tanh_g, ring, raw1, raw2, w_in, index, b1, psum, sb_all, sem):
    ctx = ExitStack()
    LAST_E = EXPERTS - 1
    TURN_AT = 8
    with ctx:
        def sb(name, shape, dt=F32):
            return sb_all(name, shape, dt, ctx)

        xg = sb("xg", [P, STILES, ROW])
        xT = [[sb(f"xT{u}_{s}", [P, KB, SLOTS], F32R) for s in ("hi", "lo")] for u in range(2)]
        gate = [sb(f"gate{u}", [P, STILES]) for u in range(2)]
        picks = [sb(f"picks{u}", [P, STILES], U32) for u in range(2)]
        h = [sb(f"h{n}", [P, SLOTS]) for n in range(2)]
        h_hi = [sb(f"h_hi{n}", [P, SLOTS], F32R) for n in range(2)]
        h_lo = [sb(f"h_lo{n}", [P, SLOTS], F32R) for n in range(2)]
        y = sb("y", [P, STILES, D])
        b2 = sb("b2", [P, D])
        H, XB, Y = psum[0:2], psum[2:4], psum[4:8]

        picked = sem("picked")
        xg_in = sem("xg_in")
        x_turned, x_hi, x_ready = sem("x_turned"), sem("xg_hi"), sem("x_ready")
        gate_ready = sem("gate_set")
        h_filled, h_hi_done = sem("h_filled"), sem("h_hi_done")
        h_full = sem("h_full")
        h_ready = sem("h_ready")
        y_step = sem("y_step")
        y_free = sem("y_free")
        y_out = sem("y_out")
        y_landed = sem("y_landed")
        y_clear = sem("y_clear")
        w_hi_done = sem("w_hi_next")
        w_ready = sem("w_ready")
        b2_in = sem("b2_in")
        passed = sem("passed")
        block = ctx.enter_context(nc.Block())

        out_rows = out.rearrange("b s d -> (b s) d")

        def experts(eng, expert):
            with eng.Fori(0, LAST_E) as e:
                expert(e, False)
            expert(LAST_E, True)

        @block.sync
        def _(sp):
            sp.dma_start(b2[:], a["L0_ffn_b2"][0].partition_broadcast(P)).then_inc(b2_in, 16)

            def expert(e, last):
                if last:
                    return
                for m in range(HB):
                    if m >= 2:
                        sp.wait_ge(w_ready, HB * (e + 1) + m - 1)
                        sp.sem_inc(passed)
                    load_block(sp, a, raw1, raw2, w_in, e + 1, m)
                sp.wait_ge(y_out, STILES * PASSES * (e + 1))
                sp.sem_inc(passed)
                sp.dma_start(b2[:], a["L0_ffn_b2"][e + 1].partition_broadcast(P)).then_inc(b2_in, 16)
                sp.wait_ge(w_ready, HB * (e + 2))
                sp.sem_inc(passed)

            experts(sp, expert)

        @block.gpsimd
        def _(pool):
            pool.sem_inc(y_clear)

            def gather(e, u, half_):
                tiles = slice(half_ * STILES, (half_ + 1) * STILES)
                pool.tensor_copy(picks[half_][:, None, :], index[:, bass.ds(e, 1), tiles]).then_inc(picked, 1)
                pool.wait_ge(picked, u + 1)
                pool.wait_ge(x_turned, KB * u)
                pool.wait_ge(gate_ready, u)
                pool.sem_inc(passed)
                for t in range(STILES):
                    pool.indirect_dma_start(
                        out=xg[:, t, :], out_offset=None, in_=rows_dram[:, :],
                        in_offset=bass.IndirectOffsetOnAxis(ap=picks[half_][:, t:t + 1], axis=0)).then_inc(xg_in, 16)

            pool.tensor_copy(picks[0][:, None, :], index[:, 0:1, 0:STILES]).then_inc(picked, 1)
            pool.wait_ge(picked, 1)
            for t in range(STILES):
                pool.indirect_dma_start(
                    out=xg[:, t, :], out_offset=None, in_=rows_dram[:, :],
                    in_offset=bass.IndirectOffsetOnAxis(ap=picks[0][:, t:t + 1], axis=0)).then_inc(xg_in, 16)

            def expert(e, last):
                for half_ in range(PASSES):
                    u = PASSES * e + half_
                    if not last or half_ + 1 < PASSES:
                        gather(e + (half_ + 1) // PASSES, u + 1, (half_ + 1) % PASSES)
                    for t in range(STILES):
                        pool.wait_ge(y_out, STILES * u + t + 1)
                        pool.sem_inc(passed)
                        pool.indirect_dma_start(
                            out=out_rows, out_offset=bass.IndirectOffsetOnAxis(ap=picks[half_][:, t:t + 1], axis=0),
                            in_=y[:, t, :], in_offset=None, compute_op=ALU.add).then_inc(y_landed, 16)
                    pool.wait_ge(y_landed, 16 * STILES * (u + 1))
                    pool.sem_inc(y_clear)

            experts(pool, expert)

        @block.scalar
        def _(act):
            act.sem_inc(h_full, 2)

            def x_high(f, u2, k):
                act.wait_ge(x_turned, f + 1)
                act.activation(xT[u2][0][:, k, :], XB[k % 2][:, :], ACT.Copy).then_inc(x_hi, 1)

            def w_high(e, m, s):
                act.wait_ge(w_in[m % 2], 32 * (HB // 2) * (e + 1) + 32 * (m // 2 + 1))
                act.wait_ge(y_step, s + 3)
                act.activation(ring["w1_hi"][:, m], raw1[m % 2][:], ACT.Copy)
                act.activation(ring["w2_hi"][:, m], raw2[m % 2][:], ACT.Copy).then_inc(w_hi_done, 1)

            for k in range(KB):
                x_high(k, 0, k)

            def expert(e, last):
                for half_ in range(PASSES):
                    u = PASSES * e + half_
                    for m in range(HB):
                        s = HB * u + m
                        act.wait_ge(h_filled, s + 1)
                        act.wait_ge(h_ready, s + 1)
                        act.sem_inc(passed)
                        act.activation(h[m % 2][:], H[m % 2][:, :], ACT.Gelu,
                                       bias=b1[:, bass.ds(e, 1), m]).then_inc(h_full, 1)
                        act.wait_ge(h_full, s + 3)
                        act.wait_ge(y_step, s + 1)
                        act.activation(h_hi[m % 2][:], h[m % 2][:], ACT.Copy).then_inc(h_hi_done, 1)
                        if half_ == PASSES - 1 and not last and m >= 1:
                            w_high(e, m - 1, s - 1)
                        if TURN_AT <= m < TURN_AT + KB and not (last and half_ == PASSES - 1):
                            k = m - TURN_AT
                            x_high(KB * (u + 1) + k, 1 - half_, k)
                if not last:
                    w_high(e, HB - 1, HB * PASSES * (e + 1) - 1)

            experts(act, expert)

        @block.vector
        def _(dve):
            dve.sem_inc(h_ready, 2)
            dve.sem_inc(y_free, STILES)
            dve.sem_inc(w_ready, HB)

            def gates_of(e, u, u2):
                dve.wait_ge(xg_in, 16 * STILES * (u + 1))
                dve.tensor_scalar(gate[u2][:, :, None], xg[:, :, bass.ds(e + D, 1)], tanh_g[:, 1:2], None,
                                  ALU.mult).then_inc(gate_ready, 1)

            def x_low(f, u2, k):
                dve.wait_ge(x_hi, f + 1)
                dve.tensor_tensor(xT[u2][1][:, k, :], XB[k % 2][:, :], xT[u2][0][:, k, :].bitcast(F32),
                                  ALU.subtract).then_inc(x_ready, 1)

            def w_low(e, m):
                dve.wait_ge(w_hi_done, HB * e + m + 1)
                dve.tensor_tensor(ring["w1_lo"][:, m], raw1[m % 2][:], ring["w1_hi"][:, m].bitcast(F32), ALU.subtract)
                dve.tensor_tensor(ring["w2_lo"][:, m], raw2[m % 2][:], ring["w2_hi"][:, m].bitcast(F32),
                                  ALU.subtract).then_inc(w_ready, 1)

            gates_of(0, 0, 0)
            for k in range(KB):
                x_low(k, 0, k)

            def expert(e, last):
                for half_ in range(PASSES):
                    u = PASSES * e + half_
                    for m in range(HB):
                        s = HB * u + m
                        dve.wait_ge(h_hi_done, s + 1)
                        dve.tensor_tensor(h_lo[m % 2][:], h[m % 2][:], h_hi[m % 2][:].bitcast(F32),
                                          ALU.subtract).then_inc(h_ready, 1)
                        if half_ == PASSES - 1 and not last and m >= 1:
                            w_low(e, m - 1)
                        if not (last and half_ == PASSES - 1):
                            if m == TURN_AT:
                                gates_of(e + (half_ + 1) // PASSES, u + 1, 1 - half_)
                            if TURN_AT <= m < TURN_AT + KB:
                                x_low(KB * (u + 1) + m - TURN_AT, 1 - half_, m - TURN_AT)
                    for t in range(STILES):
                        if t == 0:
                            dve.wait_ge(y_step, HB * (u + 1) + 2)
                            dve.wait_ge(y_clear, u + 1)
                            dve.wait_ge(b2_in, 16 * (e + 1))
                        dve.tensor_tensor(y[:, t, :], Y[t][:, :], b2[:], ALU.add).then_inc(y_free, 1)
                        dve.wait_ge(y_free, STILES * (u + 1) + t + 1)
                        dve.tensor_scalar(y[:, t, :], y[:, t, :], gate[half_][:, t:t + 1], None,
                                          ALU.mult).then_inc(y_out, 1)
                if not last:
                    w_low(e, HB - 1)

            experts(dve, expert)

        @block.tensor
        def _(pe):
            pe.sem_inc(y_step, 2)

            def turn_tokens(f, u, k):
                if k == 0:
                    pe.wait_ge(xg_in, 16 * STILES * (u + 1))
                if not isinstance(f, int) or f >= 2:
                    pe.wait_ge(x_ready, f - 1)
                for t in range(STILES):
                    ins = pe.transpose(XB[k % 2][:, t * P:(t + 1) * P], xg[:, t, k * P:(k + 1) * P], ident[:])
                ins.then_inc(x_turned, 1)

            def first_layer(e, half_, s, m):
                u2 = half_ % 2
                if m == 0:
                    pe.wait_ge(x_ready, KB * (PASSES * e + half_ + 1))
                if half_ == 0:
                    pe.wait_ge(w_ready, HB * e + m + 1)
                pe.wait_ge(h_full, s + 1)
                x_hi_, x_lo_ = xT[u2]
                at = 0
                for k in range(KB):
                    w_hi_, w_lo_ = ring["w1_hi"][:, m, k, :], ring["w1_lo"][:, m, k, :]
                    for w, x in ((w_hi_, x_hi_), (w_hi_, x_lo_), (w_lo_, x_hi_)):
                        ins = pe.matmul(H[m % 2][:, :], w, x[:, k, :], start=(at == 0), stop=(at == 3 * KB - 1))
                        at += 1
                ins.then_inc(h_filled, 1)

            def second_layer(u, s, m):
                pe.wait_ge(h_ready, s + 3)
                w_hi_, w_lo_ = ring["w2_hi"][:, m, :], ring["w2_lo"][:, m, :]
                for t in range(STILES):
                    if m == 0:
                        pe.wait_ge(y_free, STILES * u + t + 1)
                    cols = slice(t * P, (t + 1) * P)
                    hi, lo = h_hi[m % 2][:, cols], h_lo[m % 2][:, cols]
                    for n, (x, w) in enumerate(((hi, w_hi_), (hi, w_lo_), (lo, w_hi_))):
                        ins = pe.matmul(Y[t][:, :], x, w, start=(m == 0 and n == 0), stop=(m == HB - 1 and n == 2))
                ins.then_inc(y_step, 1)

            for k in range(KB):
                turn_tokens(k, 0, k)
            first_layer(0, 0, 0, 0)

            def expert(e, last):
                for half_ in range(PASSES):
                    u = PASSES * e + half_
                    for m in range(HB):
                        s = HB * u + m
                        if m + 1 < HB:
                            first_layer(e, half_, s + 1, m + 1)
                        elif half_ + 1 < PASSES:
                            first_layer(e, half_ + 1, s + 1, 0)
                        elif not last:
                            first_layer(e + 1, 0, s + 1, 0)
                        if TURN_AT <= m < TURN_AT + KB and not (last and half_ == PASSES - 1):
                            turn_tokens(KB * (u + 1) + m - TURN_AT, u + 1, m - TURN_AT)
                        second_layer(u, s, m)

            experts(pe, expert)


_OUT = (BATCH, SEQ, D)


def kernel(**inputs):
    import numpy as np
    from concourse import bacc
    from concourse.bass_utils import run_bass_kernel_spmd

    nc = bacc.Bacc("TRN2", target_bir_lowering=False, num_devices=1)
    arrays = {f"in_{n}": np.ascontiguousarray(v) for n, v in inputs.items()}
    args = {n: nc.dram_tensor(f"in_{n}", arrays[f"in_{n}"].shape, mybir.dt.from_np(arrays[f"in_{n}"].dtype),
                              kind="ExternalInput").ap() for n in inputs}
    out = nc.dram_tensor("out_x", _OUT, F32, kind="ExternalOutput").ap()
    block_program(nc, args, out)
    r = run_bass_kernel_spmd(nc, [arrays], core_ids=[0])
    return r.results[0]["out_x"]
```

```python
from contextlib import ExitStack

import concourse.bass as bass
from concourse import mybir

ALU = mybir.AluOpType
ACT = mybir.ActivationFunctionType
AX = mybir.AxisListType.X
F32 = mybir.dt.float32
F32R = mybir.dt.float32r
BF16 = mybir.dt.bfloat16
I32 = mybir.dt.int32
U32 = mybir.dt.uint32

P = 128
BATCH, SEQ, D = 16, 256, 512
HEADS = 16
DH = D // HEADS
HPB = P // DH
KB = D // P
TPB = SEQ // P
N = BATCH * SEQ
EXPERTS = 8
TOPK = max(4, -(-N * 2 // EXPERTS))
DI = 2048
HB = DI // P
SCALE = float(DH) ** -0.5
EPS = 1e-5
MASKED = -1e30
ROW = D + EXPERTS
SLOTS = 512
PASSES = TOPK // SLOTS
STILES = SLOTS // P
CHUNKS = P // EXPERTS
CHUNK = N // CHUNKS
NS = TOPK // P
STACK = (("hi", "hi", "lo"), ("hi", "lo", "hi"))
VW = DH + 1

FILLS = [("CT0", "P", 0), ("XT0", "P", 0), ("CT1", "P", 1), ("XT1", "P", 1), ("K0", "P", 2), ("AT0", "U", 3),
         ("AT1", "U", 4), ("Q0", "P", 4), ("O0", "U", 6), ("O1", "U", 8), ("V0", "P", 10), ("X2T0", "U", 12),
         ("K1", "P", 12), ("X2T1", "U", 13), ("V1", "P", 14), ("R", "U", 14), ("Q2", "P", 15), ("Q3", "P", 15)]
LONG = ("K0", "K1", "Q0", "V0", "O0", "O1")
SHORT = ("CT0", "CT1", "XT0", "XT1", "AT0", "AT1")
ORDER = [w for w, _, _ in FILLS]
LAST = BATCH
STEADY = (3, BATCH - 1)


def stages(i):
    if not isinstance(i, int):
        return "PAU"
    return "P" * (i + 1 < BATCH) + "A" * (0 <= i < BATCH) + "U" * (i >= 1)


def fills(i):
    return [(w, s, h) for w, s, h in FILLS if s in stages(i)]


def parts_at(i, n):
    if "A" not in stages(i):
        return [(w, part) for w, _, _ in fills(i) for part in ((0, 1) if w in LONG else (None,))]
    parts = []
    for w, _, at in fills(i):
        parts += [(at, w, 0), (at + 1, w, 1)] if w in LONG else [(at, w, None)]
    return [(w, part) for at, w, part in parts if at == n]


def ends_at(i, n):
    return [w for w, part in parts_at(i, n) if part != 0]


def fill(i, what):
    names = [w for w, _, _ in fills(i)]
    at = names.index(what)
    per = len(FILLS) // 2

    def before(step, bank):
        return sum(sum(n % 2 == bank for n in range(len(fills(s)))) for s in range(-1, step))

    if isinstance(i, int):
        return at % 2, before(i, at % 2) + at // 2 + 1
    return at % 2, i * per + (before(1, at % 2) - per + at // 2 + 1)


def of_row(what, b):
    stage = next(s for w, s, _ in FILLS if w == what)
    return fill(b - 1 if stage == "P" else b + 1, what)


def block_program(nc, a, out):
    ctx = ExitStack()
    with ctx:
        def sb(name, shape, dt=F32, where=ctx):
            return where.enter_context(nc.sbuf_tensor(name, shape, dt))

        def sem(name):
            return ctx.enter_context(nc.semaphore(name))

        rows_dram = nc.dram_tensor("token_rows", [N, ROW], F32)
        ident = sb("ident", [P, P])
        scores = sb("scores", [P, TPB, EXPERTS, BATCH])
        tanh_g = sb("tanh_g", [P, 2])
        psum = [ctx.enter_context(nc.psum_tensor(f"bank{i}", [P, 512], F32)) for i in range(8)]
        attention_phase(nc, a, out, rows_dram, ident, scores, tanh_g, psum, sb, sem)

        ring = {n: sb(n, shape, F32R) for n, shape in (
            ("w1_hi", [P, HB, KB, P]), ("w1_lo", [P, HB, KB, P]), ("w2_hi", [P, HB, D]), ("w2_lo", [P, HB, D]))}
        raw1 = [sb(f"w1_raw{p}", [P, KB, P]) for p in range(2)]
        raw2 = [sb(f"w2_raw{p}", [P, D]) for p in range(2)]
        index = sb("index", [P, EXPERTS, TOPK // P], U32)
        b1 = sb("b1", [P, EXPERTS, HB])
        part = sb("part", [P, 2, TPB, P], BF16)
        iota = sb("iota", [P, P], BF16)
        tile_no = sb("tile_no", [P, TPB, BATCH], BF16)
        lane = sb("lane", [P, 1])
        w_in = [sem(f"w_in{p}") for p in range(2)]
        numbers = (part, iota, tile_no, lane)
        selection_phase(nc, a, ident, scores, ring, raw1, raw2, w_in, index, b1, numbers, psum, sem)
        expert_phase(nc, a, out, rows_dram, ident, tanh_g, ring, raw1, raw2, w_in, index, b1, numbers, psum, sb, sem)


def token_numbers(eng, column, token, part, numbers, column_ready, n, ready):
    _, iota, tile_no, lane = numbers
    shape = [P, TPB, BATCH, NS]
    iotas = iota[:, 0:NS].rearrange("p (a b n) -> p a b n", a=1, b=1)
    eng.tensor_tensor(column[:], iotas.to_broadcast(shape), part[:, :, :, None].to_broadcast(shape),
                      ALU.is_equal).then_inc(column_ready, 1)
    eng.wait_ge(column_ready, n)
    eng.sem_inc(ready[1])
    eng.tensor_tensor(token[:, :, :, :, 0], column[:], tile_no[:, :, :, None].to_broadcast(shape), ALU.mult)
    eng.tensor_scalar(token[:, :, :, :, 1], column[:], lane[:, 0:1], None, ALU.mult).then_inc(ready[0], 1)


def attention_phase(nc, a, out, rows_dram, ident, scores, tanh_g, psum, sb_all, sem):
    ctx = ExitStack()
    with ctx:
        def sb(name, shape, dt=F32):
            return sb_all(name, shape, dt, ctx)

        mask = sb("mask", [P, 3 * P])
        half = sb("half", [P, TPB])
        bq = sb("bq", [P, KB])
        bk = sb("bk", [P, KB])
        bv = sb("bv", [P, D])
        bo = sb("bo", [P, D])
        wr = sb("wr", [P, KB, EXPERTS])
        names = ("wq", "wk", "wv", "wo")
        w_hi = {n: sb(n + "_hi", [P, KB, D], F32R) for n in names}
        w_lo = {n: sb(n + "_lo", [P, KB, D], F32R) for n in names}
        S, PT, O, W = psum[0:2], psum[2:4], psum[4:6], psum[6:8]

        xin = [sb(f"xin{p}", [P, TPB, D]) for p in range(2)]
        cin = [sb(f"cin{p}", [P, TPB, D]) for p in range(2)]
        x_in = [sem(f"x_in{p}") for p in range(2)]
        c_in = [sem(f"c_in{p}") for p in range(2)]
        x_v = a["x"].rearrange("b (t p) d -> b p t d", p=P)
        c_v = a["ctx_1024"].rearrange("b (t p) d -> b p t d", p=P)

        def load_first(sp):
            sp.dma_start(xin[0][:], x_v[0]).then_inc(x_in[0], 16)
            sp.dma_start(cin[0][:], c_v[0]).then_inc(c_in[0], 16)

        const_ready = sem("const_ready")
        weights_setup(nc, a, const_ready, ident, mask, half, bq, bk, bv, bo, wr, tanh_g, w_hi, w_lo, names, psum,
                      load_first, sem)

        x1 = [sb(f"x1{p}", [P, TPB, D]) for p in range(2)]
        xn = sb("xn", [P, TPB, D])
        xnT = [sb(f"xnT_{s}", [P, KB, SEQ], F32R) for s in ("hi", "lo")]
        cT = [sb(f"cT_{s}", [P, KB, SEQ], F32R) for s in ("hi", "lo")]
        aT = [sb(f"aT_{s}", [P, KB, SEQ], F32R) for s in ("hi", "lo")]
        QT = {s: sb(f"QT_{s}", [P, KB, SEQ], F32R) for s in ("hi", "lo")}
        KT = {s: sb(f"KT_{s}", [P, KB, SEQ], F32R) for s in ("hi", "lo")}
        QS = sb("Q_stacked", [len(STACK[0]) * DH, HPB, KB, SEQ], F32R)
        KS = sb("K_stacked", [len(STACK[0]) * DH, HPB, KB, SEQ], F32R)
        V = [sb(f"V{p}", [P, TPB, HEADS, VW]) for p in range(2)]
        E = [sb(f"E{p}", [P, 3 * P]) for p in range(2)]
        ET = [sb(f"ET{p}", [P, 3 * P]) for p in range(2)]
        least = [sb(f"least{p}", [P, 2]) for p in range(2)]
        attn = [sb(f"attn{p}", [P, TPB, D]) for p in range(2)]
        rsum = sb("rsum", [P, TPB * HPB])
        rows = [sb(f"rows{p}", [P, TPB, ROW]) for p in range(2)]
        xn2T = sb("xn2T", [P, TPB, KB, P])
        stats1 = sb("stats1", [P, TPB, 6])
        mv1 = sb("mv1", [P, TPB, 2])
        ve1 = sb("ve1", [P, TPB])
        rstd1 = sb("rstd1", [P, TPB])
        stats2 = sb("stats2", [P, TPB, 6])
        mv2 = sb("mv2", [P, TPB, 2])
        ve2 = sb("ve2", [P, TPB])
        rstd2 = sb("rstd2", [P, TPB])
        rmax = sb("rmax", [P, TPB])
        rdiff = sb("rdiff", [P, TPB, EXPERTS])
        rexp = sb("rexp", [P, TPB, EXPERTS])
        rtot = sb("rtot", [P, TPB])
        rinv = sb("rinv", [P, TPB])
        prob = sb("prob", [P, TPB, EXPERTS])

        xres_in = [sem(f"xres_in{p}") for p in range(2)]
        x1_stored = [sem(f"x1_stored{p}") for p in range(2)]
        rows_stored = [sem(f"rows_stored{p}") for p in range(2)]
        ones_set = sem("ones_set")
        waited = sem("waited")
        ln1_stats, ln1_mv, ln1_ve, ln1_rstd, xn_ready = map(sem, ("ln1_stats", "ln1_mv", "ln1_ve", "ln1_rstd", "xn_ready"))
        ln2_stats, ln2_mv, ln2_ve, ln2_rstd, xn2_ready = map(sem, ("ln2_stats", "ln2_mv", "ln2_ve", "ln2_rstd", "xn2_ready"))
        filled = [sem(f"filled{n}") for n in range(2)]
        drained = [sem(f"drained{n}") for n in range(2)]
        x_hi, c_hi, a_hi = map(sem, ("x_hi", "c_hi", "a_hi"))
        qk_hi = sem("qk_hi")
        stacked = [sem(f"stacked{n}") for n in range(2)]
        STACKED = 16 * 2 * len(STACK[0]) * HPB
        xb_ready = sem("xb_ready")
        s_done, least_done, e_done, t_done, et_done, pv_done = map(
            sem, ("s_done", "least_done", "e_done", "t_done", "et_done", "pv_done"))
        sums_inv, norm_done = sem("sums_inv"), sem("norm_done")
        r_max, r_exp, r_tot, r_inv, prob_ready, score_kept = map(
            sem, ("r_max", "r_exp", "r_tot", "r_inv", "prob_ready", "score_kept"))

        out_v = out.rearrange("b (t p) d -> b p t d", p=P)
        rows_v = rows_dram[:, :].rearrange("(b t p) d -> b p t d", p=P, t=TPB)

        def wait(eng, semaphore, value):
            if not isinstance(value, int) or value > 0:
                eng.wait_ge(semaphore, value)

        def wait_banks(eng, semaphores, b, whats, banks=(0, 1)):
            for bank in banks:
                of_bank = [w for w in whats if of_row(w, b)[0] == bank]
                if of_bank:
                    eng.wait_ge(semaphores[bank], of_row(max(of_bank, key=ORDER.index), b)[1])
                    if eng is nc.sync:
                        eng.sem_inc(waited)

        def wait_filled(eng, b, *whats):
            wait_banks(eng, filled, b, whats)

        def wait_drained(eng, b, *whats):
            wait_banks(eng, drained, b, whats)

        def exists(b):
            return not isinstance(b, int) or b >= 0

        def at_start(i):
            return isinstance(i, int) and i == -1

        def steps(eng, step, ahead=0):
            for i in range(-1, STEADY[0]):
                step(i, i % 2, i // 2)
            first = STEADY[0]
            turns = (STEADY[1] - ahead - first) // 2
            with eng.Fori(0, turns) as j:
                for k in range(2):
                    step(2 * j + (first + k), (first + k) % 2, j + (first + k) // 2)
            for i in range(first + 2 * turns, LAST + 1):
                step(i, i % 2, i // 2)

        block = ctx.enter_context(nc.Block())

        @block.sync
        def _(sp):
            def stack(half, to, parts, order):
                fbs = slice(half * KB // 2, (half + 1) * KB // 2)
                for n, part_ in enumerate(order):
                    for j in range(HPB):
                        sp.dma_start(to[n * DH:(n + 1) * DH, j, fbs, :].bitcast(F32),
                                     parts[part_][j * DH:(j + 1) * DH, fbs, :].bitcast(F32)).then_inc(stacked[half], 16)

            def step(i, p, h):
                if "A" in stages(i):
                    wait_drained(sp, i, "K1", "Q2", "Q3")
                    sp.sem_inc(waited)
                    wait(sp, s_done, i * HEADS)
                    sp.sem_inc(waited)
                    stack(1, KS, KT, STACK[1])
                    stack(1, QS, QT, STACK[0])
                if not isinstance(i, int) or i + 2 < BATCH:
                    wait(sp, xn_ready, TPB * (i + 1))
                    sp.sem_inc(waited)
                    sp.dma_start(xin[p][:], x_v[i + 2]).then_inc(x_in[p], 16)
                    if exists(i):
                        wait_filled(sp, i, "CT1")
                        sp.sem_inc(waited)
                    sp.dma_start(cin[p][:], c_v[i + 2]).then_inc(c_in[p], 16)
                if "A" in stages(i):
                    if exists(i - 2):
                        sp.wait_ge(x1_stored[p], 16 * h)
                        sp.sem_inc(waited)
                    sp.dma_start(x1[p][:], x_v[i]).then_inc(xres_in[p], 16)
                if "P" in stages(i):
                    if "A" in stages(i):
                        sp.wait_ge(s_done, i * HEADS + HEADS // 2)
                        sp.sem_inc(waited)
                    wait_drained(sp, i + 1, "K0")
                    sp.sem_inc(waited)
                    stack(0, KS, KT, STACK[1])
                    wait_drained(sp, i + 1, "Q0")
                    sp.sem_inc(waited)
                    stack(0, QS, QT, STACK[0])
                if "U" in stages(i):
                    q = 1 - p
                    wait_drained(sp, i - 1, "O1")
                    sp.sem_inc(waited)
                    sp.dma_start(out_v[i - 1], x1[q][:]).then_inc(x1_stored[q], 16)
                    sp.wait_ge(prob_ready, i)
                    sp.sem_inc(waited)
                    sp.dma_start(rows_v[i - 1], rows[q][:]).then_inc(rows_stored[q], 16)

            steps(sp, step, 1)
            for p in range(2):
                sp.wait_ge(x1_stored[p], 16 * (BATCH // 2))
                sp.wait_ge(rows_stored[p], 16 * (BATCH // 2))

        @block.gpsimd
        def _(pool):
            def inverse_deviation(mv, ve, rstd, ready_mv, n_mv, s_ve, n_ve, s_rstd):
                pool.wait_ge(ready_mv, n_mv)
                pool.sem_inc(waited)
                pool.tensor_scalar(ve, mv[:, :, 1], EPS, None, ALU.add).then_inc(s_ve, 1)
                pool.wait_ge(s_ve, n_ve + 1)
                pool.tensor_tensor(rstd, ve, half[:, 0:ve.shape[1]], ALU.pow).then_inc(s_rstd, 1)
                pool.wait_ge(s_rstd, n_ve + 1)
                pool.sem_inc(waited)

            def norm1(b, p):
                inverse_deviation(mv1, ve1[:], rstd1[:], ln1_mv, TPB * (b + 1), ln1_ve, b, ln1_rstd)
                if exists(b - 1):
                    wait_filled(pool, b - 1, "XT1")
                pool.sem_inc(waited)
                for t in range(TPB):
                    pool.tensor_scalar(xn[:, t, :], xin[p][:, t, :], mv1[:, t, 0:1], rstd1[:, t:t + 1],
                                       ALU.subtract, ALU.mult).then_inc(xn_ready, 1)

            def norm2(b, p, h, t):
                inverse_deviation(mv2[:, t:t + 1, :], ve2[:, t:t + 1], rstd2[:, t:t + 1], ln2_mv,
                                  TPB * b + t + 1, ln2_ve, TPB * b + t, ln2_rstd)
                if t == 0 and exists(b - 2):
                    pool.wait_ge(rows_stored[p], 16 * h)
                pool.sem_inc(waited)
                pool.tensor_scalar(rows[p][:, t, 0:D], x1[p][:, t, :], mv2[:, t, 0:1], rstd2[:, t:t + 1],
                                   ALU.subtract, ALU.mult).then_inc(xn2_ready, 1)

            def step(i, p, h):
                q = 1 - p
                hq = h if p else h - 1
                if at_start(i):
                    norm1(0, 0)
                    norm1(1, 1)
                if "U" in stages(i):
                    pool.wait_ge(xres_in[q], 16 * (hq + 1))
                    pool.tensor_tensor(x1[q][:], x1[q][:], bo[:, None, :].to_broadcast([P, TPB, D]),
                                       ALU.add).then_inc(xb_ready, 1)
                if "U" in stages(i):
                    for t in range(TPB):
                        norm2(i - 1, q, hq, t)
                if not isinstance(i, int) or 0 <= i < BATCH - 2:
                    norm1(i + 2, p)
                if "U" in stages(i):
                    pool.wait_ge(prob_ready, i)
                    pool.tensor_copy(scores[:, :, :, bass.ds(i - 1, 1)], prob[:, :, :, None]).then_inc(score_kept, 1)

            steps(pool, step, 1)

        @block.scalar
        def _(act):
            def exp_head(n, e):
                act.wait_ge(least_done, n + 1)
                act.activation(E[e][:, 0:P], E[e][:, 0:P], ACT.Exp, bias=least[e][:, 0:1], scale=-1.0)
                act.activation(E[e][:, P:3 * P], E[e][:, P:3 * P], ACT.Exp, bias=least[e][:, 1:2],
                               scale=-1.0).then_inc(e_done, 1)

            def evacuate(what, i, p):
                bank, n = fill(i, what)
                w = W[bank]
                b, q = i + 1, 1 - p
                two = w[:, :].rearrange("p (k s) -> p k s", k=2)
                if what in ("XT0", "XT1", "CT0", "CT1", "AT0", "AT1"):
                    k = 2 * int(what[-1])
                    to, s_hi = {"X": (xnT, x_hi), "C": (cT, c_hi), "A": (aT, a_hi)}[what[0]]
                    if what == "XT0" and exists(b - 1):
                        wait_filled(act, b - 1, "Q3")
                    if what == "CT0" and exists(b - 1):
                        wait_filled(act, b - 1, "K1", "V1")
                    if what == "AT0" and exists(i - 2):
                        wait_filled(act, i - 2, "O1")
                    act.wait_ge(filled[bank], n)
                    act.activation(to[0][:, k:k + 2, :], two, ACT.Copy).then_inc(s_hi, 1)
                if what in ("Q0", "Q2", "Q3", "K0", "K1"):
                    k = {"Q0": 0, "Q2": 2, "Q3": 3, "K0": 0, "K1": 2}[what]
                    last = k + (1 if what in ("Q0", "K0", "K1") else 0)
                    to, bias = (QT, bq) if what[0] == "Q" else (KT, bk)
                    wait(act, stacked[k // 2], STACKED * b)
                    act.wait_ge(filled[bank], n)
                    for f in range(k, last + 1):
                        ins = act.activation(to["hi"][:, f, :], two[:, f - k, :], ACT.Identity, bias=bias[:, f:f + 1])
                    ins.then_inc(qk_hi, 1)
                if what in ("X2T0", "X2T1"):
                    t = int(what[-1])
                    if t == 0 and exists(i - 2):
                        wait_filled(act, i - 2, "R")
                    act.wait_ge(filled[bank], n)
                    act.activation(xn2T[:, t, :, :], w[:, :].rearrange("p (k s) -> p k s", k=KB),
                                   ACT.Copy).then_inc(drained[bank], 1)
                if what == "R":
                    bank, n = fill(i, "R")
                    act.wait_ge(drained[bank], n)
                    act.activation(rexp[:], rdiff[:], ACT.Exp).then_inc(r_exp, 1)

            def step(i, p, h):
                for n in range(HEADS if "A" in stages(i) else 1):
                    if "A" in stages(i):
                        g = i * HEADS + n
                        act.wait_ge(t_done, g + 1)
                        wait(act, pv_done, g - 1)
                        act.activation(ET[n % 2][:], PT[n % 2][:, 0:3 * P], ACT.Copy).then_inc(et_done, 1)
                        if n + 1 < HEADS or "P" in stages(i):
                            exp_head(g + 1, (n + 1) % 2)
                    for what in ends_at(i, n):
                        evacuate(what, i, p)
                if at_start(i):
                    exp_head(0, 0)

            steps(act, step)

        @block.vector
        def _(dve):
            def masked_scores(n, e):
                dve.wait_ge(s_done, n + 1)
                wait(dve, t_done, n - 1)
                dve.sem_inc(waited)
                for t, (lo, hi) in enumerate(((0, P), (P, 3 * P))):
                    ins = dve.tensor_tensor_reduce(out=E[e][:, lo:hi], in0=S[e][:, lo:hi], in1=mask[:, lo:hi],
                                                   scale=-SCALE, scalar=-MASKED, op0=ALU.add, op1=ALU.min,
                                                   accum_out=least[e][:, t:t + 1])
                ins.then_inc(least_done, 1)

            def normalise_group(g, p, fb):
                o = O[fb % 2][:, 0:TPB * HPB * VW].rearrange("p (t h v) -> p t h v", t=TPB, v=VW)
                flat = O[fb % 2][:, 0:TPB * HPB * VW].rearrange("p (g v) -> p g v", v=VW)
                dve.wait_ge(pv_done, HPB * (g + 1))
                dve.reciprocal(rsum[:, :], flat[:, :, DH]).then_inc(sums_inv, 1)
                dve.wait_ge(sums_inv, g + 1)
                inv = rsum[:, :].rearrange("p (t h) -> p t h", t=TPB)[:, :, :, None].to_broadcast([P, TPB, HPB, DH])
                dve.tensor_tensor(attn[p][:, :, fb * P:(fb + 1) * P].rearrange("p t (h v) -> p t h v", v=DH),
                                  o[:, :, :, 0:DH], inv, ALU.mult).then_inc(norm_done, 1)

            def ln1(b, p, h):
                dve.wait_ge(x_in[p], 16 * (h + 1))
                wait(dve, ln1_mv, TPB * b)
                for t in range(TPB):
                    dve.bn_stats(stats1[:, t, :], xin[p][:, t, :]).then_inc(ln1_stats, 1)
                dve.wait_ge(ln1_stats, TPB * (b + 1))
                wait(dve, xn_ready, TPB * b)
                dve.sem_inc(waited)
                for t in range(TPB):
                    dve.bn_aggr(mv1[:, t, :], stats1[:, t, :]).then_inc(ln1_mv, 1)

            def evacuate(what, i, p):
                bank, n = fill(i, what.rstrip("+"))
                w = W[bank]
                b, q = i + 1, 1 - p
                two = w[:, :].rearrange("p (k s) -> p k s", k=2)
                if what in ("XT0", "XT1", "CT0", "CT1", "AT0", "AT1"):
                    f = int(what[-1])
                    k = 2 * f
                    to, s_hi = {"X": (xnT, x_hi), "C": (cT, c_hi), "A": (aT, a_hi)}[what[0]]
                    row = i - 1 if what[0] == "A" else b
                    dve.wait_ge(s_hi, 2 * row + f + 1)
                    dve.tensor_tensor(to[1][:, k:k + 2, :], two, to[0][:, k:k + 2, :].bitcast(F32),
                                      ALU.subtract).then_inc(drained[bank], 1)
                if what in ("Q0", "Q2", "Q3", "K0", "K1"):
                    k = {"Q0": 0, "Q2": 2, "Q3": 3, "K0": 0, "K1": 2}[what]
                    last = k + (1 if what in ("Q0", "K0", "K1") else 0)
                    to, bias = (QT, bq) if what[0] == "Q" else (KT, bk)
                    before = [w_ for w_ in ORDER if w_[0] in "QK"].index(what)
                    dve.wait_ge(qk_hi, 5 * b + before + 1)
                    dve.sem_inc(waited)
                    for f in range(k, last + 1):
                        ins = dve.scalar_tensor_tensor(out=to["lo"][:, f, :], in0=two[:, f - k, :],
                                                       scalar=bias[:, f:f + 1], in1=to["hi"][:, f, :].bitcast(F32),
                                                       op0=ALU.add, op1=ALU.subtract)
                    ins.then_inc(drained[bank], 1)
                if what in ("V0", "V1"):
                    t = int(what[-1])
                    if t == 0 and exists(b - 2):
                        dve.wait_ge(pv_done, HEADS * (b - 1))
                    dve.wait_ge(filled[bank], n)
                    dve.tensor_tensor(V[q][:, t, :, 0:DH], w[:, :].rearrange("p (h v) -> p h v", v=DH),
                                      bv[:, :].rearrange("p (h v) -> p h v", v=DH), ALU.add).then_inc(drained[bank], 1)
                if what in ("O0", "O1"):
                    t = int(what[-1])
                    dve.wait_ge(filled[bank], n)
                    dve.wait_ge(xb_ready, i)
                    dve.scalar_tensor_tensor(out=x1[q][:, t, :], in0=w[:, :], scalar=tanh_g[:, 0:1],
                                             in1=x1[q][:, t, :], op0=ALU.mult, op1=ALU.add).then_inc(drained[bank], 1)
                if what in ("O0+", "O1+"):
                    t = int(what[1])
                    dve.wait_ge(drained[bank], n)
                    wait(dve, ln2_mv, TPB * (i - 2) + t + 1)
                    dve.bn_stats(stats2[:, t, :], x1[q][:, t, :]).then_inc(ln2_stats, 1)
                    dve.wait_ge(ln2_stats, TPB * (i - 1) + t + 1)
                    wait(dve, xn2_ready, TPB * (i - 2) + t + 1)
                    dve.sem_inc(waited)
                    dve.bn_aggr(mv2[:, t, :], stats2[:, t, :]).then_inc(ln2_mv, 1)
                if what == "R":
                    logits = w[:, 0:TPB * EXPERTS].rearrange("p (t e) -> p t e", t=TPB)
                    dve.wait_ge(filled[bank], n)
                    dve.tensor_reduce(rmax[:], logits, AX, ALU.max).then_inc(r_max, 1)
                    dve.wait_ge(r_max, i)
                    wait(dve, r_exp, i - 1)
                    dve.tensor_tensor(rdiff[:], logits, rmax[:, :, None].to_broadcast([P, TPB, EXPERTS]),
                                      ALU.subtract).then_inc(drained[bank], 1)

            def router_end(i, p):
                q = 1 - p
                dve.wait_ge(r_exp, i)
                dve.tensor_reduce(rtot[:], rexp[:], AX, ALU.add).then_inc(r_tot, 1)
                dve.wait_ge(r_tot, i)
                dve.reciprocal(rinv[:], rtot[:]).then_inc(r_inv, 1)
                dve.wait_ge(r_inv, i)
                inv = rinv[:, :, None].to_broadcast([P, TPB, EXPERTS])
                wait(dve, score_kept, i - 1)
                dve.tensor_tensor(prob[:], rexp[:], inv, ALU.mult)
                dve.tensor_tensor(rows[q][:, :, D:ROW], rexp[:], inv, ALU.mult).then_inc(prob_ready, 1)

            def step(i, p, h):
                if at_start(i):
                    for p2 in range(2):
                        dve.memset(V[p2][:, :, :, DH:VW], 1.0).then_inc(ones_set, 1)
                if at_start(i):
                    ln1(0, 0, 0)
                for n in range(HEADS if "A" in stages(i) else 1):
                    if "A" in stages(i):
                        g = i * HEADS + n
                        if n + 1 < HEADS or "P" in stages(i):
                            masked_scores(g + 1, (n + 1) % 2)
                        if n % HPB == 1 and n > 1:
                            normalise_group(i * KB + n // HPB - 1, p, n // HPB - 1)
                    if "U" in stages(i) and n == (1 if "A" in stages(i) else 0):
                        normalise_group(i * KB - 1, 1 - p, KB - 1)
                    if "A" in stages(i):
                        for what in ends_at(i, n - 1)[-1:]:
                            if what not in SHORT:
                                evacuate(what, i, p)
                        for what in ends_at(i, n - 2):
                            if what in ("O0", "O1"):
                                evacuate(what + "+", i, p)
                        for what in ends_at(i, n):
                            if what in SHORT or what != ends_at(i, n)[-1]:
                                evacuate(what, i, p)
                    if n == 7 and not (isinstance(i, int) and i + 2 >= BATCH):
                        ln1(i + 2, p, h + 1)
                    if n == HEADS - 1 or "A" not in stages(i):
                        for what in ends_at(i, n):
                            if what == "Q3" and "A" in stages(i) and "U" in stages(i):
                                router_end(i, p)
                            if what == ends_at(i, n)[-1] or "A" not in stages(i):
                                evacuate(what, i, p)
                            if what in ("O0", "O1"):
                                evacuate(what + "+", i, p)
                        if "U" in stages(i) and not ("A" in stages(i) and "P" in stages(i)):
                            router_end(i, p)
                if at_start(i):
                    ln1(1, 1, 0)
                    masked_scores(0, 0)

            steps(dve, step, 1)

        @block.tensor
        def _(pe):
            def scores_of(i, p, n):
                fb, j = divmod(n, HPB)
                g = i * HEADS + n
                if n % (HEADS // 2) == 0:
                    pe.wait_ge(stacked[n // (HEADS // 2)], STACKED * (i + 1))
                wait(pe, least_done, g - 1)
                s = S[n % 2]
                pe.matmul(s[:, 0:P], QS[:, j, fb, 0:P], KS[:, j, fb, 0:P], start=True, stop=True)
                pe.matmul(s[:, P:3 * P], QS[:, j, fb, P:2 * P], KS[:, j, fb, :], start=True,
                          stop=True).then_inc(s_done, 1)

            def turn(i, n):
                g = i * HEADS + n
                pe.wait_ge(e_done, g + 1)
                wait(pe, et_done, g - 1)
                for k in range(3):
                    ins = pe.transpose(PT[n % 2][:, k * P:(k + 1) * P], E[n % 2][:, k * P:(k + 1) * P], ident[:])
                ins.then_inc(t_done, 1)

            def values_of(i, p, n):
                fb, j = divmod(n, HPB)
                g = i * HEADS + n
                if n == 0:
                    wait_drained(pe, i, "V0", "V1")
                    if isinstance(i, int) and i == 0:
                        pe.wait_ge(ones_set, 2)
                pe.wait_ge(et_done, g + 1)
                if j == 0:
                    wait(pe, norm_done, i * KB + fb - 1)
                o = O[fb % 2]
                at0, at1 = j * VW, (HPB + j) * VW
                et, v = ET[n % 2], V[p]
                pe.matmul(o[:, at0:at0 + VW], et[:, 0:P], v[:, 0, n, :], start=True, stop=True)
                pe.matmul(o[:, at1:at1 + VW], et[:, P:2 * P], v[:, 0, n, :], start=True, stop=False)
                pe.matmul(o[:, at1:at1 + VW], et[:, 2 * P:3 * P], v[:, 1, n, :], start=False,
                          stop=True).then_inc(pv_done, 1)

            def products(to, pairs, part):
                n = 3 * len(pairs)
                terms = [(x, y) for (lh, ll), (rh, rl) in pairs for x, y in ((lh, rh), (lh, rl), (ll, rh))]
                which = range(n) if part is None else range(part * n // 2, (part + 1) * n // 2)
                for at in which:
                    ins = pe.matmul(to, *terms[at], start=(at == 0), stop=(at == n - 1))
                return ins

            def filling(what, part, i, p):
                bank, n = fill(i, what)
                w = W[bank]
                b, q = i + 1, 1 - p
                if not part:
                    wait(pe, drained[bank], n - 1)
                if what in ("XT0", "XT1", "CT0", "CT1", "AT0", "AT1"):
                    k0 = 2 * int(what[-1])
                    if what[0] == "X":
                        src = xn
                        pe.wait_ge(xn_ready, TPB * (b + 1))
                    elif what[0] == "C":
                        src = cin[q]
                        pe.wait_ge(c_in[q], 16 * (hrow(b, q)))
                    else:
                        src = attn[q]
                        pe.wait_ge(norm_done, KB * i)
                    for k in range(2):
                        for t in range(TPB):
                            ins = pe.transpose(w[:, (k * TPB + t) * P:(k * TPB + t + 1) * P],
                                               src[:, t, (k0 + k) * P:(k0 + k + 1) * P], ident[:])
                if what in ("Q0", "Q2", "Q3", "K0", "K1"):
                    if what == "Q0" and not part:
                        wait_banks(pe, drained, b, ("XT0", "XT1"), (1 - bank,))
                    if what == "K0" and not part:
                        wait_banks(pe, drained, b, ("CT0", "CT1"), (1 - bank,))
                    k = {"Q0": 0, "Q2": 2, "Q3": 3, "K0": 0, "K1": 2}[what]
                    last = k + (1 if what in ("Q0", "K0", "K1") else 0)
                    name, src = ("wq", xnT) if what[0] == "Q" else ("wk", cT)
                    for f in range(k, last + 1) if part is None else (k + part,):
                        cols = slice(f * P, (f + 1) * P)
                        ins = products(w[:, (f - k) * SEQ:(f - k + 1) * SEQ],
                                       [((w_hi[name][:, c, cols], w_lo[name][:, c, cols]),
                                         (src[0][:, c, :], src[1][:, c, :])) for c in range(KB)], None)
                if what in ("V0", "V1", "O0", "O1"):
                    if what == "O0" and not part:
                        wait_banks(pe, drained, i - 1, ("AT0", "AT1"), (1 - bank,))
                    if what == "V0" and not part:
                        wait_banks(pe, drained, b, ("CT0", "CT1"), (1 - bank,))
                    t = int(what[-1])
                    cols = slice(t * P, (t + 1) * P)
                    name, src = ("wv", cT) if what[0] == "V" else ("wo", aT)
                    ins = products(w[:, :], [((src[0][:, c, cols], src[1][:, c, cols]),
                                              (w_hi[name][:, c, :], w_lo[name][:, c, :])) for c in range(KB)], part)
                if what in ("X2T0", "X2T1"):
                    t = int(what[-1])
                    pe.wait_ge(xn2_ready, TPB * (i - 1) + t + 1)
                    for k in range(KB):
                        ins = pe.transpose(w[:, k * P:(k + 1) * P], rows[q][:, t, k * P:(k + 1) * P], ident[:])
                if what == "R":
                    wait_banks(pe, drained, i - 1, ("X2T0", "X2T1"), (1 - bank,))
                    for t in range(TPB):
                        for k in range(KB):
                            ins = pe.matmul(w[:, t * EXPERTS:(t + 1) * EXPERTS], xn2T[:, t, k, :], wr[:, k, :],
                                            start=(k == 0), stop=(k == KB - 1))
                if part != 0:
                    ins.then_inc(filled[bank], 1)

            halves_of = {}

            def hrow(b, q):
                return halves_of["h"] + 1

            def step(i, p, h):
                halves_of["h"] = h if not p else h + 1
                for n in range(HEADS if "A" in stages(i) else 1):
                    if "A" in stages(i):
                        if n + 1 < HEADS:
                            scores_of(i, p, n + 1)
                        turn(i, n)
                    if n > 0:
                        values_of(i, p, n - 1)
                    elif "U" in stages(i):
                        values_of(i - 1, 1 - p, HEADS - 1)
                    if n == HEADS - 1 and "P" in stages(i):
                        scores_of(i + 1, 1 - p, 0)
                    for what, part in parts_at(i, n):
                        filling(what, part, i, p)
                if at_start(i):
                    scores_of(0, 0, 0)

            steps(pe, step)


def weights_setup(nc, a, const_ready, ident, mask, half, bq, bk, bv, bo, wr, tanh_g, w_hi, w_lo, names, W, load_first,
                  sem):
    ctx = ExitStack()
    with ctx:
        raw = {n: ctx.enter_context(nc.sbuf_tensor(n + "_raw", [P, KB, D], F32)) for n in names}
        gates = ctx.enter_context(nc.sbuf_tensor("gates", [P, 2], F32))
        bo_raw = ctx.enter_context(nc.sbuf_tensor("bo_raw", [P, D], F32))
        w_in = {n: sem(n + "_in") for n in names}
        small_in, cleared, ident_ready = map(sem, ("small_in", "cleared", "ident_ready"))
        gate_ready, bo_ready = sem("gate_ready"), sem("bo_ready")
        w_turned, w_hi_done, w_lo_done = map(sem, ("w_turned", "w_hi_done", "w_lo_done"))
        block = ctx.enter_context(nc.Block())
        small = 7

        @block.sync
        def _(sp):
            for n in names:
                src = a[f"L0_xattn_{n}_w"].rearrange("(f p) d -> p f d", p=P)
                for f in range(KB):
                    sp.dma_start(raw[n][:, f], src[:, f]).then_inc(w_in[n], 16)
            load_first(sp)

        @block.gpsimd
        def _(pool):
            pool.memset(ident[:], 0.0).then_inc(cleared, 1)
            pool.memset(mask[:], 0.0).then_inc(cleared, 1)
            pool.memset(half[:], -0.5).then_inc(const_ready, 1)
            pool.wait_ge(cleared, 2)
            pool.affine_select(out=ident[:], in_=ident[:], compare_op=ALU.not_equal, fill=1.0, base=0,
                               pattern=[[-1, P]], channel_multiplier=1).then_inc(ident_ready, 1)
            for c in (0, 2):
                pool.affine_select(out=mask[:, c * P:(c + 1) * P], in_=mask[:, c * P:(c + 1) * P],
                                   compare_op=ALU.is_ge, fill=MASKED, base=0, pattern=[[-1, P]],
                                   channel_multiplier=1).then_inc(const_ready, 1)
            with nc.allow_non_contiguous_dma(reason="512 words of each bias"):
                pool.dma_start(bq[:], a["L0_xattn_wq_b"].rearrange("(f p) -> p f", p=P)).then_inc(small_in, 16)
                pool.dma_start(bk[:], a["L0_xattn_wk_b"].rearrange("(f p) -> p f", p=P)).then_inc(small_in, 16)
                pool.dma_start(wr[:], a["L0_ffn_Wr"].rearrange("(k p) e -> p k e", p=P)).then_inc(small_in, 16)
            pool.dma_start(bv[:], a["L0_xattn_wv_b"].partition_broadcast(P)).then_inc(small_in, 16)
            pool.dma_start(bo_raw[:], a["L0_xattn_wo_b"].partition_broadcast(P)).then_inc(small_in, 16)
            pool.dma_start(gates[:, 0:1], a["g_xattn"].partition_broadcast(P)).then_inc(small_in, 16)
            pool.dma_start(gates[:, 1:2], a["g_ffn"].partition_broadcast(P)).then_inc(small_in, 16)
            pool.wait_ge(small_in, 16 * small)
            pool.wait_ge(gate_ready, 1)
            pool.tensor_scalar(bo[:], bo_raw[:], tanh_g[:, 0:1], None, ALU.mult).then_inc(bo_ready, 1)

        @block.scalar
        def _(act):
            for n, name in enumerate(names):
                if n == len(names) - 1:
                    act.wait_ge(small_in, 16 * small)
                    act.activation(tanh_g[:], gates[:], ACT.Tanh).then_inc(gate_ready, 1)
                for k in range(KB):
                    f = n * KB + k
                    act.wait_ge(w_turned, f + 1)
                    act.activation(w_hi[name][:, k, :], W[f % len(W)][:, :], ACT.Copy).then_inc(w_hi_done, 1)

        @block.vector
        def _(dve):
            for n, name in enumerate(names):
                for k in range(KB):
                    f = n * KB + k
                    dve.wait_ge(w_hi_done, f + 1)
                    dve.tensor_tensor(w_lo[name][:, k, :], W[f % len(W)][:, :], w_hi[name][:, k, :].bitcast(F32),
                                      ALU.subtract).then_inc(w_lo_done, 1)

        @block.tensor
        def _(pe):
            pe.wait_ge(ident_ready, 1)
            for n, name in enumerate(names):
                pe.wait_ge(w_in[name], 16 * KB)
                for k in range(KB):
                    f = n * KB + k
                    if f >= len(W):
                        pe.wait_ge(w_lo_done, f - len(W) + 1)
                    for c in range(KB):
                        ins = pe.transpose(W[f % len(W)][:, c * P:(c + 1) * P], raw[name][:, c, k * P:(k + 1) * P], ident[:])
                    ins.then_inc(w_turned, 1)


def load_block(sp, a, raw1, raw2, w_in, e, m):
    w1 = a["L0_ffn_W1"].rearrange("e (k p) (m h) -> e m p k h", p=P, h=P)
    w2 = a["L0_ffn_W2"].rearrange("e (m p) d -> e m p d", p=P)
    sp.dma_start(raw1[m % 2][:], w1[e, m]).then_inc(w_in[m % 2], 16)
    sp.dma_start(raw2[m % 2][:], w2[e, m]).then_inc(w_in[m % 2], 16)


def selection_phase(nc, a, ident, scores, ring, raw1, raw2, w_in, index, b1, numbers, psum, sem):
    ctx = ExitStack()
    TOP_BIT = 29
    part, iota, tile_no, lane = numbers
    with ctx:
        def sb(name, shape, dt=F32):
            return ctx.enter_context(nc.sbuf_tensor(name, shape, dt))

        sc = sb("sc", [P, CHUNK])
        same = sb("same_expert", [P, P], BF16)
        before = sb("chunks_before", [P, P], BF16)
        seen = sb("seen", [P, CHUNK])
        cand = sb("cand", [P, 1], I32)
        bit = [sb(f"bit{p}", [P, 1]) for p in range(2)]
        next_bit = sb("next_bit", [P, 1], I32)
        undo = sb("undo", [P, 1], I32)
        count = sb("count", [P, 1], BF16)
        larger = sb("larger", [P, CHUNK])
        equal = sb("equal", [P, CHUNK])
        zeros = sb("zeros", [P, CHUNK])
        rank = sb("rank", [P, CHUNK])
        taken = sb("taken", [P, CHUNK])
        chosen = sb("chosen", [P, CHUNK])
        place = sb("place", [P, CHUNK])
        need = sb("need", [P, 1])
        offset = sb("offset", [P, 1])
        place_i = sb("place_i", [P, TPB, P], I32)
        part_i = sb("part_i", [P, 2, TPB * P], I32)
        iota_i = sb("iota_i", [P, P], I32)
        tile_i = sb("tile_i", [P, TPB, BATCH], I32)
        lane_i = sb("lane_i", [P, 1], I32)
        slot = sb("slot_first", [P, TPB, BATCH, P], BF16)
        column = sb("column_first", [P, TPB, BATCH, NS], BF16)
        token = sb("token_first", [P, TPB, BATCH, NS, 2], BF16)
        found = sb("found_first", [P, NS, 2])

        consts, sc_turned, sc_ready = sem("sel_consts"), sem("sc_turned"), sem("sc_ready")
        made, counted, summed = sem("made"), sem("counted"), sem("summed")
        cand_ready, bit_ready, undo_ready = sem("cand_ready"), sem("bit_ready"), sem("undo_ready")
        made_up = sem("made_up")
        step_done, turned, sums = sem("step_done"), sem("place_turned"), sem("chunk_sums")
        part_ready, hot_ready, hot_used = sem("part_ready"), sem("hot_ready"), sem("hot_used")
        column_ready = sem("column_ready")
        passed = sem("passed_first")
        w_hi_done, w_lo_done, b1_in = sem("w_hi_first"), sem("w_lo_first"), sem("b1_in")
        block = ctx.enter_context(nc.Block())

        @block.sync
        def _(sp):
            with nc.allow_non_contiguous_dma(reason="the experts' first biases, one word to a partition"):
                sp.dma_start(b1[:], a["L0_ffn_b1"].rearrange("e (m p) -> p e m", p=P)).then_inc(b1_in, 16)
            for m in range(HB):
                if m >= 2:
                    sp.wait_ge(w_lo_done, m - 1)
                load_block(sp, a, raw1, raw2, w_in, 0, m)
            sp.wait_ge(b1_in, 16)

        @block.scalar
        def _(act):
            for m in range(HB):
                act.wait_ge(w_in[m % 2], 32 * (m // 2 + 1))
                act.activation(ring["w1_hi"][:, m], raw1[m % 2][:], ACT.Copy)
                act.activation(ring["w2_hi"][:, m], raw2[m % 2][:], ACT.Copy).then_inc(w_hi_done, 1)

        @block.gpsimd
        def _(pool):
            pool.memset(same[:], 1.0).then_inc(made, 1)
            pool.wait_ge(made, 1)
            by_expert = same[:].rearrange("p (e c) -> p e c", c=CHUNKS)
            pool.affine_select(out=by_expert, in_=by_expert, compare_op=ALU.is_ge, fill=0.0, base=0,
                               pattern=[[-CHUNKS, EXPERTS], [0, CHUNKS]], channel_multiplier=1).then_inc(made, 1)
            pool.wait_ge(made, 2)
            pool.affine_select(out=by_expert, in_=by_expert, compare_op=ALU.is_ge, fill=0.0, base=CHUNKS - 1,
                               pattern=[[CHUNKS, EXPERTS], [0, CHUNKS]], channel_multiplier=-1).then_inc(made, 1)
            pool.wait_ge(made, 3)
            pool.affine_select(out=before[:], in_=same[:], compare_op=ALU.is_gt, fill=0.0, base=0,
                               pattern=[[1, P]], channel_multiplier=-1).then_inc(made, 1)
            pool.iota(iota_i[:], pattern=[[1, P]], base=0, channel_multiplier=0).then_inc(made, 1)
            pool.iota(tile_i[:], pattern=[[1, TPB], [TPB, BATCH]], base=0, channel_multiplier=0).then_inc(made, 1)
            pool.iota(lane_i[:], pattern=[[0, 1]], base=0, channel_multiplier=1).then_inc(made, 1)
            pool.wait_ge(made, 7)
            pool.tensor_copy(iota[:], iota_i[:]).then_inc(consts, 1)
            pool.tensor_copy(tile_no[:], tile_i[:]).then_inc(consts, 1)
            pool.tensor_copy(lane[:], lane_i[:]).then_inc(consts, 1)
            for m in range(HB):
                pool.wait_ge(w_hi_done, m + 1)
                pool.tensor_tensor(ring["w1_lo"][:, m], raw1[m % 2][:], ring["w1_hi"][:, m].bitcast(F32), ALU.subtract)
                pool.tensor_tensor(ring["w2_lo"][:, m], raw2[m % 2][:], ring["w2_hi"][:, m].bitcast(F32),
                                   ALU.subtract).then_inc(w_lo_done, 1)

        @block.vector
        def _(dve):
            dve.memset(zeros[:], 0.0).then_inc(step_done, 1)
            dve.memset(cand[:], 1 << TOP_BIT).then_inc(step_done, 1)
            dve.memset(bit[0][:], float(1 << TOP_BIT)).then_inc(step_done, 1)
            dve.wait_ge(sc_turned, 1)
            dve.tensor_copy(sc[:], psum[0][:, 0:CHUNK]).then_inc(sc_ready, 1)
            dve.wait_ge(sc_ready, 1)
            dve.wait_ge(step_done, 3)

            with dve.Fori(1, TOP_BIT + 2, 2) as it:
                for k in range(2):
                    n = it + k
                    dve.tensor_scalar(seen[:], sc[:], cand[:].bitcast(F32), 0.0, ALU.is_ge, ALU.add,
                                      accum_out=count[:]).then_inc(counted, 1)
                    dve.tensor_scalar(bit[1 - k][:], bit[k][:], 0.5, None, ALU.mult)
                    dve.tensor_scalar(next_bit[:], bit[k][:], 0.5, None, ALU.mult).then_inc(bit_ready, 1)
                    dve.wait_ge(summed, n)
                    dve.tensor_scalar(undo[:], psum[1][:, 0:1], float(TOPK), bit[k][:, 0:1], ALU.is_lt,
                                      ALU.mult).then_inc(undo_ready, 1)
                    dve.wait_ge(undo_ready, n)
                    dve.wait_ge(bit_ready, n)
                    dve.tensor_tensor(undo[:], undo[:], next_bit[:], ALU.bitwise_or).then_inc(made_up, 1)
                    dve.wait_ge(made_up, n)
                    dve.tensor_tensor(cand[:], cand[:], undo[:], ALU.bitwise_xor).then_inc(cand_ready, 1)
                    dve.wait_ge(cand_ready, n)

            limit = cand[:].bitcast(F32)
            done = [3]

            def then(ins):
                done[0] += 1
                ins.then_inc(step_done, 1)
                dve.wait_ge(step_done, done[0])

            dve.tensor_scalar(larger[:], sc[:], limit, 0.0, ALU.is_gt, ALU.add, accum_out=count[:]).then_inc(sums, 1)
            then(dve.tensor_scalar(equal[:], sc[:], limit, None, ALU.is_equal))
            then(dve.tensor_tensor_scan(rank[:], equal[:], zeros[:], 0.0, ALU.add, ALU.add))
            dve.wait_ge(turned, 1)
            dve.tensor_scalar(need[:], psum[1][:, 0:1], -1.0, float(TOPK), ALU.mult, ALU.add)
            then(dve.tensor_copy(count[:], rank[:, CHUNK - 1:CHUNK]))
            dve.sem_inc(sums)
            dve.wait_ge(turned, 2)
            then(dve.tensor_copy(offset[:], psum[2][:, 0:1]))
            then(dve.tensor_scalar(taken[:], rank[:], offset[:, 0:1], need[:, 0:1], ALU.add, ALU.is_le))
            then(dve.tensor_tensor(taken[:], taken[:], equal[:], ALU.mult))
            then(dve.tensor_tensor(chosen[:], taken[:], larger[:], ALU.add))
            then(dve.tensor_tensor_scan(rank[:], chosen[:], zeros[:], 0.0, ALU.add, ALU.add))
            then(dve.tensor_copy(count[:], rank[:, CHUNK - 1:CHUNK]))
            dve.sem_inc(sums)
            dve.wait_ge(turned, 3)
            then(dve.tensor_copy(offset[:], psum[3][:, 0:1]))
            dve.scalar_tensor_tensor(out=place[:], in0=rank[:], scalar=offset[:, 0:1], in1=chosen[:],
                                     op0=ALU.add, op1=ALU.mult).then_inc(sums, 1)
            dve.wait_ge(turned, 4)
            then(dve.tensor_scalar(place_i[:].rearrange("p t f -> p (t f)"), psum[4][:, 0:TPB * P], -1.0, None, ALU.add))
            flat = place_i[:].rearrange("p t f -> p (t f)")
            dve.tensor_scalar(part_i[:, 0], flat, P - 1, None, ALU.bitwise_and)
            then(dve.tensor_scalar(part_i[:, 1], flat, P.bit_length() - 1, None, ALU.arith_shift_right))
            dve.tensor_copy(part[:].rearrange("p a t f -> p (a t f)"),
                            part_i[:].rearrange("p a f -> p (a f)")).then_inc(part_ready, 1)
            dve.wait_ge(part_ready, 1)
            dve.wait_ge(consts, 3)
            for t in range(TPB):
                dve.tensor_tensor(slot[:, t], iota[:, None, :].to_broadcast([P, BATCH, P]),
                                  part[:, 0, t, 0:CHUNKS, None].to_broadcast([P, BATCH, P]), ALU.is_equal)
            token_numbers(dve, column, token, part[:, 1, :, 0:CHUNKS], numbers, column_ready, 1, (hot_ready, passed))
            dve.wait_ge(hot_used, 1)
            then(dve.tensor_copy(found[:].rearrange("p s v -> p (s v)"), psum[5][:, 0:NS * 2]))
            dve.scalar_tensor_tensor(out=index[:, 0, :], in0=found[:, :, 0], scalar=float(P), in1=found[:, :, 1],
                                     op0=ALU.mult, op1=ALU.add)

        @block.tensor
        def _(pe):
            for t in range(TPB):
                ins = pe.transpose(psum[0][:, t * P:(t + 1) * P], scores[:, t].rearrange("p e c -> p (e c)"), ident[:])
            ins.then_inc(sc_turned, 1)
            pe.wait_ge(made, 4)
            with pe.Fori(1, TOP_BIT + 2) as n:
                pe.wait_ge(counted, n)
                pe.matmul(psum[1][:, 0:1], same[:], count[:], start=True, stop=True).then_inc(summed, 1)
            for k, m in enumerate((same, before, before)):
                pe.wait_ge(sums, k + 1)
                pe.matmul(psum[1 + k][:, 0:1], m[:], count[:], start=True, stop=True).then_inc(turned, 1)
            pe.wait_ge(sums, 4)
            for t in range(TPB):
                ins = pe.transpose(psum[4][:, t * P:(t + 1) * P], place[:, t * P:(t + 1) * P], ident[:])
            ins.then_inc(turned, 1)
            pe.wait_ge(hot_ready, 1)
            for n in range(N // P):
                t, c = divmod(n, BATCH)
                ins = pe.matmul(psum[5][:, 0:NS * 2], slot[:, t, c, :], token[:, t, c].rearrange("p s v -> p (s v)"),
                                start=(n == 0), stop=(n == N // P - 1))
            ins.then_inc(hot_used, 1)


def expert_phase(nc, a, out, rows_dram, ident, tanh_g, ring, raw1, raw2, w_in, index, b1, numbers, psum, sb_all, sem):
    ctx = ExitStack()
    part, iota, tile_no, lane = numbers
    PIECES = 8
    TILES = N // P // PIECES
    LAST_E = EXPERTS - 1
    TURN_AT = 9
    with ctx:
        def sb(name, shape, dt=F32):
            return sb_all(name, shape, dt, ctx)

        xg = sb("xg", [P, STILES, ROW])
        xT = [[sb(f"xT{u}_{s}", [P, KB, SLOTS], F32R) for s in ("hi", "lo")] for u in range(2)]
        gate = [sb(f"gate{u}", [P, STILES]) for u in range(2)]
        picks = [sb(f"picks{u}", [P, STILES], U32) for u in range(2)]
        h = [sb(f"h{n}", [P, SLOTS]) for n in range(2)]
        h_hi = [sb(f"h_hi{n}", [P, SLOTS], F32R) for n in range(2)]
        h_lo = [sb(f"h_lo{n}", [P, SLOTS], F32R) for n in range(2)]
        y = sb("y", [P, STILES, D])
        b2 = sb("b2", [P, D])
        part_now = sb("part_now", [P, 2, TPB, BATCH], BF16)
        column = sb("column", [P, TPB, BATCH, NS], BF16)
        token = sb("token", [P, TPB, BATCH, NS, 2], BF16)
        slot = [sb(f"slot{n}", [P, TILES, P], BF16) for n in range(2)]
        found = sb("found", [P, NS, 2])
        gated_b2 = sb("gated_b2", [P, D])
        H, XB, Y = psum[0:2], psum[2:4], psum[4:8]

        picked = sem("picked")
        xg_in = sem("xg_in")
        x_turned, x_hi, x_ready = sem("x_turned"), sem("xg_hi"), sem("x_ready")
        gate_ready = sem("gate_set")
        h_filled, h_hi_done = sem("h_filled"), sem("h_hi_done")
        h_full = sem("h_full")
        h_ready = sem("h_ready")
        y_step = sem("y_step")
        y_free = [sem(f"y_free{n}") for n in range(2)]
        y_out = sem("y_out")
        y_landed = sem("y_landed")
        y_clear = sem("y_clear")
        w_hi_done = sem("w_hi_next")
        w_ready = sem("w_ready")
        b2_in, b2_gated = sem("b2_in"), sem("b2_gated")
        part_cut, column_set, token_set = sem("part_cut"), sem("column_set"), sem("token_set")
        slot_set = sem("slot_set")
        slot_used = sem("slot_used")
        found_out, index_set = sem("found_out"), sem("index_set")
        passed = sem("passed")
        block = ctx.enter_context(nc.Block())

        out_rows = out.rearrange("b s d -> (b s) d")

        def experts(eng, expert):
            with eng.Fori(0, LAST_E) as e:
                expert(e, False)
            expert(LAST_E, True)

        @block.sync
        def _(sp):
            sp.dma_start(b2[:], a["L0_ffn_b2"][0].partition_broadcast(P)).then_inc(b2_in, 16)

            def expert(e, last):
                if last:
                    return
                for m in range(HB):
                    if m >= 2:
                        sp.wait_ge(w_ready, HB * (e + 1) + m - 1)
                        sp.sem_inc(passed)
                    load_block(sp, a, raw1, raw2, w_in, e + 1, m)
                sp.wait_ge(y_out, STILES * PASSES * (e + 1))
                sp.sem_inc(passed)
                sp.dma_start(b2[:], a["L0_ffn_b2"][e + 1].partition_broadcast(P)).then_inc(b2_in, 16)
                sp.wait_ge(w_ready, HB * (e + 2))
                sp.sem_inc(passed)

            experts(sp, expert)

        @block.gpsimd
        def _(pool):
            pool.sem_inc(y_clear)

            def gather(e, u, half_):
                tiles = slice(half_ * STILES, (half_ + 1) * STILES)
                pool.tensor_copy(picks[half_][:, None, :], index[:, bass.ds(e, 1), tiles]).then_inc(picked, 1)
                pool.wait_ge(picked, u + 1)
                pool.wait_ge(x_turned, KB * u)
                pool.wait_ge(gate_ready, u)
                pool.sem_inc(passed)
                for t in range(STILES):
                    pool.indirect_dma_start(
                        out=xg[:, t, :], out_offset=None, in_=rows_dram[:, :],
                        in_offset=bass.IndirectOffsetOnAxis(ap=picks[half_][:, t:t + 1], axis=0)).then_inc(xg_in, 16)

            pool.tensor_copy(picks[0][:, None, :], index[:, 0:1, 0:STILES]).then_inc(picked, 1)
            pool.wait_ge(picked, 1)
            for t in range(STILES):
                pool.indirect_dma_start(
                    out=xg[:, t, :], out_offset=None, in_=rows_dram[:, :],
                    in_offset=bass.IndirectOffsetOnAxis(ap=picks[0][:, t:t + 1], axis=0)).then_inc(xg_in, 16)

            def expert(e, last):
                for half_ in range(PASSES):
                    u = PASSES * e + half_
                    if half_ + 1 < PASSES:
                        gather(e, u + 1, half_ + 1)
                    elif not last:
                        pool.wait_ge(index_set, e + 1)
                        gather(e + 1, u + 1, 0)
                    pool.wait_ge(b2_in, 16 * (e + 1))
                    pool.wait_ge(gate_ready, u + 1)
                    pool.sem_inc(passed)
                    for t in range(STILES):
                        if t >= 1:
                            pool.wait_ge(y_out, STILES * u + t)
                            pool.sem_inc(passed)
                        pool.tensor_scalar(gated_b2[:], b2[:], gate[half_][:, t:t + 1], None,
                                           ALU.mult).then_inc(b2_gated, 1)
                        pool.wait_ge(b2_gated, STILES * u + t + 1)
                        pool.wait_ge(y_free[t % 2], STILES // 2 * (u + 1) + t // 2 + 1)
                        pool.tensor_tensor(y[:, t, :], y[:, t, :], gated_b2[:], ALU.add).then_inc(y_out, 1)
                        pool.wait_ge(y_out, STILES * u + t + 1)
                        pool.sem_inc(passed)
                        pool.indirect_dma_start(
                            out=out_rows, out_offset=bass.IndirectOffsetOnAxis(ap=picks[half_][:, t:t + 1], axis=0),
                            in_=y[:, t, :], in_offset=None, compute_op=ALU.add).then_inc(y_landed, 16)
                    pool.wait_ge(y_landed, 16 * STILES * (u + 1))
                    pool.sem_inc(y_clear)

            experts(pool, expert)

        @block.scalar
        def _(act):
            act.sem_inc(h_full, 2)
            act.sem_inc(y_free[1], STILES // 2)

            def x_high(f, u2, k):
                act.wait_ge(x_turned, f + 1)
                act.activation(xT[u2][0][:, k, :], XB[k % 2][:, :], ACT.Copy).then_inc(x_hi, 1)

            def w_high(e, m, s):
                act.wait_ge(w_in[m % 2], 32 * (HB // 2) * (e + 1) + 32 * (m // 2 + 1))
                act.wait_ge(y_step, s + 3)
                act.activation(ring["w1_hi"][:, m], raw1[m % 2][:], ACT.Copy)
                act.activation(ring["w2_hi"][:, m], raw2[m % 2][:], ACT.Copy).then_inc(w_hi_done, 1)

            def hidden(e, s, m):
                act.wait_ge(h_filled, s + 1)
                act.wait_ge(h_ready, s + 1)
                act.sem_inc(passed)
                act.activation(h[m % 2][:], H[m % 2][:, :], ACT.Gelu, bias=b1[:, bass.ds(e, 1), m]).then_inc(h_full, 1)
                act.wait_ge(h_full, s + 3)
                act.wait_ge(y_step, s + 1)
                act.activation(h_hi[m % 2][:], h[m % 2][:], ACT.Copy).then_inc(h_hi_done, 1)

            for k in range(KB):
                x_high(k, 0, k)
            hidden(0, 0, 0)

            def expert(e, last):
                for half_ in range(PASSES):
                    u = PASSES * e + half_
                    end = last and half_ == PASSES - 1
                    for m in range(HB):
                        s = HB * u + m
                        if m + 1 < HB or not end:
                            hidden(e + (half_ * HB + m + 1) // (PASSES * HB), s + 1, (m + 1) % HB)
                        if m == HB - 1:
                            act.wait_ge(gate_ready, u + 1)
                            act.wait_ge(y_step, HB * (u + 1) + 2)
                            act.wait_ge(y_clear, u + 1)
                            act.sem_inc(passed)
                            for t in range(1, STILES, 2):
                                act.activation(y[:, t, :], Y[t][:, :], ACT.Identity,
                                               scale=gate[half_][:, t:t + 1]).then_inc(y_free[1], 1)
                        if half_ == PASSES - 1 and not last:
                            w_high(e, m, s)
                        if TURN_AT <= m < TURN_AT + KB and not end:
                            x_high(KB * (u + 1) + m - TURN_AT, 1 - half_, m - TURN_AT)

            experts(act, expert)

        @block.vector
        def _(dve):
            dve.sem_inc(h_ready, 2)
            dve.sem_inc(y_free[0], STILES // 2)
            dve.sem_inc(w_ready, HB)

            def gates_of(e, u, u2):
                dve.wait_ge(xg_in, 16 * STILES * (u + 1))
                if not isinstance(u, int) or u >= 2:
                    dve.wait_ge(y_clear, u)
                dve.tensor_scalar(gate[u2][:, :, None], xg[:, :, bass.ds(e + D, 1)], tanh_g[:, 1:2], None,
                                  ALU.mult).then_inc(gate_ready, 1)

            def x_low(f, u2, k):
                dve.wait_ge(x_hi, f + 1)
                dve.tensor_tensor(xT[u2][1][:, k, :], XB[k % 2][:, :], xT[u2][0][:, k, :].bitcast(F32),
                                  ALU.subtract).then_inc(x_ready, 1)

            def w_low(e, m):
                dve.wait_ge(w_hi_done, HB * e + m + 1)
                dve.tensor_tensor(ring["w1_lo"][:, m], raw1[m % 2][:], ring["w1_hi"][:, m].bitcast(F32), ALU.subtract)
                dve.tensor_tensor(ring["w2_lo"][:, m], raw2[m % 2][:], ring["w2_hi"][:, m].bitcast(F32),
                                  ALU.subtract).then_inc(w_ready, 1)

            def hidden(s, m):
                dve.wait_ge(h_hi_done, s + 1)
                dve.tensor_tensor(h_lo[m % 2][:], h[m % 2][:], h_hi[m % 2][:].bitcast(F32),
                                  ALU.subtract).then_inc(h_ready, 1)

            def find_tokens(e, n):
                if n == 0:
                    dve.tensor_copy(part_now[:], part[:, :, :, bass.ds((e + 1) * CHUNKS, CHUNKS)]).then_inc(part_cut, 1)
                    dve.wait_ge(part_cut, e + 1)
                    dve.sem_inc(passed)
                    token_numbers(dve, column, token, part_now[:, 1], numbers, column_set, e + 1, (token_set, passed))
                t, c = divmod(n * TILES, BATCH)
                shape = [P, TILES, P]
                dve.wait_ge(slot_used, PIECES * e + n + 1)
                dve.sem_inc(passed)
                dve.tensor_tensor(slot[n % 2][:], iota[:, None, :].to_broadcast(shape),
                                  part_now[:, 0, t, c:c + TILES, None].to_broadcast(shape),
                                  ALU.is_equal).then_inc(slot_set, 1)

            def found_tokens(e):
                dve.wait_ge(slot_used, PIECES * (e + 1) + 2)
                dve.sem_inc(passed)
                dve.tensor_copy(found[:].rearrange("p s v -> p (s v)"), XB[0][:, 0:NS * 2]).then_inc(found_out, 1)
                dve.wait_ge(found_out, e + 1)
                dve.sem_inc(passed)
                dve.scalar_tensor_tensor(out=index[:, bass.ds(e + 1, 1), :], in0=found[:, None, :, 0], scalar=float(P),
                                         in1=found[:, None, :, 1], op0=ALU.mult, op1=ALU.add).then_inc(index_set, 1)

            gates_of(0, 0, 0)
            for k in range(KB):
                x_low(k, 0, k)
            hidden(0, 0)

            def expert(e, last):
                for half_ in range(PASSES):
                    u = PASSES * e + half_
                    end = last and half_ == PASSES - 1
                    for m in range(HB):
                        s = HB * u + m
                        if m + 1 < HB or not end:
                            hidden(s + 1, (m + 1) % HB)
                        if m == HB - 1:
                            dve.wait_ge(y_step, HB * (u + 1) + 2)
                            dve.wait_ge(y_clear, u + 1)
                            dve.sem_inc(passed)
                            for t in range(0, STILES, 2):
                                dve.tensor_scalar(y[:, t, :], Y[t][:, :], gate[half_][:, t:t + 1], None,
                                                  ALU.mult).then_inc(y_free[0], 1)
                        if half_ == 0 and not last and m < PIECES:
                            find_tokens(e, m)
                        if half_ == 0 and not last and m == PIECES:
                            found_tokens(e)
                        if half_ == PASSES - 1 and not last:
                            w_low(e, m)
                        if not end:
                            if m == TURN_AT:
                                gates_of(e + (half_ + 1) // PASSES, u + 1, 1 - half_)
                            if TURN_AT <= m < TURN_AT + KB:
                                x_low(KB * (u + 1) + m - TURN_AT, 1 - half_, m - TURN_AT)

            experts(dve, expert)

        @block.tensor
        def _(pe):
            pe.sem_inc(y_step, 2)
            pe.sem_inc(slot_used, 2)

            def turn_tokens(f, u, k):
                if k == 0:
                    pe.wait_ge(xg_in, 16 * STILES * (u + 1))
                if not isinstance(f, int) or f >= 2:
                    pe.wait_ge(x_ready, f - 1)
                for t in range(STILES):
                    ins = pe.transpose(XB[k % 2][:, t * P:(t + 1) * P], xg[:, t, k * P:(k + 1) * P], ident[:])
                ins.then_inc(x_turned, 1)

            def first_layer(e, half_, s, m):
                u2 = half_ % 2
                if m == 0:
                    pe.wait_ge(x_ready, KB * (PASSES * e + half_ + 1))
                if half_ == 0:
                    pe.wait_ge(w_ready, HB * e + m + 1)
                pe.wait_ge(h_full, s + 1)
                x_hi_, x_lo_ = xT[u2]
                at = 0
                for k in range(KB):
                    w_hi_, w_lo_ = ring["w1_hi"][:, m, k, :], ring["w1_lo"][:, m, k, :]
                    for w, x in ((w_hi_, x_hi_), (w_hi_, x_lo_), (w_lo_, x_hi_)):
                        ins = pe.matmul(H[m % 2][:, :], w, x[:, k, :], start=(at == 0), stop=(at == 3 * KB - 1))
                        at += 1
                ins.then_inc(h_filled, 1)

            def second_layer(u, s, m):
                pe.wait_ge(h_ready, s + 3)
                w_hi_, w_lo_ = ring["w2_hi"][:, m, :], ring["w2_lo"][:, m, :]
                for t in range(STILES):
                    if m == 0:
                        pe.wait_ge(y_free[t % 2], STILES // 2 * u + t // 2 + 1)
                    cols = slice(t * P, (t + 1) * P)
                    hi, lo = h_hi[m % 2][:, cols], h_lo[m % 2][:, cols]
                    for n, (x, w) in enumerate(((hi, w_hi_), (hi, w_lo_), (lo, w_hi_))):
                        ins = pe.matmul(Y[t][:, :], x, w, start=(m == 0 and n == 0), stop=(m == HB - 1 and n == 2))
                ins.then_inc(y_step, 1)

            def place_tokens(e, n):
                if n == 0:
                    pe.wait_ge(token_set, e + 1)
                pe.wait_ge(slot_set, PIECES * e + n + 1)
                for c in range(TILES):
                    tok = token[:].rearrange("p t b s v -> p (t b) (s v)")[:, n * TILES + c]
                    ins = pe.matmul(XB[0][:, 0:NS * 2], slot[n % 2][:, c, :], tok, start=(n == 0 and c == 0),
                                    stop=(n == PIECES - 1 and c == TILES - 1))
                ins.then_inc(slot_used, 1)

            for k in range(KB):
                turn_tokens(k, 0, k)
            first_layer(0, 0, 0, 0)

            def expert(e, last):
                for half_ in range(PASSES):
                    u = PASSES * e + half_
                    for m in range(HB):
                        s = HB * u + m
                        if m + 1 < HB:
                            first_layer(e, half_, s + 1, m + 1)
                        elif half_ + 1 < PASSES:
                            first_layer(e, half_ + 1, s + 1, 0)
                        elif not last:
                            first_layer(e + 1, 0, s + 1, 0)
                        if half_ == 0 and not last and 1 <= m <= PIECES:
                            place_tokens(e, m - 1)
                        if TURN_AT <= m < TURN_AT + KB and not (last and half_ == PASSES - 1):
                            if half_ == 0 and not last and m == TURN_AT:
                                pe.wait_ge(found_out, e + 1)
                            turn_tokens(KB * (u + 1) + m - TURN_AT, u + 1, m - TURN_AT)
                        second_layer(u, s, m)

            experts(pe, expert)


_OUT = (BATCH, SEQ, D)


def kernel(**inputs):
    import numpy as np
    from concourse import bacc
    from concourse.bass_utils import run_bass_kernel_spmd

    nc = bacc.Bacc("TRN2", target_bir_lowering=False, num_devices=1)
    arrays = {f"in_{n}": np.ascontiguousarray(v) for n, v in inputs.items()}
    args = {n: nc.dram_tensor(f"in_{n}", arrays[f"in_{n}"].shape, mybir.dt.from_np(arrays[f"in_{n}"].dtype),
                              kind="ExternalInput").ap() for n in inputs}
    out = nc.dram_tensor("out_x", _OUT, F32, kind="ExternalOutput").ap()
    block_program(nc, args, out)
    r = run_bass_kernel_spmd(nc, [arrays], core_ids=[0])
    return r.results[0]["out_x"]
```

```python
from contextlib import ExitStack

import concourse.bass as bass
from concourse import mybir

ALU = mybir.AluOpType
ACT = mybir.ActivationFunctionType
AX = mybir.AxisListType.X
F32 = mybir.dt.float32
F32R = mybir.dt.float32r
BF16 = mybir.dt.bfloat16
I32 = mybir.dt.int32
U32 = mybir.dt.uint32

P = 128
BATCH, SEQ, D = 16, 256, 512
HEADS = 16
DH = D // HEADS
HPB = P // DH
KB = D // P
TPB = SEQ // P
N = BATCH * SEQ
EXPERTS = 8
TOPK = max(4, -(-N * 2 // EXPERTS))
DI = 2048
HB = DI // P
SCALE = float(DH) ** -0.5
EPS = 1e-5
MASKED = -1e30
ROW = D + EXPERTS
SLOTS = 512
PASSES = TOPK // SLOTS
STILES = SLOTS // P
CHUNKS = P // EXPERTS
CHUNK = N // CHUNKS
NS = TOPK // P
STACK = (("hi", "hi", "lo"), ("hi", "lo", "hi"))
VW = DH + 1

FILLS = [("CT0", "P", 0), ("Q2", "A", 0), ("CT1", "P", 1), ("Q3", "A", 1), ("XT0", "P", 2), ("K0", "P", 2),
         ("XT1", "P", 3), ("AT0", "U", 4), ("Q0", "P", 4), ("AT1", "U", 5), ("O0", "U", 6), ("O1", "U", 8),
         ("V0", "P", 10), ("X2T0", "U", 12), ("K1", "P", 12), ("X2T1", "U", 13), ("R", "U", 14), ("V1", "P", 14)]
LONG = ("K0", "K1", "Q0", "V0", "V1", "O0", "O1")
BLOCKS = {"Q2": (2,), "Q3": (3,), "K0": (0, 1), "Q0": (0, 1), "K1": (2, 3)}
LATE = ("O0", "O1", "R", *BLOCKS)
ORDER = [w for w, _, _ in FILLS]
LAST = BATCH
STEADY = (3, BATCH - 1)


def stages(i):
    if not isinstance(i, int):
        return "PAU"
    return "P" * (i + 1 < BATCH) + "A" * (0 <= i < BATCH) + "U" * (i >= 1)


def fills(i):
    return [(w, s, h) for w, s, h in FILLS if s in stages(i)]


def parts_at(i, n):
    if "A" not in stages(i):
        return [(w, part) for w, _, _ in fills(i) for part in ((0, 1) if w in LONG else (None,))]
    parts = []
    for w, _, at in fills(i):
        parts += [(at, w, 0), (at + 1, w, 1)] if w in LONG else [(at, w, None)]
    here = [(w, part) for at, w, part in parts if at == n]
    return sorted(here, key=lambda p: p[1] == 1)


def ends_at(i, n):
    return [w for w, part in parts_at(i, n) if part != 0]


def fill(i, what):
    names = [w for w, _, _ in fills(i)]
    at = names.index(what)
    per = len(FILLS) // 2

    def before(step, bank):
        return sum(sum(n % 2 == bank for n in range(len(fills(s)))) for s in range(-1, step))

    if isinstance(i, int):
        return at % 2, before(i, at % 2) + at // 2 + 1
    return at % 2, i * per + (before(1, at % 2) - per + at // 2 + 1)


def of_row(what, b):
    stage = next(s for w, s, _ in FILLS if w == what)
    return fill({"P": b - 1, "A": b, "U": b + 1}[stage], what)


def block_program(nc, a, out):
    ctx = ExitStack()
    with ctx:
        def sb(name, shape, dt=F32, where=ctx):
            return where.enter_context(nc.sbuf_tensor(name, shape, dt))

        def sem(name):
            return ctx.enter_context(nc.semaphore(name))

        rows_dram = nc.dram_tensor("token_rows", [N, ROW], F32)
        ident = sb("ident", [P, P])
        scores = sb("scores", [P, TPB, EXPERTS, BATCH])
        tanh_g = sb("tanh_g", [P, 2])
        psum = [ctx.enter_context(nc.psum_tensor(f"bank{i}", [P, 512], F32)) for i in range(8)]
        stored = attention_phase(nc, a, out, rows_dram, ident, scores, tanh_g, psum, sb, sem)

        ring = {n: sb(n, shape, F32R) for n, shape in (
            ("w1_hi", [P, HB, KB, P]), ("w1_lo", [P, HB, KB, P]), ("w2_hi", [P, HB, D]), ("w2_lo", [P, HB, D]))}
        raw1 = [sb(f"w1_raw{p}", [P, KB, P]) for p in range(2)]
        raw2 = [sb(f"w2_raw{p}", [P, D]) for p in range(2)]
        index = sb("index", [P, EXPERTS, TOPK // P], U32)
        b1 = sb("b1", [P, EXPERTS, HB])
        part = sb("part", [P, 2, TPB, P], BF16)
        iota = sb("iota", [P, P], BF16)
        tile_no = sb("tile_no", [P, TPB, BATCH], BF16)
        lane = sb("lane", [P, 1])
        w_in = [sem(f"w_in{p}") for p in range(2)]
        numbers = (part, iota, tile_no, lane)
        selection_phase(nc, a, ident, scores, ring, index, b1, numbers, stored, psum, sem)
        expert_phase(nc, a, out, rows_dram, ident, tanh_g, ring, raw1, raw2, w_in, index, b1, numbers, psum, sb, sem)


def token_numbers(eng, column, token, part, numbers, column_ready, n, ready):
    _, iota, tile_no, lane = numbers
    shape = [P, TPB, BATCH, NS]
    iotas = iota[:, 0:NS].rearrange("p (a b n) -> p a b n", a=1, b=1)
    eng.tensor_tensor(column[:], iotas.to_broadcast(shape), part[:, :, :, None].to_broadcast(shape),
                      ALU.is_equal).then_inc(column_ready, 1)
    eng.wait_ge(column_ready, n)
    eng.sem_inc(ready[1])
    eng.tensor_tensor(token[:, :, :, :, 0], column[:], tile_no[:, :, :, None].to_broadcast(shape), ALU.mult)
    eng.tensor_scalar(token[:, :, :, :, 1], column[:], lane[:, 0:1], None, ALU.mult).then_inc(ready[0], 1)


def attention_phase(nc, a, out, rows_dram, ident, scores, tanh_g, psum, sb_all, sem):
    ctx = ExitStack()
    with ctx:
        def sb(name, shape, dt=F32):
            return sb_all(name, shape, dt, ctx)

        mask = sb("mask", [P, TPB * P])
        half = sb("half", [P, TPB])
        bq = sb("bq", [P, KB])
        bk = sb("bk", [P, KB])
        bv = sb("bv", [P, D])
        bo = sb("bo", [P, D])
        wr = sb("wr", [P, KB, EXPERTS])
        names = ("wq", "wk", "wv", "wo")
        w_hi = {n: sb(n + "_hi", [P, KB, D], F32R) for n in names}
        w_lo = {n: sb(n + "_lo", [P, KB, D], F32R) for n in names}
        S, PT, O, W = psum[0:2], psum[2:4], psum[4:6], psum[6:8]

        xin = [sb(f"xin{p}", [P, TPB, D]) for p in range(2)]
        cin = [sb(f"cin{p}", [P, TPB, D]) for p in range(2)]
        x_in = [sem(f"x_in{p}") for p in range(2)]
        c_in = [sem(f"c_in{p}") for p in range(2)]
        x_v = a["x"].rearrange("b (t p) d -> b p t d", p=P)
        c_v = a["ctx_1024"].rearrange("b (t p) d -> b p t d", p=P)

        def load_first(sp):
            sp.dma_start(xin[0][:], x_v[0]).then_inc(x_in[0], 16)
            sp.dma_start(cin[0][:], c_v[0]).then_inc(c_in[0], 16)

        const_ready = sem("const_ready")
        weights_setup(nc, a, const_ready, ident, mask, half, bq, bk, bv, bo, wr, tanh_g, w_hi, w_lo, names, psum,
                      load_first, sem)

        x1 = [sb(f"x1{p}", [P, TPB, D]) for p in range(2)]
        xn = sb("xn", [P, TPB, D])
        xnT = [sb(f"xnT_{s}", [P, KB, SEQ], F32R) for s in ("hi", "lo")]
        cT = [sb(f"cT_{s}", [P, KB, SEQ], F32R) for s in ("hi", "lo")]
        aT = [sb(f"aT_{s}", [P, KB, SEQ], F32R) for s in ("hi", "lo")]
        QT = {s: sb(f"QT_{s}", [P, KB, SEQ], F32R) for s in ("hi", "lo")}
        KT = {s: sb(f"KT_{s}", [P, KB, SEQ], F32R) for s in ("hi", "lo")}
        qk = sb("qk", [P, 2, SEQ])
        QS = sb("Q_stacked", [len(STACK[0]) * DH, HPB, KB, SEQ], F32R)
        KS = sb("K_stacked", [len(STACK[0]) * DH, HPB, KB, SEQ], F32R)
        V = [sb(f"V{p}", [P, TPB, HEADS, VW]) for p in range(2)]
        E = [sb(f"E{p}", [P, 3 * P]) for p in range(2)]
        ET = [sb(f"ET{p}", [P, 3 * P]) for p in range(2)]
        least = [sb(f"least{p}", [P, 2]) for p in range(2)]
        attn = [sb(f"attn{p}", [P, TPB, D]) for p in range(2)]
        rsum = sb("rsum", [P, TPB * HPB])
        rows = [sb(f"rows{p}", [P, TPB, ROW]) for p in range(2)]
        xn2T = sb("xn2T", [P, TPB, KB, P])
        stats1 = sb("stats1", [P, TPB, 6])
        mv1 = sb("mv1", [P, TPB, 2])
        ve1 = sb("ve1", [P, TPB])
        rstd1 = sb("rstd1", [P, TPB])
        stats2 = sb("stats2", [P, TPB, 6])
        mv2 = sb("mv2", [P, TPB, 2])
        ve2 = sb("ve2", [P, TPB])
        rstd2 = sb("rstd2", [P, TPB])
        rmax = sb("rmax", [P, TPB])
        rdiff = sb("rdiff", [P, TPB, EXPERTS])
        rexp = sb("rexp", [P, TPB, EXPERTS])
        rtot = sb("rtot", [P, TPB])
        rinv = sb("rinv", [P, TPB])
        prob = sb("prob", [P, TPB, EXPERTS])

        xres_in = [sem(f"xres_in{p}") for p in range(2)]
        x1_stored = [sem(f"x1_stored{p}") for p in range(2)]
        rows_stored = [sem(f"rows_stored{p}") for p in range(2)]
        ones_set = sem("ones_set")
        waited = sem("waited")
        ln1_stats, ln1_mv, ln1_ve, ln1_rstd, xn_ready = map(
            sem, ("ln1_stats", "ln1_mv", "ln1_ve", "ln1_rstd", "xn_ready"))
        ln2_stats, ln2_mv, ln2_ve, ln2_rstd, xn2_ready = map(
            sem, ("ln2_stats", "ln2_mv", "ln2_ve", "ln2_rstd", "xn2_ready"))
        filled = [sem(f"filled{n}") for n in range(2)]
        drained = [sem(f"drained{n}") for n in range(2)]
        x_hi, c_hi, a_hi = map(sem, ("x_hi", "c_hi", "a_hi"))
        qk_full, qk_hi, qk_lo = map(sem, ("qk_full", "qk_hi", "qk_lo"))
        stacked = [sem(f"stacked{n}") for n in range(2)]
        STACKED = 16 * 2 * len(STACK[0]) * HPB
        xb_ready = sem("xb_ready")
        s_done, least_done, e_done, t_done, et_done, pv_done = map(
            sem, ("s_done", "least_done", "e_done", "t_done", "et_done", "pv_done"))
        sums_inv, norm_done = sem("sums_inv"), sem("norm_done")
        r_max, r_exp, r_tot, r_inv, prob_ready, score_kept = map(
            sem, ("r_max", "r_exp", "r_tot", "r_inv", "prob_ready", "score_kept"))

        out_v = out.rearrange("b (t p) d -> b p t d", p=P)
        rows_v = rows_dram[:, :].rearrange("(b t p) d -> b p t d", p=P, t=TPB)

        def wait(eng, semaphore, value):
            if not isinstance(value, int) or value > 0:
                eng.wait_ge(semaphore, value)

        def wait_banks(eng, semaphores, b, whats, banks=(0, 1)):
            for bank in banks:
                of_bank = [w for w in whats if of_row(w, b)[0] == bank]
                if of_bank:
                    eng.wait_ge(semaphores[bank], of_row(max(of_bank, key=ORDER.index), b)[1])
                    if eng is nc.sync:
                        eng.sem_inc(waited)

        def wait_filled(eng, b, *whats):
            wait_banks(eng, filled, b, whats)

        def wait_drained(eng, b, *whats):
            wait_banks(eng, drained, b, whats)

        def qk_count(what, i):
            return len(BLOCKS) * (i + 1) - 2 + list(BLOCKS).index(what)

        def exists(b):
            return not isinstance(b, int) or b >= 0

        def at_start(i):
            return isinstance(i, int) and i == -1

        def steps(eng, step, ahead=0):
            for i in range(-1, STEADY[0]):
                step(i, i % 2, i // 2)
            first = STEADY[0]
            turns = (STEADY[1] - ahead - first) // 2
            with eng.Fori(0, turns) as j:
                for k in range(2):
                    step(2 * j + (first + k), (first + k) % 2, j + (first + k) // 2)
            for i in range(first + 2 * turns, LAST + 1):
                step(i, i % 2, i // 2)

        stored = [(x1_stored[p], 16 * (BATCH // 2)) for p in range(2)] + \
                 [(rows_stored[p], 16 * (BATCH // 2)) for p in range(2)]
        block = ctx.enter_context(nc.Block())

        @block.sync
        def _(sp):
            def stack(half, to, parts, order, split):
                fbs = slice(half * KB // 2, (half + 1) * KB // 2)
                for part_, ready in (("hi", qk_hi), ("lo", qk_lo)):
                    sp.wait_ge(ready, split)
                    sp.sem_inc(waited)
                    for n in (n for n, what in enumerate(order) if what == part_):
                        for j in range(HPB):
                            head = parts[part_][j * DH:(j + 1) * DH, fbs, :]
                            sp.dma_start(to[n * DH:(n + 1) * DH, j, fbs, :].bitcast(F32),
                                         head.bitcast(F32)).then_inc(stacked[half], 16)

            def step(i, p, h):
                if "A" in stages(i):
                    wait(sp, s_done, i * HEADS)
                    sp.sem_inc(waited)
                    stack(1, KS, KT, STACK[1], qk_count("K1", i - 1) + 1)
                    stack(1, QS, QT, STACK[0], qk_count("Q3", i) + 1)
                if not isinstance(i, int) or i + 2 < BATCH:
                    wait(sp, xn_ready, TPB * (i + 1))
                    sp.sem_inc(waited)
                    sp.dma_start(xin[p][:], x_v[i + 2]).then_inc(x_in[p], 16)
                    if exists(i):
                        wait_filled(sp, i, "CT1")
                        sp.sem_inc(waited)
                    sp.dma_start(cin[p][:], c_v[i + 2]).then_inc(c_in[p], 16)
                if "A" in stages(i):
                    if exists(i - 2):
                        sp.wait_ge(x1_stored[p], 16 * h)
                        sp.sem_inc(waited)
                    sp.dma_start(x1[p][:], x_v[i]).then_inc(xres_in[p], 16)
                if "P" in stages(i):
                    if "A" in stages(i):
                        sp.wait_ge(s_done, i * HEADS + HEADS // 2)
                        sp.sem_inc(waited)
                    stack(0, KS, KT, STACK[1], qk_count("K0", i) + 1)
                    stack(0, QS, QT, STACK[0], qk_count("Q0", i) + 1)
                if "U" in stages(i):
                    q = 1 - p
                    wait_drained(sp, i - 1, "O1")
                    sp.sem_inc(waited)
                    sp.dma_start(out_v[i - 1], x1[q][:]).then_inc(x1_stored[q], 16)
                    sp.wait_ge(prob_ready, i)
                    sp.sem_inc(waited)
                    sp.dma_start(rows_v[i - 1], rows[q][:]).then_inc(rows_stored[q], 16)

            steps(sp, step, 1)

        @block.gpsimd
        def _(pool):
            def inverse_deviation(mv, ve, rstd, ready_mv, n_mv, s_ve, n_ve, s_rstd):
                pool.wait_ge(ready_mv, n_mv)
                pool.sem_inc(waited)
                pool.tensor_scalar(ve, mv[:, :, 1], EPS, None, ALU.add).then_inc(s_ve, 1)
                pool.wait_ge(s_ve, n_ve + 1)
                pool.tensor_tensor(rstd, ve, half[:, 0:ve.shape[1]], ALU.pow).then_inc(s_rstd, 1)
                pool.wait_ge(s_rstd, n_ve + 1)
                pool.sem_inc(waited)

            def norm1(b, p):
                inverse_deviation(mv1, ve1[:], rstd1[:], ln1_mv, TPB * (b + 1), ln1_ve, b, ln1_rstd)
                if not exists(b - 1):
                    return
                if exists(b - 1):
                    wait_filled(pool, b - 1, "XT1")
                pool.sem_inc(waited)
                for t in range(TPB):
                    pool.tensor_scalar(xn[:, t, :], xin[p][:, t, :], mv1[:, t, 0:1], rstd1[:, t:t + 1],
                                       ALU.subtract, ALU.mult).then_inc(xn_ready, 1)

            def norm2(b, p, h, t):
                inverse_deviation(mv2[:, t:t + 1, :], ve2[:, t:t + 1], rstd2[:, t:t + 1], ln2_mv,
                                  TPB * b + t + 1, ln2_ve, TPB * b + t, ln2_rstd)
                if isinstance(b, int) and b == BATCH - 1:
                    return
                if t == 0 and exists(b - 2):
                    pool.wait_ge(rows_stored[p], 16 * h)
                pool.sem_inc(waited)
                pool.tensor_scalar(rows[p][:, t, 0:D], x1[p][:, t, :], mv2[:, t, 0:1], rstd2[:, t:t + 1],
                                   ALU.subtract, ALU.mult).then_inc(xn2_ready, 1)

            def step(i, p, h):
                q = 1 - p
                hq = h if p else h - 1
                if at_start(i):
                    norm1(0, 0)
                    norm1(1, 1)
                if "U" in stages(i):
                    pool.wait_ge(xres_in[q], 16 * (hq + 1))
                    pool.tensor_tensor(x1[q][:], x1[q][:], bo[:, None, :].to_broadcast([P, TPB, D]),
                                       ALU.add).then_inc(xb_ready, 1)
                if "U" in stages(i):
                    for t in range(TPB):
                        norm2(i - 1, q, hq, t)
                if not isinstance(i, int) or 0 <= i < BATCH - 2:
                    norm1(i + 2, p)
                if "U" in stages(i):
                    pool.wait_ge(prob_ready, i)
                    pool.tensor_copy(scores[:, :, :, bass.ds(i - 1, 1)], prob[:, :, :, None]).then_inc(score_kept, 1)

            steps(pool, step, 1)

        @block.scalar
        def _(act):
            def exp_head(n, e):
                act.wait_ge(least_done, n + 1)
                act.activation(E[e][:, 0:P], E[e][:, 0:P], ACT.Exp, bias=least[e][:, 0:1], scale=-1.0)
                act.activation(E[e][:, P:3 * P], E[e][:, P:3 * P], ACT.Exp, bias=least[e][:, 1:2],
                               scale=-1.0).then_inc(e_done, 1)

            def evacuate(what, i, p):
                bank, n = fill(i, what.rstrip("+"))
                w = W[bank]
                b, q = i + 1, 1 - p
                two = w[:, :].rearrange("p (k s) -> p k s", k=2)
                if what in ("XT0", "XT1", "CT0", "CT1", "AT0", "AT1"):
                    k = 2 * int(what[-1])
                    to, s_hi = {"X": (xnT, x_hi), "C": (cT, c_hi), "A": (aT, a_hi)}[what[0]]
                    if what == "XT0" and exists(b - 1):
                        wait_filled(act, b - 1, "Q3")
                    if what == "CT0" and exists(b - 1):
                        wait_filled(act, b - 1, "K1", "V1")
                    if what == "AT0" and exists(i - 2):
                        wait_filled(act, i - 2, "O1")
                    act.wait_ge(filled[bank], n)
                    act.activation(to[0][:, k:k + 2, :], two, ACT.Copy).then_inc(s_hi, 1)
                if what in BLOCKS:
                    k = BLOCKS[what][0]
                    bias = bq if what[0] == "Q" else bk
                    wait(act, qk_lo, qk_count(what, i))
                    act.wait_ge(filled[bank], n)
                    for f in BLOCKS[what]:
                        ins = act.activation(qk[:, f - k, :], two[:, f - k, :], ACT.Identity, bias=bias[:, f:f + 1])
                    ins.then_inc(drained[bank], 1)
                if what.rstrip("+") in BLOCKS and what[-1] == "+":
                    what = what[:-1]
                    k = BLOCKS[what][0]
                    to = QT if what[0] == "Q" else KT
                    row = i if what in ("Q2", "Q3") else b
                    wait(act, stacked[k // 2], STACKED * row)
                    act.wait_ge(drained[bank], n)
                    blocks = slice(k, k + len(BLOCKS[what]))
                    act.activation(to["hi"][:, blocks, :], qk[:, 0:len(BLOCKS[what]), :], ACT.Copy).then_inc(qk_hi, 1)
                if what in ("X2T0", "X2T1"):
                    t = int(what[-1])
                    if t == 0 and exists(i - 2):
                        wait_filled(act, i - 2, "R")
                    act.wait_ge(filled[bank], n)
                    act.activation(xn2T[:, t, :, :], w[:, :].rearrange("p (k s) -> p k s", k=KB),
                                   ACT.Copy).then_inc(drained[bank], 1)
                if what == "R":
                    bank, n = fill(i, "R")
                    act.wait_ge(drained[bank], n)
                    act.activation(rexp[:], rdiff[:], ACT.Exp).then_inc(r_exp, 1)

            def step(i, p, h):
                for n in range(HEADS if "A" in stages(i) else 1):
                    if "A" in stages(i):
                        g = i * HEADS + n
                        act.wait_ge(t_done, g + 1)
                        wait(act, pv_done, g - 1)
                        act.activation(ET[n % 2][:], PT[n % 2][:, 0:3 * P], ACT.Copy).then_inc(et_done, 1)
                        if n + 1 < HEADS or "P" in stages(i):
                            exp_head(g + 1, (n + 1) % 2)
                    for what in ends_at(i, n):
                        if what != "R" or "A" not in stages(i):
                            evacuate(what, i, p)
                        if what in BLOCKS and "A" not in stages(i):
                            evacuate(what + "+", i, p)
                    for what in ends_at(i, n) if "A" in stages(i) else ():
                        if what in BLOCKS:
                            evacuate(what + "+", i, p)
                    if n == HEADS - 1 and "U" in stages(i):
                        evacuate("R", i, p)
                if at_start(i):
                    exp_head(0, 0)

            steps(act, step)

        @block.vector
        def _(dve):
            def masked_scores(n, e):
                dve.wait_ge(s_done, n + 1)
                wait(dve, t_done, n - 1)
                dve.sem_inc(waited)
                for t, (lo, hi) in enumerate(((0, P), (P, 3 * P))):
                    ins = dve.tensor_tensor_reduce(out=E[e][:, lo:hi], in0=S[e][:, lo:hi],
                                                   in1=mask[:, (1 - t) * P:2 * P], scale=-SCALE, scalar=-MASKED, op0=ALU.add, op1=ALU.min,
                                                   accum_out=least[e][:, t:t + 1])
                ins.then_inc(least_done, 1)

            def normalise_group(g, p, fb):
                o = O[fb % 2][:, 0:TPB * HPB * VW].rearrange("p (t h v) -> p t h v", t=TPB, v=VW)
                flat = O[fb % 2][:, 0:TPB * HPB * VW].rearrange("p (g v) -> p g v", v=VW)
                dve.wait_ge(pv_done, HPB * (g + 1))
                dve.reciprocal(rsum[:, :], flat[:, :, DH]).then_inc(sums_inv, 1)
                dve.wait_ge(sums_inv, g + 1)
                inv = rsum[:, :].rearrange("p (t h) -> p t h", t=TPB)[:, :, :, None].to_broadcast([P, TPB, HPB, DH])
                dve.tensor_tensor(attn[p][:, :, fb * P:(fb + 1) * P].rearrange("p t (h v) -> p t h v", v=DH),
                                  o[:, :, :, 0:DH], inv, ALU.mult).then_inc(norm_done, 1)

            def ln1(b, p, h):
                dve.wait_ge(x_in[p], 16 * (h + 1))
                wait(dve, ln1_mv, TPB * b)
                for t in range(TPB):
                    dve.bn_stats(stats1[:, t, :], xin[p][:, t, :]).then_inc(ln1_stats, 1)
                dve.wait_ge(ln1_stats, TPB * (b + 1))
                wait(dve, xn_ready, TPB * b)
                dve.sem_inc(waited)
                for t in range(TPB):
                    dve.bn_aggr(mv1[:, t, :], stats1[:, t, :]).then_inc(ln1_mv, 1)

            def evacuate(what, i, p):
                bank, n = fill(i, what.rstrip("+"))
                w = W[bank]
                b, q = i + 1, 1 - p
                two = w[:, :].rearrange("p (k s) -> p k s", k=2)
                if what in ("XT0", "XT1", "CT0", "CT1", "AT0", "AT1"):
                    f = int(what[-1])
                    k = 2 * f
                    to, s_hi = {"X": (xnT, x_hi), "C": (cT, c_hi), "A": (aT, a_hi)}[what[0]]
                    row = i - 1 if what[0] == "A" else b
                    dve.wait_ge(s_hi, 2 * row + f + 1)
                    dve.tensor_tensor(to[1][:, k:k + 2, :], two, to[0][:, k:k + 2, :].bitcast(F32),
                                      ALU.subtract).then_inc(drained[bank], 1)
                if what in BLOCKS:
                    k = BLOCKS[what][0]
                    to = QT if what[0] == "Q" else KT
                    blocks = slice(k, k + len(BLOCKS[what]))
                    dve.wait_ge(qk_hi, qk_count(what, i) + 1)
                    dve.tensor_tensor(to["lo"][:, blocks, :], qk[:, 0:len(BLOCKS[what]), :],
                                      to["hi"][:, blocks, :].bitcast(F32), ALU.subtract).then_inc(qk_lo, 1)
                if what in ("V0", "V1"):
                    t = int(what[-1])
                    if t == 0 and exists(b - 2):
                        dve.wait_ge(pv_done, HEADS * (b - 1))
                    dve.wait_ge(filled[bank], n)
                    dve.tensor_tensor(V[q][:, t, :, 0:DH], w[:, :].rearrange("p (h v) -> p h v", v=DH),
                                      bv[:, :].rearrange("p (h v) -> p h v", v=DH), ALU.add).then_inc(drained[bank], 1)
                if what in ("O0", "O1"):
                    t = int(what[-1])
                    dve.wait_ge(filled[bank], n)
                    dve.wait_ge(xb_ready, i)
                    dve.scalar_tensor_tensor(out=x1[q][:, t, :], in0=w[:, :], scalar=tanh_g[:, 0:1],
                                             in1=x1[q][:, t, :], op0=ALU.mult, op1=ALU.add).then_inc(drained[bank], 1)
                if what in ("O0+", "O1+"):
                    t = int(what[1])
                    dve.wait_ge(drained[bank], n)
                    wait(dve, ln2_mv, TPB * (i - 2) + t + 1)
                    dve.bn_stats(stats2[:, t, :], x1[q][:, t, :]).then_inc(ln2_stats, 1)
                    dve.wait_ge(ln2_stats, TPB * (i - 1) + t + 1)
                    wait(dve, xn2_ready, TPB * (i - 2) + t + 1)
                    dve.sem_inc(waited)
                    dve.bn_aggr(mv2[:, t, :], stats2[:, t, :]).then_inc(ln2_mv, 1)
                    if isinstance(i, int) and i == LAST:
                        dve.wait_ge(ln2_rstd, TPB * (i - 1) + t + 1)
                        dve.wait_ge(ln2_mv, TPB * (i - 1) + t + 1)
                        dve.wait_ge(rows_stored[q], 16 * ((i - 1) // 2))
                        dve.tensor_scalar(rows[q][:, t, 0:D], x1[q][:, t, :], mv2[:, t, 0:1], rstd2[:, t:t + 1],
                                          ALU.subtract, ALU.mult).then_inc(xn2_ready, 1)
                if what == "R":
                    logits = w[:, 0:TPB * EXPERTS].rearrange("p (t e) -> p t e", t=TPB)
                    dve.wait_ge(filled[bank], n)
                    dve.tensor_reduce(rmax[:], logits, AX, ALU.max).then_inc(r_max, 1)
                    dve.wait_ge(r_max, i)
                    wait(dve, r_exp, i - 1)
                    dve.tensor_tensor(rdiff[:], logits, rmax[:, :, None].to_broadcast([P, TPB, EXPERTS]),
                                      ALU.subtract).then_inc(drained[bank], 1)

            def router_end(i, p):
                q = 1 - p
                dve.wait_ge(r_exp, i)
                dve.tensor_reduce(rtot[:], rexp[:], AX, ALU.add).then_inc(r_tot, 1)
                dve.wait_ge(r_tot, i)
                dve.reciprocal(rinv[:], rtot[:]).then_inc(r_inv, 1)
                dve.wait_ge(r_inv, i)
                inv = rinv[:, :, None].to_broadcast([P, TPB, EXPERTS])
                wait(dve, score_kept, i - 1)
                dve.tensor_tensor(prob[:], rexp[:], inv, ALU.mult)
                dve.tensor_tensor(rows[q][:, :, D:ROW], rexp[:], inv, ALU.mult).then_inc(prob_ready, 1)

            def step(i, p, h):
                if at_start(i):
                    for p2 in range(2):
                        dve.memset(V[p2][:, :, :, DH:VW], 1.0).then_inc(ones_set, 1)
                if at_start(i):
                    ln1(0, 0, 0)
                    dve.wait_ge(ln1_rstd, 1)
                    dve.wait_ge(ln1_mv, TPB)
                    for t in range(TPB):
                        dve.tensor_scalar(xn[:, t, :], xin[0][:, t, :], mv1[:, t, 0:1], rstd1[:, t:t + 1],
                                          ALU.subtract, ALU.mult).then_inc(xn_ready, 1)
                for n in range(HEADS if "A" in stages(i) else 1):
                    if "A" in stages(i):
                        g = i * HEADS + n
                        if n + 1 < HEADS or "P" in stages(i):
                            masked_scores(g + 1, (n + 1) % 2)
                        if n % HPB == 1 and n > 1:
                            normalise_group(i * KB + n // HPB - 1, p, n // HPB - 1)
                    if "U" in stages(i) and n == (1 if "A" in stages(i) else 0):
                        normalise_group(i * KB - 1, 1 - p, KB - 1)
                    if "A" in stages(i):
                        for what in ends_at(i, n - 1):
                            if what in LATE:
                                evacuate(what, i, p)
                        for what in ends_at(i, n - 2):
                            if what in ("O0", "O1"):
                                evacuate(what + "+", i, p)
                        for what in ends_at(i, n):
                            if what not in LATE and n < HEADS - 1:
                                evacuate(what, i, p)
                    if n == 7 and not (isinstance(i, int) and i + 2 >= BATCH):
                        ln1(i + 2, p, h + 1)
                    if n == HEADS - 1 or "A" not in stages(i):
                        for what in ends_at(i, n):
                            if what == "V1" and "A" in stages(i) and "U" in stages(i):
                                router_end(i, p)
                            evacuate(what, i, p)
                            if what in ("O0", "O1"):
                                evacuate(what + "+", i, p)
                        if "U" in stages(i) and not ("A" in stages(i) and "P" in stages(i)):
                            router_end(i, p)
                if at_start(i):
                    ln1(1, 1, 0)
                    masked_scores(0, 0)

            steps(dve, step, 1)

        @block.tensor
        def _(pe):
            def scores_of(i, p, n):
                fb, j = divmod(n, HPB)
                g = i * HEADS + n
                if n % (HEADS // 2) == 0:
                    pe.wait_ge(stacked[n // (HEADS // 2)], STACKED * (i + 1))
                wait(pe, least_done, g - 1)
                s = S[n % 2]
                pe.matmul(s[:, 0:P], QS[:, j, fb, 0:P], KS[:, j, fb, 0:P], start=True, stop=True)
                pe.matmul(s[:, P:3 * P], QS[:, j, fb, P:2 * P], KS[:, j, fb, :], start=True,
                          stop=True).then_inc(s_done, 1)

            def turn(i, n):
                g = i * HEADS + n
                pe.wait_ge(e_done, g + 1)
                wait(pe, et_done, g - 1)
                for k in range(3):
                    ins = pe.transpose(PT[n % 2][:, k * P:(k + 1) * P], E[n % 2][:, k * P:(k + 1) * P], ident[:])
                ins.then_inc(t_done, 1)

            def values_of(i, p, n):
                fb, j = divmod(n, HPB)
                g = i * HEADS + n
                if n == 0:
                    wait_drained(pe, i, "V0", "V1")
                    if isinstance(i, int) and i == 0:
                        pe.wait_ge(ones_set, 2)
                pe.wait_ge(et_done, g + 1)
                if j == 0:
                    wait(pe, norm_done, i * KB + fb - 1)
                o = O[fb % 2]
                at0, at1 = j * VW, (HPB + j) * VW
                et, v = ET[n % 2], V[p]
                pe.matmul(o[:, at0:at0 + VW], et[:, 0:P], v[:, 0, n, :], start=True, stop=True)
                pe.matmul(o[:, at1:at1 + VW], et[:, P:2 * P], v[:, 0, n, :], start=True, stop=False)
                pe.matmul(o[:, at1:at1 + VW], et[:, 2 * P:3 * P], v[:, 1, n, :], start=False,
                          stop=True).then_inc(pv_done, 1)

            def products(to, pairs, part):
                n = 3 * len(pairs)
                terms = [(x, y) for (lh, ll), (rh, rl) in pairs for x, y in ((lh, rh), (lh, rl), (ll, rh))]
                which = range(n) if part is None else range(part * n // 2, (part + 1) * n // 2)
                for at in which:
                    ins = pe.matmul(to, *terms[at], start=(at == 0), stop=(at == n - 1))
                return ins

            def filling(what, part, i, p):
                bank, n = fill(i, what)
                w = W[bank]
                b, q = i + 1, 1 - p
                if not part:
                    wait(pe, drained[bank], n - 1)
                if what in ("XT0", "XT1", "CT0", "CT1", "AT0", "AT1"):
                    k0 = 2 * int(what[-1])
                    if what[0] == "X":
                        src = xn
                        pe.wait_ge(xn_ready, TPB * (b + 1))
                    elif what[0] == "C":
                        src = cin[q]
                        pe.wait_ge(c_in[q], 16 * (hrow(b, q)))
                    else:
                        src = attn[q]
                        pe.wait_ge(norm_done, KB * i)
                    for k in range(2):
                        for t in range(TPB):
                            ins = pe.transpose(w[:, (k * TPB + t) * P:(k * TPB + t + 1) * P],
                                               src[:, t, (k0 + k) * P:(k0 + k + 1) * P], ident[:])
                if what in BLOCKS:
                    if what == "Q0" and not part:
                        wait_banks(pe, drained, b, ("XT0", "XT1"), (1 - bank,))
                    if what == "K0" and not part:
                        wait_banks(pe, drained, b, ("CT0", "CT1"), (1 - bank,))
                    k = BLOCKS[what][0]
                    name, src = ("wq", xnT) if what[0] == "Q" else ("wk", cT)
                    for f in BLOCKS[what] if part is None else (k + part,):
                        cols = slice(f * P, (f + 1) * P)
                        ins = products(w[:, (f - k) * SEQ:(f - k + 1) * SEQ],
                                       [((w_hi[name][:, c, cols], w_lo[name][:, c, cols]),
                                         (src[0][:, c, :], src[1][:, c, :])) for c in range(KB)], None)
                if what in ("V0", "V1", "O0", "O1"):
                    if what == "O0" and not part:
                        wait_banks(pe, drained, i - 1, ("AT0", "AT1"), (1 - bank,))
                    if what == "V0" and not part:
                        wait_banks(pe, drained, b, ("CT0", "CT1"), (1 - bank,))
                    t = int(what[-1])
                    cols = slice(t * P, (t + 1) * P)
                    name, src = ("wv", cT) if what[0] == "V" else ("wo", aT)
                    ins = products(w[:, :], [((src[0][:, c, cols], src[1][:, c, cols]),
                                              (w_hi[name][:, c, :], w_lo[name][:, c, :])) for c in range(KB)], part)
                if what in ("X2T0", "X2T1"):
                    t = int(what[-1])
                    pe.wait_ge(xn2_ready, TPB * (i - 1) + t + 1)
                    for k in range(KB):
                        ins = pe.transpose(w[:, k * P:(k + 1) * P], rows[q][:, t, k * P:(k + 1) * P], ident[:])
                if what == "R":
                    wait_banks(pe, drained, i - 1, ("X2T0", "X2T1"), (1 - bank,))
                    for t in range(TPB):
                        for k in range(KB):
                            ins = pe.matmul(w[:, t * EXPERTS:(t + 1) * EXPERTS], xn2T[:, t, k, :], wr[:, k, :],
                                            start=(k == 0), stop=(k == KB - 1))
                if part != 0:
                    ins.then_inc(filled[bank], 1)

            halves_of = {}

            def hrow(b, q):
                return halves_of["h"] + 1

            def step(i, p, h):
                halves_of["h"] = h if not p else h + 1
                for n in range(HEADS if "A" in stages(i) else 1):
                    if "A" in stages(i):
                        if n + 1 < HEADS:
                            scores_of(i, p, n + 1)
                        turn(i, n)
                    if n > 0:
                        values_of(i, p, n - 1)
                    elif "U" in stages(i):
                        values_of(i - 1, 1 - p, HEADS - 1)
                    if n == HEADS - 1 and "P" in stages(i):
                        scores_of(i + 1, 1 - p, 0)
                    for what, part in parts_at(i, n):
                        filling(what, part, i, p)
                if at_start(i):
                    scores_of(0, 0, 0)

            steps(pe, step)

        return stored


def weights_setup(nc, a, const_ready, ident, mask, half, bq, bk, bv, bo, wr, tanh_g, w_hi, w_lo, names, W, load_first,
                  sem):
    ctx = ExitStack()
    with ctx:
        raw = {n: ctx.enter_context(nc.sbuf_tensor(n + "_raw", [P, KB, D], F32)) for n in names}
        gates = ctx.enter_context(nc.sbuf_tensor("gates", [P, 2], F32))
        bo_raw = ctx.enter_context(nc.sbuf_tensor("bo_raw", [P, D], F32))
        w_in = {n: sem(n + "_in") for n in names}
        small_in, cleared, ident_ready = map(sem, ("small_in", "cleared", "ident_ready"))
        gate_ready, bo_ready = sem("gate_ready"), sem("bo_ready")
        w_turned, w_hi_done, w_lo_done = map(sem, ("w_turned", "w_hi_done", "w_lo_done"))
        block = ctx.enter_context(nc.Block())
        small = 7

        @block.sync
        def _(sp):
            for n in names:
                src = a[f"L0_xattn_{n}_w"].rearrange("(f p) d -> p f d", p=P)
                for f in range(KB):
                    sp.dma_start(raw[n][:, f], src[:, f]).then_inc(w_in[n], 16)
            load_first(sp)

        @block.gpsimd
        def _(pool):
            pool.memset(ident[:], 0.0).then_inc(cleared, 1)
            pool.memset(mask[:], 0.0).then_inc(cleared, 1)
            pool.memset(half[:], -0.5).then_inc(const_ready, 1)
            pool.wait_ge(cleared, 2)
            pool.affine_select(out=ident[:], in_=ident[:], compare_op=ALU.not_equal, fill=1.0, base=0,
                               pattern=[[-1, P]], channel_multiplier=1).then_inc(ident_ready, 1)
            pool.affine_select(out=mask[:, P:2 * P], in_=mask[:, P:2 * P], compare_op=ALU.is_ge, fill=MASKED, base=0,
                               pattern=[[-1, P]], channel_multiplier=1).then_inc(const_ready, 1)
            with nc.allow_non_contiguous_dma(reason="512 words of each bias"):
                pool.dma_start(bq[:], a["L0_xattn_wq_b"].rearrange("(f p) -> p f", p=P)).then_inc(small_in, 16)
                pool.dma_start(bk[:], a["L0_xattn_wk_b"].rearrange("(f p) -> p f", p=P)).then_inc(small_in, 16)
                pool.dma_start(wr[:], a["L0_ffn_Wr"].rearrange("(k p) e -> p k e", p=P)).then_inc(small_in, 16)
            pool.dma_start(bv[:], a["L0_xattn_wv_b"].partition_broadcast(P)).then_inc(small_in, 16)
            pool.dma_start(bo_raw[:], a["L0_xattn_wo_b"].partition_broadcast(P)).then_inc(small_in, 16)
            pool.dma_start(gates[:, 0:1], a["g_xattn"].partition_broadcast(P)).then_inc(small_in, 16)
            pool.dma_start(gates[:, 1:2], a["g_ffn"].partition_broadcast(P)).then_inc(small_in, 16)
            pool.wait_ge(small_in, 16 * small)
            pool.wait_ge(gate_ready, 1)
            pool.tensor_scalar(bo[:], bo_raw[:], tanh_g[:, 0:1], None, ALU.mult).then_inc(bo_ready, 1)

        @block.scalar
        def _(act):
            for n, name in enumerate(names):
                if n == len(names) - 1:
                    act.wait_ge(small_in, 16 * small)
                    act.activation(tanh_g[:], gates[:], ACT.Tanh).then_inc(gate_ready, 1)
                for k in range(KB):
                    f = n * KB + k
                    act.wait_ge(w_turned, f + 1)
                    act.activation(w_hi[name][:, k, :], W[f % len(W)][:, :], ACT.Copy).then_inc(w_hi_done, 1)

        @block.vector
        def _(dve):
            for n, name in enumerate(names):
                for k in range(KB):
                    f = n * KB + k
                    dve.wait_ge(w_hi_done, f + 1)
                    dve.tensor_tensor(w_lo[name][:, k, :], W[f % len(W)][:, :], w_hi[name][:, k, :].bitcast(F32),
                                      ALU.subtract).then_inc(w_lo_done, 1)

        @block.tensor
        def _(pe):
            pe.wait_ge(ident_ready, 1)
            for n, name in enumerate(names):
                pe.wait_ge(w_in[name], 16 * KB)
                for k in range(KB):
                    f = n * KB + k
                    if f >= len(W):
                        pe.wait_ge(w_lo_done, f - len(W) + 1)
                    for c in range(KB):
                        ins = pe.transpose(W[f % len(W)][:, c * P:(c + 1) * P],
                                           raw[name][:, c, k * P:(k + 1) * P], ident[:])
                    ins.then_inc(w_turned, 1)


def load_block(sp, a, raw1, raw2, w_in, e, m):
    w1 = a["L0_ffn_W1"].rearrange("e (k p) (m h) -> e m p k h", p=P, h=P)
    w2 = a["L0_ffn_W2"].rearrange("e (m p) d -> e m p d", p=P)
    at = m % len(raw1)
    sp.dma_start(raw1[at][:], w1[e, m]).then_inc(w_in[at], 16)
    sp.dma_start(raw2[at][:], w2[e, m]).then_inc(w_in[at], 16)


def selection_phase(nc, a, ident, scores, ring, index, b1, numbers, stored, psum, sem):
    ctx = ExitStack()
    BITS = 30
    RADIX_BITS = 2
    DIGITS = (1 << RADIX_BITS) - 1
    ROUNDS = BITS // RADIX_BITS
    UNROLL = 5
    RAWS = 4
    part, iota, tile_no, lane = numbers
    with ctx:
        def sb(name, shape, dt=F32):
            return ctx.enter_context(nc.sbuf_tensor(name, shape, dt))

        sc = sb("sc", [P, CHUNK])
        same = sb("same_expert", [P, P], BF16)
        before = sb("chunks_before", [P, P], BF16)
        seen = sb("seen", [P, DIGITS, CHUNK])
        base = sb("base", [P, 1], I32)
        cands = sb("cands", [P, DIGITS], I32)
        steps_ = sb("steps", [P, DIGITS], I32)
        base_steps = sb("base_steps", [P, DIGITS], I32)
        unit = [sb(f"unit{k}", [P, 1]) for k in range(UNROLL)]
        counts = sb("counts", [P, DIGITS], BF16)
        enough = sb("enough", [P, DIGITS])
        digit = sb("digit", [P, 1])
        more = sb("more", [P, 1], I32)
        count = sb("count", [P, 1], BF16)
        b1_rows = sb("b1_rows", [EXPERTS * HB, P])
        raw1 = [sb(f"w1_first{p}", [P, KB, P]) for p in range(RAWS)]
        raw2 = [sb(f"w2_first{p}", [P, D]) for p in range(RAWS)]
        larger = sb("larger", [P, CHUNK])
        equal = sb("equal", [P, CHUNK])
        zeros = sb("zeros", [P, CHUNK])
        rank = sb("rank", [P, CHUNK])
        taken = sb("taken", [P, CHUNK])
        chosen = sb("chosen", [P, CHUNK])
        place = sb("place", [P, CHUNK])
        need = sb("need", [P, 1])
        offset = sb("offset", [P, 1])
        place_i = sb("place_i", [P, TPB, P], I32)
        part_i = sb("part_i", [P, 2, TPB * P], I32)
        iota_i = sb("iota_i", [P, P], I32)
        tile_i = sb("tile_i", [P, TPB, BATCH], I32)
        lane_i = sb("lane_i", [P, 1], I32)
        slot = sb("slot_first", [P, TPB, BATCH, P], BF16)
        column = sb("column_first", [P, TPB, BATCH, NS], BF16)
        token = sb("token_first", [P, TPB, BATCH, NS, 2], BF16)
        found = sb("found_first", [P, NS, 2])

        consts, sc_turned, sc_ready = sem("sel_consts"), sem("sc_turned"), sem("sc_ready")
        made, counted, summed = sem("made"), sem("counted"), sem("summed")
        cands_ready, prepared = sem("cands_ready"), sem("prepared")
        digit_ready, more_ready, base_ready = sem("digit_ready"), sem("more_ready"), sem("base_ready")
        w_in = [sem(f"w_in_first{p}") for p in range(RAWS)]
        step_done, turned, sums = sem("step_done"), sem("place_turned"), sem("chunk_sums")
        part_ready, hot_ready, hot_used = sem("part_ready"), sem("hot_ready"), sem("hot_used")
        column_ready = sem("column_ready")
        passed = sem("passed_first")
        w_hi_done, w_lo_done = sem("w_hi_first"), sem("w_lo_first")
        b1_in, b1_turned = sem("b1_in"), sem("b1_turned")
        block = ctx.enter_context(nc.Block())

        @block.sync
        def _(sp):
            for semaphore, value in stored:
                sp.wait_ge(semaphore, value)
            sp.dma_start(b1_rows[:], a["L0_ffn_b1"].rearrange("e (m p) -> (e m) p", p=P)).then_inc(b1_in, 16)
            for m in range(HB):
                if m >= RAWS:
                    sp.wait_ge(w_lo_done, m - RAWS + 1)
                load_block(sp, a, raw1, raw2, w_in, 0, m)

        @block.scalar
        def _(act):
            for m in range(HB):
                act.wait_ge(w_in[m % RAWS], 32 * (m // RAWS + 1))
                act.activation(ring["w1_hi"][:, m], raw1[m % RAWS][:], ACT.Copy)
                act.activation(ring["w2_hi"][:, m], raw2[m % RAWS][:], ACT.Copy).then_inc(w_hi_done, 1)
            act.wait_ge(b1_turned, 1)
            act.activation(b1[:].rearrange("p e m -> p (e m)"), psum[6][:, 0:P], ACT.Copy)

        @block.gpsimd
        def _(pool):
            pool.memset(same[:], 1.0).then_inc(made, 1)
            pool.wait_ge(made, 1)
            by_expert = same[:].rearrange("p (e c) -> p e c", c=CHUNKS)
            pool.affine_select(out=by_expert, in_=by_expert, compare_op=ALU.is_ge, fill=0.0, base=0,
                               pattern=[[-CHUNKS, EXPERTS], [0, CHUNKS]], channel_multiplier=1).then_inc(made, 1)
            pool.wait_ge(made, 2)
            pool.affine_select(out=by_expert, in_=by_expert, compare_op=ALU.is_ge, fill=0.0, base=CHUNKS - 1,
                               pattern=[[CHUNKS, EXPERTS], [0, CHUNKS]], channel_multiplier=-1).then_inc(made, 1)
            pool.wait_ge(made, 3)
            pool.affine_select(out=before[:], in_=same[:], compare_op=ALU.is_gt, fill=0.0, base=0,
                               pattern=[[1, P]], channel_multiplier=-1).then_inc(made, 1)
            pool.iota(iota_i[:], pattern=[[1, P]], base=0, channel_multiplier=0).then_inc(made, 1)
            pool.iota(tile_i[:], pattern=[[1, TPB], [TPB, BATCH]], base=0, channel_multiplier=0).then_inc(made, 1)
            pool.iota(lane_i[:], pattern=[[0, 1]], base=0, channel_multiplier=1).then_inc(made, 1)
            pool.wait_ge(made, 7)
            pool.tensor_copy(iota[:], iota_i[:]).then_inc(consts, 1)
            pool.tensor_copy(tile_no[:], tile_i[:]).then_inc(consts, 1)
            pool.tensor_copy(lane[:], lane_i[:]).then_inc(consts, 1)
            for m in range(HB):
                pool.wait_ge(w_hi_done, m + 1)
                pool.tensor_tensor(ring["w1_lo"][:, m], raw1[m % RAWS][:], ring["w1_hi"][:, m].bitcast(F32),
                                   ALU.subtract)
                pool.tensor_tensor(ring["w2_lo"][:, m], raw2[m % RAWS][:], ring["w2_hi"][:, m].bitcast(F32),
                                   ALU.subtract).then_inc(w_lo_done, 1)

        @block.vector
        def _(dve):
            dve.memset(zeros[:], 0.0).then_inc(step_done, 1)
            dve.memset(base[:], 0).then_inc(step_done, 1)
            dve.memset(unit[0][:], float(1 << (BITS - RADIX_BITS))).then_inc(step_done, 1)
            for j in range(DIGITS):
                dve.memset(cands[:, j:j + 1], (j + 1) << (BITS - RADIX_BITS)).then_inc(step_done, 1)
                dve.memset(steps_[:, j:j + 1], (j + 1) << (BITS - 2 * RADIX_BITS)).then_inc(step_done, 1)
            dve.wait_ge(sc_turned, 1)
            dve.tensor_copy(sc[:], psum[0][:, 0:CHUNK]).then_inc(sc_ready, 1)
            dve.wait_ge(sc_ready, 1)
            dve.wait_ge(step_done, 3 + 2 * DIGITS)

            with dve.Fori(1, ROUNDS + 1, UNROLL) as it:
                for k in range(UNROLL):
                    n = it + k
                    for j in range(DIGITS):
                        ins = dve.tensor_scalar(seen[:, j], sc[:], cands[:, j:j + 1].bitcast(F32), 0.0,
                                                ALU.is_ge, ALU.add, accum_out=counts[:, j:j + 1])
                    ins.then_inc(counted, 1)
                    dve.tensor_tensor(base_steps[:], base[:, 0:1].to_broadcast([P, DIGITS]), steps_[:], ALU.bitwise_or)
                    dve.tensor_scalar(steps_[:], steps_[:], RADIX_BITS, None, ALU.arith_shift_right)
                    dve.tensor_scalar(unit[(k + 1) % UNROLL][:], unit[k][:], 1.0 / (1 << RADIX_BITS), None,
                                      ALU.mult).then_inc(prepared, 1)
                    dve.wait_ge(summed, n)
                    dve.tensor_scalar(enough[:], psum[1][:, 0:DIGITS], float(TOPK), 0.0, ALU.is_ge, ALU.add,
                                      accum_out=digit[:]).then_inc(digit_ready, 1)
                    dve.wait_ge(digit_ready, n)
                    dve.tensor_scalar(more[:], digit[:], unit[k][:, 0:1], None, ALU.mult).then_inc(more_ready, 1)
                    dve.wait_ge(more_ready, n)
                    dve.wait_ge(prepared, n)
                    dve.tensor_tensor(cands[:], base_steps[:], more[:, 0:1].to_broadcast([P, DIGITS]),
                                      ALU.bitwise_or).then_inc(cands_ready, 1)
                    dve.tensor_tensor(base[:], base[:], more[:], ALU.bitwise_or).then_inc(base_ready, 1)
                    dve.wait_ge(cands_ready, n)
                    dve.wait_ge(base_ready, n)

            limit = base[:].bitcast(F32)
            done = [3 + 2 * DIGITS]

            def then(ins):
                done[0] += 1
                ins.then_inc(step_done, 1)
                dve.wait_ge(step_done, done[0])

            dve.tensor_scalar(larger[:], sc[:], limit, 0.0, ALU.is_gt, ALU.add, accum_out=count[:]).then_inc(sums, 1)
            then(dve.tensor_scalar(equal[:], sc[:], limit, None, ALU.is_equal))
            then(dve.tensor_tensor_scan(rank[:], equal[:], zeros[:], 0.0, ALU.add, ALU.add))
            dve.wait_ge(turned, 1)
            dve.tensor_scalar(need[:], psum[1][:, 0:1], -1.0, float(TOPK), ALU.mult, ALU.add)
            then(dve.tensor_copy(count[:], rank[:, CHUNK - 1:CHUNK]))
            dve.sem_inc(sums)
            dve.wait_ge(turned, 2)
            then(dve.tensor_copy(offset[:], psum[2][:, 0:1]))
            then(dve.tensor_scalar(taken[:], rank[:], offset[:, 0:1], need[:, 0:1], ALU.add, ALU.is_le))
            then(dve.tensor_tensor(taken[:], taken[:], equal[:], ALU.mult))
            then(dve.tensor_tensor(chosen[:], taken[:], larger[:], ALU.add))
            then(dve.tensor_tensor_scan(rank[:], chosen[:], zeros[:], 0.0, ALU.add, ALU.add))
            then(dve.tensor_copy(count[:], rank[:, CHUNK - 1:CHUNK]))
            dve.sem_inc(sums)
            dve.wait_ge(turned, 3)
            then(dve.tensor_copy(offset[:], psum[3][:, 0:1]))
            dve.scalar_tensor_tensor(out=place[:], in0=rank[:], scalar=offset[:, 0:1], in1=chosen[:],
                                     op0=ALU.add, op1=ALU.mult).then_inc(sums, 1)
            dve.wait_ge(turned, 4)
            flat = place_i[:].rearrange("p t f -> p (t f)")
            then(dve.tensor_scalar(flat, psum[4][:, 0:TPB * P], -1.0, None, ALU.add))
            dve.tensor_scalar(part_i[:, 0], flat, P - 1, None, ALU.bitwise_and)
            then(dve.tensor_scalar(part_i[:, 1], flat, P.bit_length() - 1, None, ALU.arith_shift_right))
            dve.tensor_copy(part[:].rearrange("p a t f -> p (a t f)"),
                            part_i[:].rearrange("p a f -> p (a f)")).then_inc(part_ready, 1)
            dve.wait_ge(part_ready, 1)
            dve.wait_ge(consts, 3)
            for t in range(TPB):
                dve.tensor_tensor(slot[:, t], iota[:, None, :].to_broadcast([P, BATCH, P]),
                                  part[:, 0, t, 0:CHUNKS, None].to_broadcast([P, BATCH, P]), ALU.is_equal)
            token_numbers(dve, column, token, part[:, 1, :, 0:CHUNKS], numbers, column_ready, 1, (hot_ready, passed))
            dve.wait_ge(hot_used, 1)
            then(dve.tensor_copy(found[:].rearrange("p s v -> p (s v)"), psum[5][:, 0:NS * 2]))
            dve.scalar_tensor_tensor(out=index[:, 0, :], in0=found[:, :, 0], scalar=float(P), in1=found[:, :, 1],
                                     op0=ALU.mult, op1=ALU.add)

        @block.tensor
        def _(pe):
            for t in range(TPB):
                ins = pe.transpose(psum[0][:, t * P:(t + 1) * P], scores[:, t].rearrange("p e c -> p (e c)"), ident[:])
            ins.then_inc(sc_turned, 1)
            pe.wait_ge(made, 4)
            with pe.Fori(1, ROUNDS + 1) as n:
                pe.wait_ge(counted, n)
                pe.matmul(psum[1][:, 0:DIGITS], same[:], counts[:], start=True, stop=True).then_inc(summed, 1)
            pe.wait_ge(b1_in, 16)
            pe.transpose(psum[6][:, 0:P], b1_rows[:], ident[:]).then_inc(b1_turned, 1)
            for k, m in enumerate((same, before, before)):
                pe.wait_ge(sums, k + 1)
                pe.matmul(psum[1 + k][:, 0:1], m[:], count[:], start=True, stop=True).then_inc(turned, 1)
            pe.wait_ge(sums, 4)
            for t in range(TPB):
                ins = pe.transpose(psum[4][:, t * P:(t + 1) * P], place[:, t * P:(t + 1) * P], ident[:])
            ins.then_inc(turned, 1)
            pe.wait_ge(hot_ready, 1)
            for n in range(N // P):
                t, c = divmod(n, BATCH)
                ins = pe.matmul(psum[5][:, 0:NS * 2], slot[:, t, c, :], token[:, t, c].rearrange("p s v -> p (s v)"),
                                start=(n == 0), stop=(n == N // P - 1))
            ins.then_inc(hot_used, 1)


def expert_phase(nc, a, out, rows_dram, ident, tanh_g, ring, raw1, raw2, w_in, index, b1, numbers, psum, sb_all, sem):
    ctx = ExitStack()
    part, iota, tile_no, lane = numbers
    PIECES = 8
    TILES = N // P // PIECES
    LAST_E = EXPERTS - 1
    TURN_AT = 9
    with ctx:
        def sb(name, shape, dt=F32):
            return sb_all(name, shape, dt, ctx)

        xg = sb("xg", [P, STILES, ROW])
        xT = [[sb(f"xT{u}_{s}", [P, KB, SLOTS], F32R) for s in ("hi", "lo")] for u in range(2)]
        gate = [sb(f"gate{u}", [P, STILES]) for u in range(2)]
        picks = [sb(f"picks{u}", [P, STILES], U32) for u in range(2)]
        h = [sb(f"h{n}", [P, SLOTS]) for n in range(2)]
        h_hi = [sb(f"h_hi{n}", [P, SLOTS], F32R) for n in range(2)]
        h_lo = [sb(f"h_lo{n}", [P, SLOTS], F32R) for n in range(2)]
        y = sb("y", [P, STILES, D])
        b2 = sb("b2", [P, D])
        part_now = sb("part_now", [P, 2, TPB, BATCH], BF16)
        column = sb("column", [P, TPB, BATCH, NS], BF16)
        token = sb("token", [P, TPB, BATCH, NS, 2], BF16)
        slot = [sb(f"slot{n}", [P, TILES, P], BF16) for n in range(2)]
        found = sb("found", [P, NS, 2])
        table = sb("table", [P, 1])
        H, XB, Y = psum[0:2], psum[2:4], psum[4:8]

        picked = sem("picked")
        xg_in = sem("xg_in")
        x_turned, x_hi, x_ready = sem("x_turned"), sem("xg_hi"), sem("x_ready")
        gate_ready = sem("gate_set")
        h_filled, h_hi_done = sem("h_filled"), sem("h_hi_done")
        h_full = sem("h_full")
        h_ready = sem("h_ready")
        y_step = sem("y_step")
        y_free = [sem(f"y_free{n}") for n in range(2)]
        y_out = sem("y_out")
        y_landed = sem("y_landed")
        y_clear = sem("y_clear")
        w_hi_done = sem("w_hi_next")
        w_ready = sem("w_ready")
        b2_in = sem("b2_in")
        part_cut, column_set, token_set = sem("part_cut"), sem("column_set"), sem("token_set")
        slot_set = sem("slot_set")
        slot_used = sem("slot_used")
        found_out, index_set = sem("found_out"), sem("index_set")
        passed = sem("passed")
        block = ctx.enter_context(nc.Block())

        out_rows = out.rearrange("b s d -> (b s) d")

        def experts(eng, expert):
            with eng.Fori(0, LAST_E) as e:
                expert(e, False)
            expert(LAST_E, True)

        @block.sync
        def _(sp):
            sp.dma_start(b2[:], a["L0_ffn_b2"][0].partition_broadcast(P)).then_inc(b2_in, 16)

            def expert(e, last):
                if last:
                    return
                for m in range(HB):
                    if m >= 2:
                        sp.wait_ge(w_ready, HB * (e + 1) + m - 1)
                        sp.sem_inc(passed)
                    load_block(sp, a, raw1, raw2, w_in, e + 1, m)
                sp.wait_ge(y_out, STILES * PASSES * (e + 1))
                sp.sem_inc(passed)
                sp.dma_start(b2[:], a["L0_ffn_b2"][e + 1].partition_broadcast(P)).then_inc(b2_in, 16)
                sp.wait_ge(w_ready, HB * (e + 2))
                sp.sem_inc(passed)

            experts(sp, expert)

        @block.gpsimd
        def _(pool):
            pool.sem_inc(y_clear)

            def gather(e, u, half_):
                tiles = slice(half_ * STILES, (half_ + 1) * STILES)
                pool.tensor_copy(picks[half_][:, None, :], index[:, bass.ds(e, 1), tiles]).then_inc(picked, 1)
                pool.wait_ge(picked, u + 1)
                pool.wait_ge(x_turned, KB * u)
                pool.wait_ge(gate_ready, u)
                pool.sem_inc(passed)
                for t in range(STILES):
                    pool.indirect_dma_start(
                        out=xg[:, t, :], out_offset=None, in_=rows_dram[:, :],
                        in_offset=bass.IndirectOffsetOnAxis(ap=picks[half_][:, t:t + 1], axis=0)).then_inc(xg_in, 16)

            pool.tensor_copy(picks[0][:, None, :], index[:, 0:1, 0:STILES]).then_inc(picked, 1)
            pool.wait_ge(picked, 1)
            for t in range(STILES):
                pool.indirect_dma_start(
                    out=xg[:, t, :], out_offset=None, in_=rows_dram[:, :],
                    in_offset=bass.IndirectOffsetOnAxis(ap=picks[0][:, t:t + 1], axis=0)).then_inc(xg_in, 16)

            def expert(e, last):
                for half_ in range(PASSES):
                    u = PASSES * e + half_
                    if half_ + 1 < PASSES:
                        gather(e, u + 1, half_ + 1)
                    elif not last:
                        pool.wait_ge(index_set, e + 1)
                        gather(e + 1, u + 1, 0)
                    for t in range(STILES):
                        pool.wait_ge(y_out, STILES * u + t + 1)
                        pool.sem_inc(passed)
                        pool.indirect_dma_start(
                            out=out_rows, out_offset=bass.IndirectOffsetOnAxis(ap=picks[half_][:, t:t + 1], axis=0),
                            in_=y[:, t, :], in_offset=None, compute_op=ALU.add).then_inc(y_landed, 16)
                    pool.wait_ge(y_landed, 16 * STILES * (u + 1))
                    pool.sem_inc(y_clear)

            experts(pool, expert)

        @block.scalar
        def _(act):
            act.sem_inc(h_full, 2)
            act.sem_inc(y_free[1], STILES // 2)
            act.activation(table[:], ident[:, 0:1], ACT.Gelu)

            def x_high(f, u2, k):
                act.wait_ge(x_turned, f + 1)
                act.activation(xT[u2][0][:, k, :], XB[k % 2][:, :], ACT.Copy).then_inc(x_hi, 1)

            def w_high(e, m, s):
                act.wait_ge(w_in[m % 2], 32 * (HB // 2) * e + 32 * (m // 2 + 1))
                act.wait_ge(y_step, s + 3)
                act.activation(ring["w1_hi"][:, m], raw1[m % 2][:], ACT.Copy)
                act.activation(ring["w2_hi"][:, m], raw2[m % 2][:], ACT.Copy).then_inc(w_hi_done, 1)

            def hidden(e, s, m):
                act.wait_ge(h_filled, s + 1)
                act.wait_ge(h_ready, s + 1)
                act.sem_inc(passed)
                act.activation(h[m % 2][:], H[m % 2][:, :], ACT.Gelu, bias=b1[:, bass.ds(e, 1), m]).then_inc(h_full, 1)
                act.wait_ge(h_full, s + 3)
                act.wait_ge(y_step, s + 1)
                act.activation(h_hi[m % 2][:], h[m % 2][:], ACT.Copy).then_inc(h_hi_done, 1)

            for k in range(KB):
                x_high(k, 0, k)
            hidden(0, 0, 0)

            def expert(e, last):
                for half_ in range(PASSES):
                    u = PASSES * e + half_
                    end = last and half_ == PASSES - 1
                    for m in range(HB):
                        s = HB * u + m
                        if m + 1 < HB or not end:
                            hidden(e + (half_ * HB + m + 1) // (PASSES * HB), s + 1, (m + 1) % HB)
                        if m == HB - 1:
                            act.wait_ge(gate_ready, u + 1)
                            act.wait_ge(y_step, HB * (u + 1) + 2)
                            act.wait_ge(y_clear, u + 1)
                            act.sem_inc(passed)
                            for t in range(1, STILES, 2):
                                act.activation(y[:, t, :], Y[t][:, :], ACT.Identity,
                                               scale=gate[half_][:, t:t + 1]).then_inc(y_free[1], 1)
                        if half_ == PASSES - 1 and not last:
                            w_high(e, m, s)
                        if TURN_AT <= m < TURN_AT + KB and not end:
                            x_high(KB * (u + 1) + m - TURN_AT, 1 - half_, m - TURN_AT)

            experts(act, expert)

        @block.vector
        def _(dve):
            dve.sem_inc(h_ready, 2)
            dve.sem_inc(y_free[0], STILES // 2)
            dve.sem_inc(w_ready, HB)

            def gates_of(e, u, u2):
                dve.wait_ge(xg_in, 16 * STILES * (u + 1))
                if not isinstance(u, int) or u >= 2:
                    dve.wait_ge(y_clear, u)
                dve.tensor_scalar(gate[u2][:, :, None], xg[:, :, bass.ds(e + D, 1)], tanh_g[:, 1:2], None,
                                  ALU.mult).then_inc(gate_ready, 1)

            def x_low(f, u2, k):
                dve.wait_ge(x_hi, f + 1)
                dve.tensor_tensor(xT[u2][1][:, k, :], XB[k % 2][:, :], xT[u2][0][:, k, :].bitcast(F32),
                                  ALU.subtract).then_inc(x_ready, 1)

            def w_low(e, m):
                dve.wait_ge(w_hi_done, HB * e + m + 1)
                dve.tensor_tensor(ring["w1_lo"][:, m], raw1[m % 2][:], ring["w1_hi"][:, m].bitcast(F32), ALU.subtract)
                dve.tensor_tensor(ring["w2_lo"][:, m], raw2[m % 2][:], ring["w2_hi"][:, m].bitcast(F32),
                                  ALU.subtract).then_inc(w_ready, 1)

            def hidden(s, m):
                dve.wait_ge(h_hi_done, s + 1)
                dve.tensor_tensor(h_lo[m % 2][:], h[m % 2][:], h_hi[m % 2][:].bitcast(F32),
                                  ALU.subtract).then_inc(h_ready, 1)

            def find_tokens(e, n):
                if n == 0:
                    dve.tensor_copy(part_now[:], part[:, :, :, bass.ds((e + 1) * CHUNKS, CHUNKS)]).then_inc(part_cut, 1)
                    dve.wait_ge(part_cut, e + 1)
                    dve.sem_inc(passed)
                    token_numbers(dve, column, token, part_now[:, 1], numbers, column_set, e + 1, (token_set, passed))
                t, c = divmod(n * TILES, BATCH)
                shape = [P, TILES, P]
                dve.wait_ge(slot_used, PIECES * e + n + 1)
                dve.sem_inc(passed)
                dve.tensor_tensor(slot[n % 2][:], iota[:, None, :].to_broadcast(shape),
                                  part_now[:, 0, t, c:c + TILES, None].to_broadcast(shape),
                                  ALU.is_equal).then_inc(slot_set, 1)

            def found_tokens(e):
                dve.wait_ge(slot_used, PIECES * (e + 1) + 2)
                dve.sem_inc(passed)
                dve.tensor_copy(found[:].rearrange("p s v -> p (s v)"), XB[0][:, 0:NS * 2]).then_inc(found_out, 1)
                dve.wait_ge(found_out, e + 1)
                dve.sem_inc(passed)
                dve.scalar_tensor_tensor(out=index[:, bass.ds(e + 1, 1), :], in0=found[:, None, :, 0], scalar=float(P),
                                         in1=found[:, None, :, 1], op0=ALU.mult, op1=ALU.add).then_inc(index_set, 1)

            gates_of(0, 0, 0)
            for k in range(KB):
                x_low(k, 0, k)
            hidden(0, 0)

            def expert(e, last):
                for half_ in range(PASSES):
                    u = PASSES * e + half_
                    end = last and half_ == PASSES - 1
                    for m in range(HB):
                        s = HB * u + m
                        if m + 1 < HB or not end:
                            hidden(s + 1, (m + 1) % HB)
                        if m == HB - 1:
                            dve.wait_ge(y_step, HB * (u + 1) + 2)
                            dve.wait_ge(y_clear, u + 1)
                            dve.sem_inc(passed)
                            for t in range(0, STILES, 2):
                                dve.tensor_scalar(y[:, t, :], Y[t][:, :], gate[half_][:, t:t + 1], None,
                                                  ALU.mult).then_inc(y_free[0], 1)
                            dve.wait_ge(b2_in, 16 * (e + 1))
                            for t in range(STILES):
                                dve.wait_ge(y_free[t % 2], STILES // 2 * (u + 1) + t // 2 + 1)
                                dve.sem_inc(passed)
                                dve.scalar_tensor_tensor(out=y[:, t, :], in0=b2[:], scalar=gate[half_][:, t:t + 1],
                                                         in1=y[:, t, :], op0=ALU.mult, op1=ALU.add).then_inc(y_out, 1)
                        if half_ == 0 and not last and m < PIECES:
                            find_tokens(e, m)
                        if half_ == 0 and not last and m == PIECES:
                            found_tokens(e)
                        if half_ == PASSES - 1 and not last:
                            w_low(e, m)
                        if not end:
                            if m == TURN_AT:
                                gates_of(e + (half_ + 1) // PASSES, u + 1, 1 - half_)
                            if TURN_AT <= m < TURN_AT + KB:
                                x_low(KB * (u + 1) + m - TURN_AT, 1 - half_, m - TURN_AT)

            experts(dve, expert)

        @block.tensor
        def _(pe):
            pe.sem_inc(y_step, 2)
            pe.sem_inc(slot_used, 2)

            def turn_tokens(f, u, k):
                if k == 0:
                    pe.wait_ge(xg_in, 16 * STILES * (u + 1))
                if not isinstance(f, int) or f >= 2:
                    pe.wait_ge(x_ready, f - 1)
                for t in range(STILES):
                    ins = pe.transpose(XB[k % 2][:, t * P:(t + 1) * P], xg[:, t, k * P:(k + 1) * P], ident[:])
                ins.then_inc(x_turned, 1)

            def first_layer(e, half_, s, m):
                u2 = half_ % 2
                if m == 0:
                    pe.wait_ge(x_ready, KB * (PASSES * e + half_ + 1))
                if half_ == 0:
                    pe.wait_ge(w_ready, HB * e + m + 1)
                pe.wait_ge(h_full, s + 1)
                x_hi_, x_lo_ = xT[u2]
                at = 0
                for k in range(KB):
                    w_hi_, w_lo_ = ring["w1_hi"][:, m, k, :], ring["w1_lo"][:, m, k, :]
                    for w, x in ((w_hi_, x_hi_), (w_hi_, x_lo_), (w_lo_, x_hi_)):
                        ins = pe.matmul(H[m % 2][:, :], w, x[:, k, :], start=(at == 0), stop=(at == 3 * KB - 1))
                        at += 1
                ins.then_inc(h_filled, 1)

            def second_layer(u, s, m):
                pe.wait_ge(h_ready, s + 3)
                w_hi_, w_lo_ = ring["w2_hi"][:, m, :], ring["w2_lo"][:, m, :]
                for t in range(STILES):
                    if m == 0:
                        pe.wait_ge(y_free[t % 2], STILES // 2 * u + t // 2 + 1)
                    cols = slice(t * P, (t + 1) * P)
                    hi, lo = h_hi[m % 2][:, cols], h_lo[m % 2][:, cols]
                    for n, (x, w) in enumerate(((hi, w_hi_), (hi, w_lo_), (lo, w_hi_))):
                        ins = pe.matmul(Y[t][:, :], x, w, start=(m == 0 and n == 0), stop=(m == HB - 1 and n == 2))
                ins.then_inc(y_step, 1)

            def place_tokens(e, n):
                if n == 0:
                    pe.wait_ge(token_set, e + 1)
                pe.wait_ge(slot_set, PIECES * e + n + 1)
                for c in range(TILES):
                    tok = token[:].rearrange("p t b s v -> p (t b) (s v)")[:, n * TILES + c]
                    ins = pe.matmul(XB[0][:, 0:NS * 2], slot[n % 2][:, c, :], tok, start=(n == 0 and c == 0),
                                    stop=(n == PIECES - 1 and c == TILES - 1))
                ins.then_inc(slot_used, 1)

            for k in range(KB):
                turn_tokens(k, 0, k)
            first_layer(0, 0, 0, 0)

            def expert(e, last):
                for half_ in range(PASSES):
                    u = PASSES * e + half_
                    for m in range(HB):
                        s = HB * u + m
                        if m + 1 < HB:
                            first_layer(e, half_, s + 1, m + 1)
                        elif half_ + 1 < PASSES:
                            first_layer(e, half_ + 1, s + 1, 0)
                        elif not last:
                            first_layer(e + 1, 0, s + 1, 0)
                        if half_ == 0 and not last and 1 <= m <= PIECES:
                            place_tokens(e, m - 1)
                        if TURN_AT <= m < TURN_AT + KB and not (last and half_ == PASSES - 1):
                            if half_ == 0 and not last and m == TURN_AT:
                                pe.wait_ge(found_out, e + 1)
                            turn_tokens(KB * (u + 1) + m - TURN_AT, u + 1, m - TURN_AT)
                        second_layer(u, s, m)

            experts(pe, expert)


_OUT = (BATCH, SEQ, D)


def kernel(**inputs):
    import numpy as np
    from concourse import bacc
    from concourse.bass_utils import run_bass_kernel_spmd

    nc = bacc.Bacc("TRN2", target_bir_lowering=False, num_devices=1)
    arrays = {f"in_{n}": np.ascontiguousarray(v) for n, v in inputs.items()}
    args = {n: nc.dram_tensor(f"in_{n}", arrays[f"in_{n}"].shape, mybir.dt.from_np(arrays[f"in_{n}"].dtype),
                              kind="ExternalInput").ap() for n in inputs}
    out = nc.dram_tensor("out_x", _OUT, F32, kind="ExternalOutput").ap()
    block_program(nc, args, out)
    r = run_bass_kernel_spmd(nc, [arrays], core_ids=[0])
    return r.results[0]["out_x"]
```
